# Optimizing a Trainium2 kernel written in Bass

```python
import numpy as np
import jax
import jax.numpy as jnp

def _softmax(x, axis=-1):
    return jax.nn.softmax(x, axis=axis)

def _gelu(x):
    return jax.nn.gelu(x, approximate=True)

def _silu(x):
    return jax.nn.silu(x)

def _sigmoid(x):
    return jax.nn.sigmoid(x)

def _layernorm(x, axis=-1, eps=1e-05):
    m = jnp.mean(x, axis=axis, keepdims=True)
    v = jnp.var(x, axis=axis, keepdims=True)
    return (x - m) / jnp.sqrt(v + eps)

def _scatter_add(tgt, idx, src, axis=0):
    return tgt.at[idx].add(src)

def _segment_sum(src, seg, n):
    return jax.ops.segment_sum(src, seg, n)
kernel_name = 'mk_conv_attn_hybrid_d4_conv_nchw384_r4_3f19fc'

def setup_inputs(seed: int=0):
    np.random.seed(seed)
    _w = jnp.asarray

    def _rec_inputs():
        import jax
        import jax.numpy as jnp
        _gk = jax.random.key(seed)
        x = -0.0002221 + 1 * jax.random.normal(jax.random.fold_in(_gk, 1), (16, 96, 16, 16), jnp.float32)
        return x
    x = _rec_inputs()

    def _L0_conv_setup():
        import jax, jax.numpy as jnp
        import numpy as np
        STOKEN = (8, 8)
        N_ITER = 1
        NUM_HEADS = 8

        def _unfold9(x):
            B, C, h, w = x.shape
            xp = jnp.pad(x, ((0, 0), (0, 0), (1, 1), (1, 1)))
            return jnp.stack([xp[:, :, i:i + h, j:j + w] for i in range(3) for j in range(3)], axis=2)

        def _fold9(x):
            lead = x.shape[:-3]
            h, w = (x.shape[-2], x.shape[-1])
            xp = jnp.pad(x, [(0, 0)] * len(lead) + [(0, 0), (1, 1), (1, 1)])
            out = jnp.zeros(lead + (h, w), x.dtype)
            for i in range(3):
                for j in range(3):
                    out = out + xp[..., i * 3 + j, 2 - i:2 - i + h, 2 - j:2 - j + w]
            return out

        def _forward(x, qkv_w, proj_w, proj_b):
            B, C, H0, W0 = x.shape
            h, w = STOKEN
            scale = C ** (-0.5)
            pad_r = (w - W0 % w) % w
            pad_bt = (h - H0 % h) % h
            if pad_r or pad_bt:
                x = jnp.pad(x, ((0, 0), (0, 0), (0, pad_bt), (0, pad_r)))
            H, W = (x.shape[2], x.shape[3])
            hh, ww = (H // h, W // w)
            N = hh * ww
            blocks = x.reshape(B, C, hh, h, ww, w)
            stf = blocks.mean(axis=(3, 5))
            pix = blocks.transpose(0, 2, 4, 3, 5, 1).reshape(B, N, h * w, C)
            affinity = None
            aff_sum = None
            for idx in range(N_ITER):
                s9 = _unfold9(stf).reshape(B, C, 9, N).transpose(0, 3, 1, 2)
                affinity = jax.nn.softmax(jnp.einsum('bnpc,bnck->bnpk', pix, s9) * scale, axis=-1)
                aff_sum = _fold9(affinity.sum(axis=2).transpose(0, 2, 1).reshape(B, 9, hh, ww))
                if idx < N_ITER - 1:
                    s = jnp.einsum('bnpc,bnpk->bnck', pix, affinity)
                    stf = _fold9(s.transpose(0, 2, 3, 1).reshape(B, C, 9, hh, ww)) / (aff_sum[:, None] + 1e-12)
            affinity = jax.lax.stop_gradient(affinity)
            aff_sum = jax.lax.stop_gradient(aff_sum)
            s = jnp.einsum('bnpc,bnpk->bnck', pix, affinity)
            stf = _fold9(s.transpose(0, 2, 3, 1).reshape(B, C, 9, hh, ww)) / (aff_sum[:, None] + 1e-12)
            hd = C // NUM_HEADS
            qkv = jnp.einsum('oc,bchw->bohw', qkv_w, stf).reshape(B, NUM_HEADS, 3 * hd, N)
            q, k, v = jnp.split(qkv, 3, axis=2)
            attn = jax.nn.softmax(jnp.einsum('bhdn,bhdm->bhnm', k, q) * hd ** (-0.5), axis=-2)
            o = jnp.einsum('bhdn,bhnm->bhdm', v, attn).reshape(B, C, hh, ww)
            stf = jnp.einsum('oc,bchw->bohw', proj_w, o) + proj_b[None, :, None, None]
            s9 = _unfold9(stf).reshape(B, C, 9, N).transpose(0, 3, 1, 2)
            pix_out = jnp.einsum('bnck,bnpk->bncp', s9, affinity)
            out = pix_out.reshape(B, hh, ww, C, h, w).transpose(0, 3, 1, 4, 2, 5).reshape(B, C, H, W)
            if pad_r or pad_bt:
                out = out[:, :, :H0, :W0]
            return out
        key = jax.random.key(seed)
        k1, k2, k3, k4 = jax.random.split(key, 4)
        B, C, H, W = (16, 96, 16, 16)
        return {'x': jax.random.normal(k1, (B, C, H, W), jnp.float32), 'qkv_w': jax.random.normal(k2, (3 * C, C), jnp.float32) * 0.02, 'proj_w': jax.random.normal(k3, (C, C), jnp.float32) * 0.02, 'proj_b': jax.random.normal(k4, (C,), jnp.float32) * 0.02}
    _L0_conv_all = _L0_conv_setup()
    _L0_conv_in = {k: v for k, v in _L0_conv_all.items() if k in ('qkv_w', 'proj_w', 'proj_b')}
    del _L0_conv_all

    def _L1_conv_setup():
        import jax, jax.numpy as jnp
        import numpy as np
        B, C, H, W = (8, 96, 32, 32)
        NH = 6
        HD = C // NH
        T = H * W
        EPS = 1e-05
        key = jax.random.key(seed)
        ks = jax.random.split(key, 8)
        s = 1.0 / np.sqrt(C)
        x = jax.random.normal(ks[0], (B, C, H, W), dtype=jnp.float32)
        Wq = jax.random.normal(ks[1], (C, C), dtype=jnp.float32) * s
        Wk = jax.random.normal(ks[2], (C, C), dtype=jnp.float32) * s
        Wv = jax.random.normal(ks[3], (C, C), dtype=jnp.float32) * s
        head_w = jax.random.normal(ks[4], (NH, NH), dtype=jnp.float32) * (1.0 / np.sqrt(NH))
        gamma = jnp.ones((NH,), dtype=jnp.float32)
        beta = jnp.zeros((NH,), dtype=jnp.float32)
        projW = jax.random.normal(ks[5], (C, C), dtype=jnp.float32) * s
        projb = jnp.zeros((C,), dtype=jnp.float32)
        return {'x': x, 'Wq': Wq, 'Wk': Wk, 'Wv': Wv, 'head_w': head_w, 'gamma': gamma, 'beta': beta, 'projW': projW, 'projb': projb}
    _L1_conv_all = _L1_conv_setup()
    _L1_conv_in = {k: v for k, v in _L1_conv_all.items() if k in ('Wq', 'Wk', 'Wv', 'head_w', 'gamma', 'beta', 'projW', 'projb')}
    del _L1_conv_all

    def _L2_attn_setup():
        import jax, jax.numpy as jnp
        import numpy as np
        import math
        B, T, N_EMBD, N_HEAD = (4, 1024, 96, 6)
        HEAD_DIM = N_EMBD // N_HEAD
        key = jax.random.key(seed)
        k1, k2, k3 = jax.random.split(key, 3)
        x = jax.random.normal(k1, (B, T, N_EMBD), dtype=jnp.float32)
        w_attn = jax.random.normal(k2, (N_EMBD, 3 * N_EMBD), dtype=jnp.float32) * 0.02
        w_proj = jax.random.normal(k3, (N_EMBD, N_EMBD), dtype=jnp.float32) * 0.02
        return {'x': x, 'w_attn': w_attn, 'w_proj': w_proj}
    _L2_attn_all = _L2_attn_setup()
    _L2_attn_in = {k: v for k, v in _L2_attn_all.items() if k in ('w_attn', 'w_proj')}
    del _L2_attn_all

    def _L2_ffn_setup():
        import jax, jax.numpy as jnp
        import numpy as np
        NUM_GROUPS = 5
        EPS = 1e-05
        QB = 128.0

        def _binarize_weights_groupwise(W):
            n_out = W.shape[0]
            gs = n_out // NUM_GROUPS
            Wb = jnp.zeros_like(W)
            for g in range(NUM_GROUPS):
                wg = W[g * gs:(g + 1) * gs]
                z = wg - wg.mean()
                ste = z + jax.lax.stop_gradient(jnp.sign(z) - z)
                Wb = Wb.at[g * gs:(g + 1) * gs].set(ste)
            return Wb

        def _quantize_activations_groupwise(x):
            n = x.shape[0]
            gs = n // NUM_GROUPS
            xq = jnp.zeros_like(x)
            for g in range(NUM_GROUPS):
                ag = x[g * gs:(g + 1) * gs]
                gamma = jnp.max(jnp.abs(ag))
                xq = xq.at[g * gs:(g + 1) * gs].set(jnp.clip(ag * QB / (gamma + EPS), -QB + EPS, QB - EPS))
            return xq

        def _bitlinear(x, W, b):
            Wb = _binarize_weights_groupwise(W)
            y = jnp.einsum('btc,oc->bto', x, Wb) + b
            return _quantize_activations_groupwise(y)
        key = jax.random.key(seed)
        k1, k2, k3, k4, k5 = jax.random.split(key, 5)
        B, T, C = (10, 512, 96)
        H = 4 * C
        lim1 = 1.0 / np.sqrt(C)
        lim2 = 1.0 / np.sqrt(H)
        x = jax.random.normal(k1, (B, T, C), dtype=jnp.float32)
        W1 = jax.random.uniform(k2, (H, C), minval=-lim1, maxval=lim1, dtype=jnp.float32)
        b1 = jax.random.uniform(k3, (H,), minval=-lim1, maxval=lim1, dtype=jnp.float32)
        W2 = jax.random.uniform(k4, (C, H), minval=-lim2, maxval=lim2, dtype=jnp.float32)
        b2 = jax.random.uniform(k5, (C,), minval=-lim2, maxval=lim2, dtype=jnp.float32)
        return {'x': x, 'W1': W1, 'b1': b1, 'W2': W2, 'b2': b2}
    _L2_ffn_all = _L2_ffn_setup()
    _L2_ffn_in = {k: v for k, v in _L2_ffn_all.items() if k in ('W1', 'b1', 'W2', 'b2')}
    del _L2_ffn_all

    def _L3_attn_setup():
        import jax, jax.numpy as jnp
        import numpy as np
        B, T, D = (4, 512, 96)
        H = 6
        HD = D // H
        key = jax.random.key(seed)
        k1, k2, k3, k4, k5 = jax.random.split(key, 5)
        s = 0.02
        return {'x': jax.random.normal(k1, (B, T, D), dtype=jnp.float32), 'qkv_w': jax.random.normal(k2, (3 * D, D), dtype=jnp.float32) * s, 'qkv_b': jax.random.normal(k3, (3 * D,), dtype=jnp.float32) * s, 'out_w': jax.random.normal(k4, (D, D), dtype=jnp.float32) * s, 'out_b': jax.random.normal(k5, (D,), dtype=jnp.float32) * s}
    _L3_attn_all = _L3_attn_setup()
    _L3_attn_in = {k: v for k, v in _L3_attn_all.items() if k in ('qkv_w', 'qkv_b', 'out_w', 'out_b')}
    del _L3_attn_all

    def _L3_ffn_setup():
        import jax, jax.numpy as jnp
        import numpy as np
        NUM_EXPERTS = 4
        TOP_K = 2
        DIM = 96
        HID = 4 * DIM
        key = jax.random.key(seed)
        ks = jax.random.split(key, 5)
        B, S = (16, 512)
        scale_in = 1.0 / np.sqrt(DIM)
        scale_hid = 1.0 / np.sqrt(HID)
        return {'x': jax.random.normal(ks[0], (B, S, DIM), dtype=jnp.float32), 'gate_w': jax.random.normal(ks[1], (DIM, NUM_EXPERTS), dtype=jnp.float32) * scale_in, 'gate_b': jnp.zeros((NUM_EXPERTS,), dtype=jnp.float32), 'w1': jax.random.normal(ks[2], (NUM_EXPERTS, DIM, HID), dtype=jnp.float32) * scale_in, 'b1': jnp.zeros((NUM_EXPERTS, HID), dtype=jnp.float32), 'w2': jax.random.normal(ks[3], (NUM_EXPERTS, HID, DIM), dtype=jnp.float32) * scale_hid, 'b2': jnp.zeros((NUM_EXPERTS, DIM), dtype=jnp.float32)}
    _L3_ffn_all = _L3_ffn_setup()
    _L3_ffn_in = {k: v for k, v in _L3_ffn_all.items() if k in ('gate_w', 'gate_b', 'w1', 'b1', 'w2', 'b2')}
    del _L3_ffn_all
    return {'x': x, 'L0_conv_qkv_w': _L0_conv_in['qkv_w'], 'L0_conv_proj_w': _L0_conv_in['proj_w'], 'L0_conv_proj_b': _L0_conv_in['proj_b'], 'L1_conv_Wq': _L1_conv_in['Wq'], 'L1_conv_Wk': _L1_conv_in['Wk'], 'L1_conv_Wv': _L1_conv_in['Wv'], 'L1_conv_head_w': _L1_conv_in['head_w'], 'L1_conv_gamma': _L1_conv_in['gamma'], 'L1_conv_beta': _L1_conv_in['beta'], 'L1_conv_projW': _L1_conv_in['projW'], 'L1_conv_projb': _L1_conv_in['projb'], 'L2_attn_w_attn': _L2_attn_in['w_attn'], 'L2_attn_w_proj': _L2_attn_in['w_proj'], 'L2_ffn_W1': _L2_ffn_in['W1'], 'L2_ffn_b1': _L2_ffn_in['b1'], 'L2_ffn_W2': _L2_ffn_in['W2'], 'L2_ffn_b2': _L2_ffn_in['b2'], 'L3_attn_qkv_w': _L3_attn_in['qkv_w'], 'L3_attn_qkv_b': _L3_attn_in['qkv_b'], 'L3_attn_out_w': _L3_attn_in['out_w'], 'L3_attn_out_b': _L3_attn_in['out_b'], 'L3_ffn_gate_w': _L3_ffn_in['gate_w'], 'L3_ffn_gate_b': _L3_ffn_in['gate_b'], 'L3_ffn_w1': _L3_ffn_in['w1'], 'L3_ffn_b1': _L3_ffn_in['b1'], 'L3_ffn_w2': _L3_ffn_in['w2'], 'L3_ffn_b2': _L3_ffn_in['b2']}

def reference(x, L0_conv_qkv_w, L0_conv_proj_w, L0_conv_proj_b, L1_conv_Wq, L1_conv_Wk, L1_conv_Wv, L1_conv_head_w, L1_conv_gamma, L1_conv_beta, L1_conv_projW, L1_conv_projb, L2_attn_w_attn, L2_attn_w_proj, L2_ffn_W1, L2_ffn_b1, L2_ffn_W2, L2_ffn_b2, L3_attn_qkv_w, L3_attn_qkv_b, L3_attn_out_w, L3_attn_out_b, L3_ffn_gate_w, L3_ffn_gate_b, L3_ffn_w1, L3_ffn_b1, L3_ffn_w2, L3_ffn_b2):
    import jax
    import jax.numpy as jnp

    def _L0_conv_ref(x, qkv_w, proj_w, proj_b):
        import jax, jax.numpy as jnp
        import numpy as np
        STOKEN = (8, 8)
        N_ITER = 1
        NUM_HEADS = 8

        def _unfold9(x):
            B, C, h, w = x.shape
            xp = jnp.pad(x, ((0, 0), (0, 0), (1, 1), (1, 1)))
            return jnp.stack([xp[:, :, i:i + h, j:j + w] for i in range(3) for j in range(3)], axis=2)

        def _fold9(x):
            lead = x.shape[:-3]
            h, w = (x.shape[-2], x.shape[-1])
            xp = jnp.pad(x, [(0, 0)] * len(lead) + [(0, 0), (1, 1), (1, 1)])
            out = jnp.zeros(lead + (h, w), x.dtype)
            for i in range(3):
                for j in range(3):
                    out = out + xp[..., i * 3 + j, 2 - i:2 - i + h, 2 - j:2 - j + w]
            return out

        def _forward(x, qkv_w, proj_w, proj_b):
            B, C, H0, W0 = x.shape
            h, w = STOKEN
            scale = C ** (-0.5)
            pad_r = (w - W0 % w) % w
            pad_bt = (h - H0 % h) % h
            if pad_r or pad_bt:
                x = jnp.pad(x, ((0, 0), (0, 0), (0, pad_bt), (0, pad_r)))
            H, W = (x.shape[2], x.shape[3])
            hh, ww = (H // h, W // w)
            N = hh * ww
            blocks = x.reshape(B, C, hh, h, ww, w)
            stf = blocks.mean(axis=(3, 5))
            pix = blocks.transpose(0, 2, 4, 3, 5, 1).reshape(B, N, h * w, C)
            affinity = None
            aff_sum = None
            for idx in range(N_ITER):
                s9 = _unfold9(stf).reshape(B, C, 9, N).transpose(0, 3, 1, 2)
                affinity = jax.nn.softmax(jnp.einsum('bnpc,bnck->bnpk', pix, s9) * scale, axis=-1)
                aff_sum = _fold9(affinity.sum(axis=2).transpose(0, 2, 1).reshape(B, 9, hh, ww))
                if idx < N_ITER - 1:
                    s = jnp.einsum('bnpc,bnpk->bnck', pix, affinity)
                    stf = _fold9(s.transpose(0, 2, 3, 1).reshape(B, C, 9, hh, ww)) / (aff_sum[:, None] + 1e-12)
            affinity = jax.lax.stop_gradient(affinity)
            aff_sum = jax.lax.stop_gradient(aff_sum)
            s = jnp.einsum('bnpc,bnpk->bnck', pix, affinity)
            stf = _fold9(s.transpose(0, 2, 3, 1).reshape(B, C, 9, hh, ww)) / (aff_sum[:, None] + 1e-12)
            hd = C // NUM_HEADS
            qkv = jnp.einsum('oc,bchw->bohw', qkv_w, stf).reshape(B, NUM_HEADS, 3 * hd, N)
            q, k, v = jnp.split(qkv, 3, axis=2)
            attn = jax.nn.softmax(jnp.einsum('bhdn,bhdm->bhnm', k, q) * hd ** (-0.5), axis=-2)
            o = jnp.einsum('bhdn,bhnm->bhdm', v, attn).reshape(B, C, hh, ww)
            stf = jnp.einsum('oc,bchw->bohw', proj_w, o) + proj_b[None, :, None, None]
            s9 = _unfold9(stf).reshape(B, C, 9, N).transpose(0, 3, 1, 2)
            pix_out = jnp.einsum('bnck,bnpk->bncp', s9, affinity)
            out = pix_out.reshape(B, hh, ww, C, h, w).transpose(0, 3, 1, 4, 2, 5).reshape(B, C, H, W)
            if pad_r or pad_bt:
                out = out[:, :, :H0, :W0]
            return out
        return _forward(x, qkv_w, proj_w, proj_b)

    def _L1_conv_ref(x, Wq, Wk, Wv, head_w, gamma, beta, projW, projb):
        import jax, jax.numpy as jnp
        import numpy as np
        B, C, H, W = (8, 96, 32, 32)
        NH = 6
        HD = C // NH
        T = H * W
        EPS = 1e-05
        b, c, h, w = x.shape
        t = h * w
        scale = HD ** (-0.5)
        xf = x.reshape(b, c, t)
        q = jnp.einsum('oc,bct->bot', Wq, xf).reshape(b, NH, HD, t)
        k = jnp.einsum('oc,bct->bot', Wk, xf).reshape(b, NH, HD, t)
        v = jnp.einsum('oc,bct->bot', Wv, xf).reshape(b, NH, HD, t)
        scores = jnp.einsum('bhdq,bhdt->bhqt', q, k) * scale
        mixed = jnp.einsum('gh,bhqt->bgqt', head_w, scores)
        attn = jax.nn.softmax(mixed, axis=-1)
        mean = jnp.mean(attn, axis=(2, 3), keepdims=True)
        var = jnp.var(attn, axis=(2, 3), keepdims=True)
        attn = (attn - mean) * jax.lax.rsqrt(var + EPS)
        attn = attn * gamma[None, :, None, None] + beta[None, :, None, None]
        out = jnp.einsum('bhqt,bhdt->bhqd', attn, v)
        out = out.reshape(b, t, c)
        y = out @ projW.T + projb
        return jnp.transpose(y, (0, 2, 1)).reshape(b, c, h, w)

    def _L2_attn_ref(x, w_attn, w_proj):
        import jax, jax.numpy as jnp
        import numpy as np
        import math
        B, T, N_EMBD, N_HEAD = (4, 1024, 96, 6)
        HEAD_DIM = N_EMBD // N_HEAD
        b, t, c = x.shape
        qkv = x @ w_attn
        q, k, v = jnp.split(qkv, 3, axis=-1)
        q = q.reshape(b, t, N_HEAD, HEAD_DIM)
        k = k.reshape(b, t, N_HEAD, HEAD_DIM)
        v = v.reshape(b, t, N_HEAD, HEAD_DIM)
        scale = 1.0 / math.sqrt(HEAD_DIM)
        att = jnp.einsum('bqhd,bkhd->bhqk', q, k) * scale
        causal = jnp.tril(jnp.ones((t, t), dtype=bool))
        att = jnp.where(causal[None, None], att, jnp.finfo(att.dtype).min)
        att = jax.nn.softmax(att, axis=-1)
        out = jnp.einsum('bhqk,bkhd->bqhd', att, v).reshape(b, t, c)
        return out @ w_proj

    def _L2_ffn_ref(x, W1, b1, W2, b2):
        import jax, jax.numpy as jnp
        import numpy as np
        NUM_GROUPS = 5
        EPS = 1e-05
        QB = 128.0

        def _binarize_weights_groupwise(W):
            n_out = W.shape[0]
            gs = n_out // NUM_GROUPS
            Wb = jnp.zeros_like(W)
            for g in range(NUM_GROUPS):
                wg = W[g * gs:(g + 1) * gs]
                z = wg - wg.mean()
                ste = z + jax.lax.stop_gradient(jnp.sign(z) - z)
                Wb = Wb.at[g * gs:(g + 1) * gs].set(ste)
            return Wb

        def _quantize_activations_groupwise(x):
            n = x.shape[0]
            gs = n // NUM_GROUPS
            xq = jnp.zeros_like(x)
            for g in range(NUM_GROUPS):
                ag = x[g * gs:(g + 1) * gs]
                gamma = jnp.max(jnp.abs(ag))
                xq = xq.at[g * gs:(g + 1) * gs].set(jnp.clip(ag * QB / (gamma + EPS), -QB + EPS, QB - EPS))
            return xq

        def _bitlinear(x, W, b):
            Wb = _binarize_weights_groupwise(W)
            y = jnp.einsum('btc,oc->bto', x, Wb) + b
            return _quantize_activations_groupwise(y)
        h = _bitlinear(x, W1, b1)
        h = jax.nn.gelu(h, approximate=False)
        out = _bitlinear(h, W2, b2)
        return out

    def _L3_attn_ref(x, qkv_w, qkv_b, out_w, out_b):
        import jax, jax.numpy as jnp
        import numpy as np
        B, T, D = (4, 512, 96)
        H = 6
        HD = D // H
        b, t, c = x.shape
        qkv = jnp.einsum('btc,oc->bto', x, qkv_w) + qkv_b
        q, k, v = jnp.split(qkv, 3, axis=-1)
        q = q.reshape(b, t, H, HD).transpose(0, 2, 1, 3)
        k = k.reshape(b, t, H, HD).transpose(0, 2, 1, 3)
        v = v.reshape(b, t, H, HD).transpose(0, 2, 1, 3)
        scale = 1.0 / jnp.sqrt(jnp.float32(HD))
        att = jnp.einsum('bhqd,bhkd->bhqk', q, k) * scale
        causal = jnp.tril(jnp.ones((t, t), dtype=bool))
        att = jnp.where(causal, att, jnp.finfo(att.dtype).min)
        att = jax.nn.softmax(att, axis=-1)
        out = jnp.einsum('bhqk,bhkd->bhqd', att, v)
        out = out.transpose(0, 2, 1, 3).reshape(b, t, c)
        out = jnp.einsum('btc,oc->bto', out, out_w) + out_b
        return out

    def _L3_ffn_ref(x, gate_w, gate_b, w1, b1, w2, b2):
        import jax, jax.numpy as jnp
        import numpy as np
        NUM_EXPERTS = 4
        TOP_K = 2
        DIM = 96
        HID = 4 * DIM
        scores = jnp.einsum('bsd,de->bse', x, gate_w) + gate_b
        probs = jax.nn.softmax(scores, axis=-1)
        topk_vals, topk_idx = jax.lax.top_k(probs, TOP_K)
        mask = jnp.sum(jax.nn.one_hot(topk_idx, NUM_EXPERTS, dtype=probs.dtype), axis=-2)
        masked = probs * mask
        masked = masked / (jnp.sum(masked, axis=-1, keepdims=True) + 1e-09)
        h = jax.nn.gelu(jnp.einsum('bsd,edh->ebsh', x, w1) + b1[:, None, None, :], approximate=False)
        y = jnp.einsum('ebsh,ehd->ebsd', h, w2) + b2[:, None, None, :]
        out = jnp.einsum('bse,ebsd->bsd', masked, y)
        return out

    def _gn(v, G=32, eps=1e-05):
        B_, C_, H_, W_ = v.shape
        g = v.reshape(B_, G, C_ // G, H_, W_)
        m = jnp.mean(g, axis=(2, 3, 4), keepdims=True)
        s = jnp.var(g, axis=(2, 3, 4), keepdims=True)
        return ((g - m) / jnp.sqrt(s + eps)).reshape(v.shape)

    def _ln_c(v, eps=1e-06):
        m = jnp.mean(v, axis=1, keepdims=True)
        s = jnp.var(v, axis=1, keepdims=True)
        return (v - m) / jnp.sqrt(s + eps)

    def _ln_t(v, eps=1e-05):
        m = jnp.mean(v, axis=-1, keepdims=True)
        s = jnp.var(v, axis=-1, keepdims=True)
        return (v - m) / jnp.sqrt(s + eps)

    def _to_tokens(v):
        B_, C_, H_, W_ = v.shape
        return v.reshape(B_, C_, H_ * W_).transpose(0, 2, 1)

    def _from_tokens(t, like):
        B_, C_, H_, W_ = like.shape
        return t.transpose(0, 2, 1).reshape(B_, C_, H_, W_)
    x = x + _L0_conv_ref(_gn(x), L0_conv_qkv_w, L0_conv_proj_w, L0_conv_proj_b)
    x = x + _L1_conv_ref(_gn(x), L1_conv_Wq, L1_conv_Wk, L1_conv_Wv, L1_conv_head_w, L1_conv_gamma, L1_conv_beta, L1_conv_projW, L1_conv_projb)
    t = _to_tokens(x)
    t = t + _L2_attn_ref(_ln_t(t), L2_attn_w_attn, L2_attn_w_proj)
    t = t + _L2_ffn_ref(_ln_t(t), L2_ffn_W1, L2_ffn_b1, L2_ffn_W2, L2_ffn_b2)
    t = t + _L3_attn_ref(_ln_t(t), L3_attn_qkv_w, L3_attn_qkv_b, L3_attn_out_w, L3_attn_out_b)
    t = t + _L3_ffn_ref(_ln_t(t), L3_ffn_gate_w, L3_ffn_gate_b, L3_ffn_w1, L3_ffn_b1, L3_ffn_w2, L3_ffn_b2)
    x = _from_tokens(t, x)
    return x

_drawn_inputs = setup_inputs


def setup_inputs(seed=0):
    import zlib

    import numpy as np

    out = dict(_drawn_inputs(seed))
    spreads = {'L1_conv_gamma': (1.0, 0.2),
     'L1_conv_beta': (0.0, 0.272),
     'L1_conv_projb': (0.0, 0.8),
     'L3_ffn_gate_b': (0.0, 0.8),
     'L3_ffn_b1': (0.0, 0.8),
     'L3_ffn_b2': (0.0, 2.0)}
    factors = {'L0_conv_qkv_w': 8.0,
     'L0_conv_proj_w': 8.0,
     'L0_conv_proj_b': 5.432,
     'L2_attn_w_attn': 8.0,
     'L2_attn_w_proj': 8.0,
     'L2_ffn_b1': 8.0,
     'L2_ffn_b2': 64.0,
     'L3_attn_qkv_w': 8.0,
     'L3_attn_qkv_b': 42.47,
     'L3_attn_out_w': 8.0,
     'L3_attn_out_b': 52.786,
     'L3_ffn_gate_w': 4.368,
     'L3_ffn_w1': 4.444,
     'L3_ffn_w2': 3.852}
    for name, (base, spread) in spreads.items():
        noise = np.random.default_rng([zlib.crc32(name.encode()), seed]).standard_normal(out[name].shape)
        drawn = base * np.exp(spread * noise) if base else spread * noise
        out[name] = jnp.asarray(drawn.astype(out[name].dtype))
    for name, factor in factors.items():
        out[name] = (out[name] * factor).astype(out[name].dtype)
    return out
```

```python
import numpy as np
from contextlib import ExitStack

import concourse.bass as bass
from concourse import mybir

F32 = mybir.dt.float32
BF16 = mybir.dt.bfloat16
ALU = mybir.AluOpType
ACT = mybir.ActivationFunctionType
AX = mybir.AxisListType

B, C, HH, WW = 16, 96, 16, 16
N = HH * WW
P = 128
NT = B * N // P
TPI = N // P
SB = 8
M = (HH // SB) * (WW // SB)
H0 = 8
NH, HD = 6, 16
QS = HD ** -0.5
HID = 4 * C
NJ = HID // P
NG = 5
GI = B // NG
GT = GI * N
NE = 4
QB = 128.0
QEPS = 1e-5
START = 1
NEG = -1e30

W96 = [("l0_q", C), ("l0_k", C), ("l0_v", C), ("l0_p", C), ("l0_pb", 1),
       ("l1_q", C), ("l1_k", C), ("l1_v", C), ("l1_hw", NH), ("l1_p", C),
       ("l2_q", 2 * C), ("l2_k", 2 * C), ("l2_v", C), ("l2_p", C),
       ("f2_w1", HID),
       ("l3_q", 2 * C), ("l3_k", 2 * C), ("l3_v", C), ("l3_p", C), ("l3_qb", 2), ("l3_kb", 2),
       ("f3_gate", NE), ("f3_w1", NE * HID)]
W128 = [("ident", P), ("avg3", C), ("sum12", C), ("mask", P),
        ("l1_pb", C), ("l1_gamma", NH), ("l1_beta", NH),
        ("f2_b1", NJ), ("f2_w2", NJ * C), ("f2_b2", C),
        ("l3_vb", C), ("l3_pb", C),
        ("f3_gateb", NE), ("f3_b1", NE * NJ), ("f3_w2", NE * NJ * C), ("f3_b2", NE * C)]


def columns(parts):
    at, where = 0, {}
    for name, n in parts:
        where[name] = (at, at + n)
        at += n
    return where, at


NORM = {"gn0": 1, "gn1": 2, "ln2": 3, "lnf2": 4, "ln3": 5, "lnf3": 6}
TURN = {"ln2": 0, "lnf2": 8, "ln3": 16, "lnf3": 24}


C96, N96 = columns(W96)
C128, N128 = columns(W128)


def hybrid_kernel(nc, x_d, w96_d, w128_d, out_d):
    ctx = ExitStack()
    with ctx:
        def sb(name, shape, dt=F32):
            return ctx.enter_context(nc.sbuf_tensor(name, shape, dt))

        sems = {}

        def sg(name):
            if name not in sems:
                sems[name] = ctx.enter_context(nc.semaphore(name))
            return sems[name]

        mix_d = nc.dram_tensor("l1_mix", [B, NH, N, HD], F32, kind="Internal").ap()

        w96 = sb("w96", [C, N96])
        w128 = sb("w128", [P, N128])
        xc = sb("xc", [C, B * N])
        xn = sb("xn", [C, (B + 1) * N])
        tok = sb("tok", [P, NT, C])
        on = sb("on", [P, NT, C])
        big = sb("big", [P, NJ * NG * GT])
        ones = sb("ones", [P, P])
        identb = sb("identb", [P, P], BF16)
        maskb = sb("maskb", [P, P], BF16)
        chst = sb("chst", [P, NT, 6])
        chmv = sb("chmv", [P, NT, 2])
        st = sb("st", [P, 8, NT])
        xb = sb("xb", [C, 2, N])
        qs = sb("qs", [C, N])
        qh = sb("qh", [C, 2, NH, N])
        kh = sb("kh", [C, 2, 2, N])
        vh = sb("vh", [P, 2, TPI, NH, HD + 1])
        nmax = sb("nmax", [P, 2, 2, TPI])
        ee = sb("ee", [P, 2, 2, TPI, N])
        et = sb("et", [P, 2, 2 * TPI, P])
        junk = sb("junk", [P, N])
        sqj = sb("sqj", [P, 2, TPI, N])
        ssq = sb("ssq", [P, 2, NH, TPI])
        rden = sb("rden", [P, 2, TPI, NH])
        sqw = sb("sqw", [P, 2, NH, TPI])
        ssqa = sb("ssqa", [P, B, NH, TPI])
        h3 = sb("h3", [P, 4, 512])
        ysc = sb("ysc", [P, NE, C])

        ps = ctx.enter_context(nc.psum_tensor("ps", [P, 8, 512], F32))

        def wa(name):
            a, b = C96[name]
            return w96[:, a:b]

        def wb(name, rows=P):
            a, b = C128[name]
            return w128[0:rows, a:b]

        ident = wb("ident")

        def last_dim(ap, n):
            return ap.unsqueeze(ap.ndim).broadcast_to(list(ap.shape) + [n])

        def mid_dim(ap, at, n):
            shape = list(ap.shape)
            return ap.unsqueeze(at).broadcast_to(shape[:at] + [n] + shape[at:])

        bd_w = 2 * M * B + M
        l0_xt = big[:, 0:NT * C].rearrange("p (t c) -> p t c", c=C)
        l0_bd = big[:, NT * C:NT * C + B * bd_w]
        l0_at = big[0:B * M, NT * C + B * bd_w:NT * C + B * bd_w + B * N]
        qkv0 = sb("qkv0", [C, 3, B * M])
        rowsum = sb("rowsum", [C, B * N // SB])
        stf = sb("stf", [C, B * M])
        aff = sb("aff", [P, NT, M])
        a0 = sb("a0", [P, NT, M])
        pr = sb("pr", [C, B, M, M])
        pr2 = sb("pr2", [C, B, M, M])
        s64 = sb("s64", [C, 6, B * M])
        stft = sb("stft", [B * M, C])
        xsr = big[0:C, 2048:2048 + B * P].rearrange("p (i r) -> p i r", r=P)
        y1 = big[:, :].rearrange("p (j t) -> p j t", j=NJ)
        y2 = on
        amax = sb("amax", [P, 4, NG])
        gate = sb("gate", [P, 2, NT, NE])
        cmp = sb("cmp", [P, 6, NT])
        gsel = sb("gsel", [P, NE, NT])

        block = ctx.enter_context(nc.Block())

        def scores_cols(l, qc):
            return N if l == 1 else P * (qc + 1)

        def blocks(l):
            return [(q, t) for q in range(TPI) for t in range(TPI) if l == 1 or t <= q]

        @block.sync
        def _(sp):
            half = B * N // 4
            for i in range(4):
                sp.dma_start(xc[:, i * half:(i + 1) * half], x_d[:, i * half:(i + 1) * half]).then_inc(sg(f"x_loaded{i}"), 16)
            sp.dma_start(w128[:, :], w128_d).then_inc(sg("w128_loaded"), 16)
            sp.dma_start(w96[:, :], w96_d).then_inc(sg("w96_loaded"), 16)
            on_v = on[:, :, :].rearrange("p (i q) (g d) -> p i q g d", q=TPI, d=HD)
            for i in range(B):
                sp.wait_ge(sg("l1_out"), i // 4 + 1)
                for q in range(TPI):
                    sp.dma_start(mix_d[i, :, q * P:(q + 1) * P, :].rearrange("g q d -> q g d"),
                                 on_v[:, i, q]).then_inc(sg(f"l1_stored{i // 4}"), 16)
            flat = mix_d.rearrange("i g q d -> (i g q d)").rearrange("(t p c) -> p t c", p=P, c=C)
            for r in range(4):
                sp.wait_ge(sg(f"l1_stored{r}"), 16 * TPI * 4)
                sp.dma_start(tok[:, r * 8:(r + 1) * 8, :], flat[:, r * 8:(r + 1) * 8, :]).then_inc(sg(f"l1_mixed{r}"), 16)
            with sp.Fori(0, NT // 4) as t:
                sp.wait_ge(sg("moe_block"), t + 1)
                sp.dma_start(out_d[:, bass.ds(t * 4, 4), :], tok[:, bass.ds(t * 4, 4), :]).then_inc(sg("stored"), 16)
            sp.wait_ge(sg("stored"), 16 * (NT // 4))


        @block.gpsimd
        def _(pool):
            nc.gpsimd.memset(ones[:, :], 1.0).then_inc(sg("ones_set"), 1)
            nc.gpsimd.memset(l0_bd, 0.0).then_inc(sg("bd_zeroed"), 1)
            nc.gpsimd.memset(xn[:, B * N:], 0.0).then_inc(sg("pad_zeroed"), 1)
            nc.gpsimd.memset(vh[:, :, :, :, HD:HD + 1], 1.0).then_inc(sg("v_ones"), 1)
            pool.wait_ge(sg("w128_loaded"), 16)
            nc.gpsimd.tensor_copy(identb[:, :], ident).then_inc(sg("bf_consts"), 1)
            nc.gpsimd.tensor_copy(maskb[:, :], wb("mask")).then_inc(sg("bf_consts"), 1)
            pool.wait_ge(sg("pad_zeroed"), 1)

            def stage(l, n, par):
                pool.wait_ge(sg("pad_zeroed"), 1)
                nc.gpsimd.tensor_copy(xb[:, par, :], xn[:, bass.ds(n * N, N)]).then_inc(sg(f"l{l}_xb"), 1)

            def mix(l, n, par):
                pool.wait_ge(sg(f"l{l}_q_sb"), n + 1)
                for g in range(NH):
                    last = nc.gpsimd.tensor_tensor(qh[:, par, g, :], qs[:, :], wa("l1_hw")[:, g:g + 1].broadcast_to([C, N]), ALU.mult)
                last.then_inc(sg(f"l{l}_qmix"), 1)

            for l in (1, 2, 3):
                pool.wait_ge(sg(f"l{l}_xn"), 1)
                pool.wait_ge(sg("w96_loaded"), 16)
                stage(l, 0, 0)
                if l == 1:
                    mix(l, 0, 0)
                with pool.Fori(0, B // 2) as it:
                    for par in range(2):
                        n = it * 2 + (par + 1)
                        pool.wait_ge(sg(f"l{l}_v_ps"), START + n - 1)
                        stage(l, n, 1 - par)
                        if l == 1:
                            pool.wait_ge(sg("l1_s_ps"), START + n * 3 - 3)
                            mix(l, n, 1 - par)
                if l == 2:
                    for k in range(2):
                        pool.wait_ge(sg(f"f2_amax{k}"), 1)
                        nc.gpsimd.partition_all_reduce(amax[:, 2 * k + 1, :], amax[:, 2 * k, :], P,
                                                       bass.bass_isa.ReduceOp.max).then_inc(sg(f"f2_gmax{k}"), 1)

        @block.scalar
        def _(act):
            for name in ["l1_exp", "l2_exp", "l3_exp", "l1_et0", "l1_et1", "l2_et1", "l3_et1", "moe_h"]:
                act.sem_inc(sg(name), START)
            def norm_sqrt(name, rows, cols):
                act.wait_ge(sg("norm_ve"), NORM[name])
                nc.scalar.activation(st[0:rows, 3, 0:cols], st[0:rows, 2, 0:cols], ACT.Sqrt).then_inc(sg("norm_sd"), 1)

            norm_sqrt("gn0", C, B)
            for g in range(8):
                act.wait_ge(sg("l0_xt_ps"), g + 1)
                nc.scalar.activation(l0_xt[:, g * 4:(g + 1) * 4, :], ps[:, 4 + g % 2, 0:4 * C].rearrange("p (t c) -> p t c", c=C),
                                     ACT.Copy).then_inc(sg("l0_xt"), 1)
            act.wait_ge(sg("l0_logit"), 1)
            nc.scalar.activation(aff[:, :, :], a0[:, :, :], ACT.Exp, scale=C ** -0.5).then_inc(sg("l0_exp"), 1)
            nc.scalar.activation(st[:, 5, :], st[:, 4, :], ACT.Exp, scale=-C ** -0.5).then_inc(sg("l0_exp"), 1)
            act.wait_ge(sg("l0_qkv_ps"), 1)
            nc.scalar.activation(qkv0[:, :, :], ps[0:C, 2, 0:3 * B * M].rearrange("p (a b) -> p a b", a=3), ACT.Copy).then_inc(sg("l0_qkv"), 1)
            act.wait_ge(sg("l0_sc"), 1)
            nc.scalar.activation(pr2[:, :, :, :], pr[:, :, :, :], ACT.Exp, scale=(C // H0) ** -0.5).then_inc(sg("l0_sexp"), 1)
            act.wait_ge(sg("l0_proj_ps"), 1)
            nc.scalar.activation(s64[:, 5, :], ps[0:C, 0, 0:B * M], ACT.Identity, bias=wa("l0_pb")).then_inc(sg("l0_stf2"), 1)
            act.wait_ge(sg("l0_stft_ps"), 1)
            nc.scalar.activation(stft[:, :], ps[0:B * M, 1, 0:C], ACT.Copy).then_inc(sg("l0_stft"), 1)
            for g in range(8):
                act.wait_ge(sg("l0_at_ps"), g + 1)
                nc.scalar.activation(l0_at[:, g * 512:(g + 1) * 512], ps[0:B * M, 4 + g % 2, :], ACT.Copy).then_inc(sg("l0_at"), 1)

            def copy_scores(l, k, hh):
                nb = len(blocks(l))
                act.wait_ge(sg(f"l{l}_tr"), START + 2 * k + hh + 1)
                nc.scalar.activation(et[:, hh, 0:nb, :], ps[:, 4 + hh, 0:nb * P].rearrange("p (b q) -> p b q", q=P),
                                     ACT.Copy).then_inc(sg(f"l{l}_et{hh}"), 1)

            def exps(l, k, kp):
                act.wait_ge(sg(f"l{l}_max"), k + 1)
                if not isinstance(k, int):
                    act.wait_ge(sg(f"l{l}_tr"), START + 2 * k - 2)
                    if l == 1:
                        act.wait_ge(sg("l1_ssq"), START + k - 1)
                for hh in range(2):
                    for qc in range(TPI):
                        w = scores_cols(l, qc)
                        src = ps[:, 2 * kp + hh, qc * N:qc * N + w]
                        last = nc.scalar.activation(ee[:, kp, hh, qc, 0:w], src, ACT.Exp, bias=nmax[:, kp, hh, qc:qc + 1])
                    last.then_inc(sg(f"l{l}_exp"), 1)

            def queries(l, n, par):
                act.wait_ge(sg(f"l{l}_q_ps"), n + 1)
                if l == 1:
                    if not isinstance(n, int):
                        act.wait_ge(sg("l1_qmix"), n)
                    nc.scalar.activation(qs[:, :], ps[0:C, 7, 0:N], ACT.Copy, scale=QS).then_inc(sg("l1_q_sb"), 1)
                    nc.scalar.activation(kh[:, par, 0, :], ps[0:C, 7, N:2 * N], ACT.Copy).then_inc(sg("l1_k_sb"), 1)
                else:
                    for a in range(2):
                        bias = l3b[:, a:a + 1] if l == 3 else 0.0
                        last = nc.scalar.activation(qh[:, par, a, :], ps[0:C, 7, a * N:(a + 1) * N], ACT.Identity, bias=bias, scale=QS)
                    last.then_inc(sg(f"l{l}_q_sb"), 1)

            l3b = s64[:, 0, 0:2]
            for l in (1, 2, 3):
                if l == 1:
                    norm_sqrt("gn1", C, B)
                else:
                    norm_sqrt(f"ln{l}", P, NT)
                    for g in range(8):
                        act.wait_ge(sg("ln_t_ps"), TURN[f"ln{l}"] + g + 1)
                        nc.scalar.activation(xn[:, g * 512:(g + 1) * 512], ps[0:C, 4 + g % 4, :], ACT.Copy).then_inc(sg("xn_copied"), 1)
                    act.wait_ge(sg("xn_copied"), TURN[f"ln{l}"] + 8)
                    act.sem_inc(sg(f"l{l}_xn"), 1)
                if l == 3:
                    act.wait_ge(sg("l3_bias"), 1)
                queries(l, 0, 0)
                exps(l, 0, 0)
                with act.Fori(0, B // 2) as it:
                    for j in range(6):
                        k, n, par = it * 6 + j, it * 2 + (j // 3 + 1), 1 - j // 3
                        if l == 1:
                            copy_scores(l, k, 0)
                        copy_scores(l, k, 1)
                        if j % 3 == 0:
                            queries(l, n, par)
                        exps(l, k + 1, (j + 1) % 2)
                if l == 1:
                    act.wait_ge(sg("l1_var"), 1)
                    nc.scalar.activation(st[:, 0:3, :], st[:, 3:6, :], ACT.Sqrt).then_inc(sg("l1_sd"), 1)
                    for g in range(8):
                        act.wait_ge(sg("l1_mt_ps"), g + 1)
                        nc.scalar.activation(xn[:, g * 512:(g + 1) * 512], ps[0:C, 4 + g % 2, :], ACT.Copy).then_inc(sg("l1_mt"), 1)
                else:
                    for g in range(8):
                        act.wait_ge(sg(f"l{l}_ot_ps"), g + 1)
                        nc.scalar.activation(xn[:, g * 512:(g + 1) * 512], ps[0:C, 4 + g % 2, :], ACT.Copy).then_inc(sg(f"l{l}_ot"), 1)
                if l == 2:
                    act.wait_ge(sg("f2_z"), 1)
                    for g in range(NG):
                        n = HID // NG
                        nc.scalar.activation(wa("f2_w1")[:, g * n:(g + 1) * n], wa("f2_w1")[:, g * n:(g + 1) * n], ACT.Sign,
                                             bias=s64[:, 1, g:g + 1]).then_inc(sg("f2_w1s"), 1)
                    for g in range(NG):
                        n = C // NG
                        v = wb("f2_w2").rearrange("p (j o) -> p j o", j=NJ)[:, :, g * n:(g + 1) * n]
                        nc.scalar.activation(v, v, ACT.Sign, bias=amax[:, 3, g:g + 1]).then_inc(sg("f2_w2s"), 1)
                    norm_sqrt("lnf2", P, NT)
                    for g in range(8):
                        act.wait_ge(sg("ln_t_ps"), TURN["lnf2"] + g + 1)
                        nc.scalar.activation(xn[:, g * 512:(g + 1) * 512], ps[0:C, 4 + g % 4, :], ACT.Copy).then_inc(sg("xn_copied"), 1)
                    act.sem_inc(sg("f2_y1"), 6)
                    with act.Fori(0, NG) as g:
                        for b in range(2):
                            for j in range(NJ):
                                act.wait_ge(sg("f2_y1_ps"), g * 6 + (b * NJ + j + 1))
                                nc.scalar.activation(y1[:, j, bass.ds(g * GT + b * (GT // 2), GT // 2)], ps[:, b * NJ + j, 0:GT // 2],
                                                     ACT.Identity, bias=wb("f2_b1")[:, j:j + 1]).then_inc(sg("f2_y1"), 1)
                    for g in range(NG):
                        act.wait_ge(sg("f2_quant"), g + 1)
                        nc.scalar.activation(y1[:, :, g * GT:(g + 1) * GT], y1[:, :, g * GT:(g + 1) * GT], ACT.Gelu).then_inc(sg("f2_gelu"), 1)
            norm_sqrt("lnf3", P, NT)
            for g in range(8):
                act.wait_ge(sg("ln_t_ps"), TURN["lnf3"] + g + 1)
                nc.scalar.activation(xn[:, g * 512:(g + 1) * 512], ps[0:C, 4 + g % 4, :], ACT.Copy).then_inc(sg("xn_copied"), 1)
            act.wait_ge(sg("f3_gl"), 1)
            nc.scalar.activation(gate[:, 1, :, :], gate[:, 0, :, :], ACT.Exp).then_inc(sg("f3_gexp"), 1)
            with act.Fori(0, NT // 4) as t:
                for s in range(NE * NJ):
                    act.wait_ge(sg("moe_h_ps"), t * (NE * NJ) + (s + 1))
                    nc.scalar.activation(h3[:, s % 4, :], ps[:, 4 + s % 4, :], ACT.Gelu, bias=wb("f3_b1")[:, s:s + 1]).then_inc(sg("moe_h"), 1)

        @block.tensor
        def _(pe):
            for name in [f"l{l}_{what}" for l in (1, 2, 3) for what in ("v_ps", "s_ps", "tr", "av")]:
                pe.sem_inc(sg(name), START)
            mm = nc.tensor.matmul

            def group_sums(name):
                pe.wait_ge(sg("gn_mv"), NORM[name])
                mm(ps[0:C, 0, 0:B], wb("avg3", C), chmv[0:C, 0:B, 0], start=True, stop=True).then_inc(sg("gn_mg"), 1)
                pe.wait_ge(sg("gn_e"), NORM[name])
                mm(ps[0:C, 0, B:2 * B], wb("avg3", C), st[0:C, 1, 0:B], start=True, stop=True).then_inc(sg("gn_vg"), 1)

            def normed_to_channels(name):
                for g in range(8):
                    pe.wait_ge(sg("ln_tn"), TURN[name] + g + 1)
                    if g >= 4:
                        pe.wait_ge(sg("xn_copied"), TURN[name] + g - 3)
                    for t in range(4):
                        last = nc.tensor.transpose(ps[0:C, 4 + g % 4, t * P:(t + 1) * P], on[:, g * 4 + t, :], ident)
                    last.then_inc(sg("ln_t_ps"), 1)

            def tiles_to_channels(src, ready, done, freed, nbank):
                for g in range(8):
                    if ready is not None:
                        ready(g)
                    if g >= nbank:
                        pe.wait_ge(freed, g - nbank + 1)
                    for t in range(4):
                        last = nc.tensor.transpose(ps[0:C, 4 + g % nbank, t * P:(t + 1) * P], src[:, g * 4 + t, :], ident)
                    last.then_inc(done, 1)

            pe.wait_ge(sg("w128_loaded"), 16)
            group_sums("gn0")
            pe.wait_ge(sg("gn0_xn"), 1)
            for g in range(8):
                if g >= 2:
                    pe.wait_ge(sg("l0_xt"), g - 1)
                for t in range(4):
                    a = (g * 4 + t) * P
                    last = nc.tensor.transpose(ps[:, 4 + g % 2, t * C:(t + 1) * C], xn[:, a:a + P], wb("ident", C)[:, 0:C])
                last.then_inc(sg("l0_xt_ps"), 1)
            pe.wait_ge(sg("l0_stf"), 1)
            for t in range(NT):
                i = t // TPI
                last = mm(ps[:, 1, t * M:(t + 1) * M], xn[:, t * P:(t + 1) * P], stf[:, i * M:(i + 1) * M], start=True, stop=True)
            last.then_inc(sg("l0_logit_ps"), 1)
            pe.wait_ge(sg("l0_aff"), 1)
            pe.wait_ge(sg("ones_set"), 1)
            mm(ps[0:C, 0, 0:NT * M], ones[:, 0:C], aff[:, :, :], start=True, stop=True)
            pe.wait_ge(sg("l0_xt"), 8)
            for i in range(B):
                for t in range(TPI):
                    last = mm(ps[0:C, 3, i * M:(i + 1) * M], l0_xt[:, i * TPI + t, :], aff[:, i * TPI + t, :], start=(t == 0), stop=(t == TPI - 1))
            last.then_inc(sg("l0_sums_ps"), 1)
            pe.wait_ge(sg("l0_bd"), 1)
            pe.wait_ge(sg("w96_loaded"), 16)
            pe.wait_ge(sg("l0_stf1"), 1)
            for a, name in enumerate(("l0_q", "l0_k", "l0_v")):
                last = mm(ps[0:C, 2, a * B * M:(a + 1) * B * M], wa(name), s64[:, 2, :], start=True, stop=True)
            last.then_inc(sg("l0_qkv_ps"), 1)
            pe.wait_ge(sg("l0_prod"), 1)
            mm(ps[0:C, 1, 0:B * M * M], wb("sum12", C), pr[:, :, :, :], start=True, stop=True).then_inc(sg("l0_sc_ps"), 1)
            pe.wait_ge(sg("l0_o"), 1)
            mm(ps[0:C, 0, 0:B * M], wa("l0_p"), s64[:, 4, :], start=True, stop=True).then_inc(sg("l0_proj_ps"), 1)
            pe.wait_ge(sg("l0_stf2"), 1)
            nc.tensor.transpose(ps[0:B * M, 1, 0:C], s64[:, 5, :], wb("ident", C)[:, 0:C]).then_inc(sg("l0_stft_ps"), 1)
            for g in range(8):
                if g >= 2:
                    pe.wait_ge(sg("l0_at"), g - 1)
                for t in range(4):
                    a = (g * 4 + t) * B * M
                    last = nc.tensor.transpose(ps[0:B * M, 4 + g % 2, t * P:(t + 1) * P], l0_bd[:, a:a + B * M], ident)
                last.then_inc(sg("l0_at_ps"), 1)
            pe.wait_ge(sg("l0_stft"), 1)
            for g in range(8):
                pe.wait_ge(sg("l0_at"), g + 1)
                if g >= 2:
                    pe.wait_ge(sg("l0_res"), g - 1)
                mm(ps[0:C, 2 + g % 2, :], stft[:, :], l0_at[:, g * 512:(g + 1) * 512], start=True, stop=True).then_inc(sg("l0_out_ps"), 1)

            def score_unit(l, par, u, kp, k):
                if not isinstance(k, int):
                    pe.wait_ge(sg(f"l{l}_exp"), START + 2 * k - 2)
                if l == 1:
                    for hh in range(2):
                        for qc in range(TPI):
                            last = mm(ps[:, 2 * kp + hh, qc * N:(qc + 1) * N], qh[:, par, 2 * u + hh, qc * P:(qc + 1) * P],
                                      kh[:, par, 0, :], start=True, stop=True)
                else:
                    for qc in range(TPI):
                        w = scores_cols(l, qc)
                        for hh in range(2):
                            h = 2 * u + hh
                            r, a = 32 * (h % 3), h // 3
                            mm(ps[:, 2 * kp + hh, qc * N:qc * N + w], qh[r:r + HD, par, a, qc * P:(qc + 1) * P],
                               kh[r:r + HD, par, a, 0:w], start=True, stop=False)
                        for hh in range(2):
                            last = mm(ps[:, 2 * kp + hh, qc * N + qc * P:qc * N + (qc + 1) * P], identb[:, :], maskb[:, :], start=False, stop=True)
                last.then_inc(sg(f"l{l}_s_ps"), 1)

            def project_qk(l, n, par):
                pe.wait_ge(sg(f"l{l}_xb"), n + 1)
                if not isinstance(n, int):
                    pe.wait_ge(sg(f"l{l}_v_sb"), n)
                if l == 1:
                    mm(ps[0:C, 7, 0:N], wa("l1_q"), xb[:, par, :], start=True, stop=True)
                    mm(ps[0:C, 7, N:2 * N], wa("l1_k"), xb[:, par, :], start=True, stop=True).then_inc(sg("l1_q_ps"), 1)
                else:
                    for a in range(2):
                        last = mm(ps[0:C, 7, a * N:(a + 1) * N], wa(f"l{l}_q")[:, a * C:(a + 1) * C], xb[:, par, :], start=True, stop=True)
                    last.then_inc(sg(f"l{l}_q_ps"), 1)

            def project_k(l, n, par):
                if l == 1:
                    return
                pe.wait_ge(sg(f"l{l}_q_sb"), n + 1)
                for a in range(2):
                    last = mm(ps[0:C, 7, a * N:(a + 1) * N], wa(f"l{l}_k")[:, a * C:(a + 1) * C], xb[:, par, :], start=True, stop=True)
                last.then_inc(sg(f"l{l}_k_ps"), 1)

            def project_v(l, n, par):
                pe.wait_ge(sg(f"l{l}_q_sb"), n + 1)
                pe.wait_ge(sg(f"l{l}_k_sb"), n + 1)
                for t in range(TPI):
                    last = mm(ps[:, 7, t * C:(t + 1) * C], xb[:, par, t * P:(t + 1) * P], wa(f"l{l}_v"), start=True, stop=True)
                last.then_inc(sg(f"l{l}_v_ps"), 1)

            def keys_ready(l, n):
                pe.wait_ge(sg(f"l{l}_k_sb"), n + 1)
                pe.wait_ge(sg("l1_qmix") if l == 1 else sg(f"l{l}_q_sb"), n + 1)

            for l in (1, 2, 3):
                if l == 1:
                    group_sums("gn1")
                    pe.wait_ge(sg("l0_res"), 8)
                else:
                    normed_to_channels(f"ln{l}")
                pe.wait_ge(sg("bf_consts"), 2)
                pe.wait_ge(sg("v_ones"), 1)
                if l > 1:
                    pe.wait_ge(sg(f"l{l}_xn"), 1)
                project_qk(l, 0, 0)
                project_k(l, 0, 0)
                project_v(l, 0, 0)
                keys_ready(l, 0)
                score_unit(l, 0, 0, 0, 0)
                with pe.Fori(0, B // 2) as it:
                    for j in range(6):
                        k, u, par = it * 6 + j, j % 3, j // 3
                        i, n, npar = it * 2 + par, it * 2 + par + 1, 1 - par
                        if u < 2:
                            score_unit(l, par, u + 1, (j + 1) % 2, k + 1)
                        else:
                            keys_ready(l, n)
                            score_unit(l, npar, 0, (j + 1) % 2, k + 1)
                        for hh in range(2):
                            pe.wait_ge(sg(f"l{l}_exp"), START + 2 * k + (hh + 1))
                            pe.wait_ge(sg(f"l{l}_et{hh}"), START + k)
                            for b, (qc, tc) in enumerate(blocks(l)):
                                last = nc.tensor.transpose(ps[:, 4 + hh, b * P:(b + 1) * P], ee[:, j % 2, hh, qc, tc * P:(tc + 1) * P], ident)
                            last.then_inc(sg(f"l{l}_tr"), 1)
                        if u == 0:
                            project_qk(l, n, npar)
                        elif u == 1:
                            project_v(l, n, npar)
                        if u == 0:
                            pe.wait_ge(sg(f"l{l}_v_sb"), i + 1)
                            pe.wait_ge(sg(f"l{l}_on"), START + i)
                        for hh in range(2):
                            pe.wait_ge(sg(f"l{l}_et{hh}"), START + k + 1)
                            h = 2 * u + hh
                            for b, (qc, tc) in enumerate(blocks(l)):
                                a = (qc * NH + h) * (HD + 1)
                                last = mm(ps[:, 6, a:a + HD + 1], et[:, hh, b, :], vh[:, par, tc, h, :], start=(tc == 0),
                                          stop=(tc == (qc if l > 1 else TPI - 1)))
                            last.then_inc(sg(f"l{l}_av"), 1)
                        if u == 0:
                            project_k(l, n, npar)
                pe.wait_ge(sg(f"l{l}_exp"), START + 2 * (3 * B + 1))
                pe.wait_ge(sg(f"l{l}_v_sb"), B + 1)
                for hh in range(2):
                    pe.wait_ge(sg(f"l{l}_et{hh}"), START + 3 * B)
                if l == 1:
                    pe.wait_ge(sg("l1_on"), START + B)
                    pe.wait_ge(sg("l1_sqa"), B)
                    mm(ps[:, 0, 0:B * NH * TPI], ones[:, :], ssqa[:, :, :, :], start=True, stop=True).then_inc(sg("l1_ssq_ps"), 1)
                    pe.wait_ge(sg("l1_xsum"), 1)
                    for i in range(B):
                        last = mm(ps[:, 1 + i // 5, (i % 5) * C:(i % 5 + 1) * C], xsr[:, i, :], wa("l1_v"), start=True, stop=True)
                        if i % 5 == 4 or i == B - 1:
                            last.then_inc(sg("l1_vs_ps"), 1)
                    pe.wait_ge(sg("l1_sd"), 1)
                    tiles_to_channels(tok, lambda g: pe.wait_ge(sg(f"l1_mixed{g // 2}"), 16), sg("l1_mt_ps"), sg("l1_mt"), 2)
                    for g in range(8):
                        pe.wait_ge(sg("l1_mt"), g + 1)
                        if g >= 2:
                            pe.wait_ge(sg("l1_tok"), g - 1)
                        for t in range(4):
                            a = (g * 4 + t) * P
                            mm(ps[:, 6 + g % 2, t * C:(t + 1) * C], xc[:, a:a + P], wb("ident", C)[:, 0:C], start=True, stop=False)
                            last = mm(ps[:, 6 + g % 2, t * C:(t + 1) * C], xn[:, a:a + P], wa("l1_p"), start=False, stop=True)
                        last.then_inc(sg("l1_y_ps"), 1)
                else:
                    pe.wait_ge(sg(f"l{l}_on"), START + B)
                    tiles_to_channels(on, None, sg(f"l{l}_ot_ps"), sg(f"l{l}_ot"), 2)
                    for g in range(8):
                        pe.wait_ge(sg(f"l{l}_ot"), g + 1)
                        if g >= 2:
                            pe.wait_ge(sg(f"l{l}_tok"), g - 1)
                        for t in range(4):
                            a = (g * 4 + t) * P
                            last = mm(ps[:, 6 + g % 2, t * C:(t + 1) * C], xn[:, a:a + P], wa(f"l{l}_p"), start=True, stop=True)
                        last.then_inc(sg(f"l{l}_y_ps"), 1)
                if l == 2:
                    pe.wait_ge(sg("f2_wsum"), 2)
                    mm(ps[0:C, 0, 0:NG], ones[0:C, 0:C], s64[:, 0, 0:NG], start=True, stop=True)
                    mm(ps[:, 1, 0:NG], ones[:, :], amax[:, 2, :], start=True, stop=True).then_inc(sg("f2_wtot"), 1)
                    normed_to_channels("lnf2")
                    pe.wait_ge(sg("xn_copied"), TURN["lnf2"] + 8)
                    pe.wait_ge(sg("f2_w1z"), 1)
                    pe.wait_ge(sg("f2_w1s"), NG)
                    with pe.Fori(0, NG) as g:
                        for b in range(2):
                            for j in range(NJ):
                                pe.wait_ge(sg("f2_y1"), g * 6 + (b * NJ + j + 1))
                                mm(ps[:, b * NJ + j, 0:GT // 2], wa("f2_w1")[:, j * P:(j + 1) * P],
                                   xn[:, bass.ds(g * GT + b * (GT // 2), GT // 2)], start=True, stop=True).then_inc(sg("f2_y1_ps"), 1)
                    pe.wait_ge(sg("f2_w2s"), NG)
                    pe.wait_ge(sg("f2_w2z"), 1)
                    for g in range(NG):
                        pe.wait_ge(sg("f2_gelu"), g + 1)
                        for b in range(2):
                            if g >= 2:
                                pe.wait_ge(sg("f2_y2"), 2 * (g - 2) + b + 1)
                            for t in range(3):
                                for j in range(NJ):
                                    a = g * GT + (b * 3 + t) * P
                                    last = mm(ps[:, 4 + (g % 2) * 2 + b, t * C:(t + 1) * C], y1[:, j, a:a + P],
                                              wb("f2_w2")[:, j * C:(j + 1) * C], start=(j == 0), stop=(j == NJ - 1))
                            last.then_inc(sg("f2_y2_ps"), 1)
            normed_to_channels("lnf3")
            pe.wait_ge(sg("xn_copied"), TURN["lnf3"] + 8)
            for t in range(NT):
                last = mm(ps[:, 0, t * NE:(t + 1) * NE], xn[:, t * P:(t + 1) * P], wa("f3_gate"), start=True, stop=True)
            last.then_inc(sg("f3_gl_ps"), 1)
            pe.wait_ge(sg("f3_gl"), 1)
            NS = NE * NJ

            def hidden(t, s):
                if s >= 4:
                    pe.wait_ge(sg("moe_h"), START + t * NS + (s - 3))
                mm(ps[:, 4 + s % 4, :], wa("f3_w1")[:, s * P:(s + 1) * P], xn[:, bass.ds(t * 512, 512)],
                   start=True, stop=True).then_inc(sg("moe_h_ps"), 1)

            with pe.Fori(0, NT // 4) as t:
                for s in range(NS + 2):
                    if s < NS:
                        if s < 4:
                            pe.wait_ge(sg("moe_h"), START + t * NS)
                        hidden(t, s)
                    if s >= 2:
                        r = s - 2
                        e, j = r // NJ, r % NJ
                        pe.wait_ge(sg("moe_h"), START + t * NS + (r + 1))
                        for q in range(4):
                            if r == 0:
                                pe.wait_ge(sg("moe_y"), START + t * 4)
                            last = mm(ps[:, q, e * C:(e + 1) * C], h3[:, r % 4, q * P:(q + 1) * P],
                                      wb("f3_w2")[:, r * C:(r + 1) * C], start=(j == 0), stop=(j == NJ - 1))
                last.then_inc(sg("moe_y_ps"), 1)

        @block.vector
        def _(dve):
            for name in ["l1_ssq", "l1_on", "l2_on", "l3_on", "l2_et0", "l3_et0", "moe_y"]:
                dve.sem_inc(sg(name), START)
            V = nc.vector
            chain = [0]

            def link(ins):
                chain[0] += 1
                ins.then_inc(sg("dve_chain"), 1)
                dve.wait_ge(sg("dve_chain"), chain[0])

            def group_norm(name):
                for i in range(B):
                    if name == "gn0" and i % 4 == 0:
                        dve.wait_ge(sg(f"x_loaded{i // 4}"), 16)
                    last = V.bn_stats(chst[0:C, i, :], xc[:, i * N:(i + 1) * N])
                link(last)
                for i in range(B):
                    last = V.bn_aggr(chmv[0:C, i, :], chst[0:C, i, :])
                last.then_inc(sg("gn_mv"), 1)
                dve.wait_ge(sg("gn_mv"), NORM[name])
                dve.wait_ge(sg("gn_mg"), NORM[name])
                link(V.tensor_copy(st[0:C, 4, 0:B], ps[0:C, 0, 0:B]))
                link(V.tensor_tensor(st[0:C, 0, 0:B], chmv[0:C, 0:B, 0], st[0:C, 4, 0:B], ALU.subtract))
                link(V.tensor_tensor(st[0:C, 1, 0:B], st[0:C, 0, 0:B], st[0:C, 0, 0:B], ALU.mult))
                V.tensor_tensor(st[0:C, 1, 0:B], st[0:C, 1, 0:B], chmv[0:C, 0:B, 1], ALU.add).then_inc(sg("gn_e"), 1)
                dve.wait_ge(sg("gn_vg"), NORM[name])
                V.tensor_scalar(st[0:C, 2, 0:B], ps[0:C, 0, B:2 * B], 1e-5, None, ALU.add).then_inc(sg("norm_ve"), 1)
                dve.wait_ge(sg("norm_sd"), NORM[name])
                link(V.reciprocal(st[0:C, 5, 0:B], st[0:C, 3, 0:B]))
                link(V.scalar_tensor_tensor(out=st[0:C, 6, 0:B], in0=st[0:C, 4, 0:B], scalar=-1.0, in1=st[0:C, 5, 0:B], op0=ALU.mult, op1=ALU.mult))
                for i in range(B):
                    last = V.tensor_scalar(xn[:, i * N:(i + 1) * N], xc[:, i * N:(i + 1) * N], st[0:C, 5, i:i + 1], st[0:C, 6, i:i + 1], ALU.mult, ALU.add)
                return last

            def layer_norm(name):
                for t in range(NT):
                    last = V.bn_stats(chst[:, t, :], tok[:, t, :])
                link(last)
                for t in range(NT):
                    last = V.bn_aggr(chmv[:, t, :], chst[:, t, :])
                link(last)
                V.tensor_scalar(st[:, 2, :], chmv[:, :, 1], 1e-5, None, ALU.add).then_inc(sg("norm_ve"), 1)
                dve.wait_ge(sg("norm_sd"), NORM[name])
                link(V.reciprocal(st[:, 5, :], st[:, 3, :]))
                link(V.scalar_tensor_tensor(out=st[:, 6, :], in0=chmv[:, :, 0], scalar=-1.0, in1=st[:, 5, :], op0=ALU.mult, op1=ALU.mult))
                for t in range(NT):
                    last = V.tensor_scalar(on[:, t, :], tok[:, t, :], st[:, 5, t:t + 1], st[:, 6, t:t + 1], ALU.mult, ALU.add)
                    if t % 4 == 3:
                        last.then_inc(sg("ln_tn"), 1)

            group_norm("gn0").then_inc(sg("gn0_xn"), 1)
            dve.wait_ge(sg("gn0_xn"), 1)
            link(V.tensor_reduce(out=rowsum[:, :], in_=xn[:, 0:B * N].rearrange("p (a w) -> p a w", w=SB), axis=AX.X, op=ALU.add))
            link(V.tensor_reduce(out=stf[:, :].rearrange("p (g w) -> p g w", w=WW // SB),
                                 in_=rowsum[:, :].rearrange("p (g h w) -> p g w h", h=SB, w=WW // SB), axis=AX.X, op=ALU.add))
            V.tensor_scalar(stf[:, :], stf[:, :], 1.0 / (SB * SB), None, ALU.mult).then_inc(sg("l0_stf"), 1)
            dve.wait_ge(sg("l0_logit_ps"), 1)
            lg = ps[:, 1, 0:NT * M].rearrange("p (t m) -> p t m", m=M)
            link(V.tensor_reduce(out=st[:, 4, :], in_=lg, axis=AX.X, op=ALU.max))
            link(V.tensor_scalar(st[:, 4, :], st[:, 4, :], 0.0, None, ALU.max))
            V.tensor_tensor(a0[:, :, :], lg, last_dim(st[:, 4, :], M), ALU.subtract).then_inc(sg("l0_logit"), 1)
            dve.wait_ge(sg("l0_exp"), 2)
            link(V.tensor_reduce(out=st[:, 6, :], in_=aff[:, :, :], axis=AX.X, op=ALU.add))
            link(V.scalar_tensor_tensor(out=st[:, 6, :], in0=st[:, 5, :], scalar=float(9 - M), in1=st[:, 6, :], op0=ALU.mult, op1=ALU.add))
            link(V.reciprocal(st[:, 7, :], st[:, 6, :]))
            V.tensor_tensor(aff[:, :, :], aff[:, :, :], last_dim(st[:, 7, :], M), ALU.mult).then_inc(sg("l0_aff"), 1)
            dve.wait_ge(sg("bd_zeroed"), 1)
            dve.wait_ge(sg("l0_aff"), 1)
            bd = l0_bd.rearrange("p (i x) -> p i x", x=bd_w)[:, :, 0:2 * B * M].rearrange("p i (t x) -> p i t x", t=TPI)[:, :, :, 0:M]
            V.tensor_copy(bd, aff[:, :, :].rearrange("p (i t) m -> p i t m", t=TPI)).then_inc(sg("l0_bd"), 1)
            dve.wait_ge(sg("l0_sums_ps"), 1)
            link(V.tensor_reduce(out=s64[:, 0, :].rearrange("p (i m) -> p i m", m=M),
                                 in_=ps[0:C, 0, 0:NT * M].rearrange("p (i t m) -> p i m t", t=TPI, m=M), axis=AX.X, op=ALU.add))
            link(V.tensor_scalar(s64[:, 0, :], s64[:, 0, :], 1e-12, None, ALU.add))
            link(V.reciprocal(s64[:, 1, :], s64[:, 0, :]))
            V.tensor_tensor(s64[:, 2, :], ps[0:C, 3, 0:B * M], s64[:, 1, :], ALU.mult).then_inc(sg("l0_stf1"), 1)
            dve.wait_ge(sg("l0_qkv"), 1)
            q0, k0, v0 = (qkv0[:, a, :].rearrange("p (i m) -> p i m", m=M) for a in range(3))
            V.tensor_tensor(pr[:, :, :, :], last_dim(q0, M), mid_dim(k0, 2, M), ALU.mult).then_inc(sg("l0_prod"), 1)
            dve.wait_ge(sg("l0_sc_ps"), 1)
            sc = ps[0:C, 1, 0:B * M * M].rearrange("p (a n) -> p a n", n=M)
            link(V.tensor_reduce(out=s64[:, 3, :], in_=sc, axis=AX.X, op=ALU.max))
            pr_f = pr[:, :, :, :].rearrange("p i m n -> p (i m) n")
            pr2_f = pr2[:, :, :, :].rearrange("p i m n -> p (i m) n")
            V.tensor_tensor(pr_f, sc, last_dim(s64[:, 3, :], M), ALU.subtract).then_inc(sg("l0_sc"), 1)
            dve.wait_ge(sg("l0_sexp"), 1)
            link(V.tensor_reduce(out=s64[:, 3, :], in_=pr2_f, axis=AX.X, op=ALU.add))
            link(V.reciprocal(s64[:, 1, :], s64[:, 3, :]))
            link(V.tensor_tensor(pr_f, pr2_f, last_dim(s64[:, 1, :], M), ALU.mult))
            link(V.tensor_tensor(pr2[:, :, :, :], pr[:, :, :, :], mid_dim(v0, 2, M), ALU.mult))
            V.tensor_reduce(out=s64[:, 4, :], in_=pr2_f, axis=AX.X, op=ALU.add).then_inc(sg("l0_o"), 1)
            for g in range(8):
                dve.wait_ge(sg("l0_out_ps"), g + 1)
                V.tensor_tensor(xc[:, g * 512:(g + 1) * 512], ps[0:C, 2 + g % 2, :], xc[:, g * 512:(g + 1) * 512], ALU.add).then_inc(sg("l0_res"), 1)
            dve.wait_ge(sg("l0_res"), 8)

            def maxima(l, k, kp):
                dve.wait_ge(sg(f"l{l}_s_ps"), START + k + 1)
                if l == 1:
                    src = ps[:, 2 * kp:2 * kp + 2, :].rearrange("p h (q t) -> p (h q) t", q=TPI)
                    V.tensor_reduce(out=nmax[:, kp, :, :].rearrange("p h q -> p (h q)"), in_=src, axis=AX.X, op=ALU.max, negate=True).then_inc(sg("l1_max"), 1)
                else:
                    for qc in range(TPI):
                        last = V.tensor_reduce(out=nmax[:, kp, :, qc], in_=ps[:, 2 * kp:2 * kp + 2, qc * N:qc * N + scores_cols(l, qc)],
                                               axis=AX.X, op=ALU.max, negate=True)
                    last.then_inc(sg(f"l{l}_max"), 1)

            def keys(l, n, par):
                if l == 1:
                    return
                dve.wait_ge(sg(f"l{l}_k_ps"), n + 1)
                src = ps[0:C, 7, :].rearrange("p (a t) -> p a t", a=2)
                if l == 2:
                    V.tensor_copy(kh[:, par, :, :], src).then_inc(sg("l2_k_sb"), 1)
                else:
                    for a in range(2):
                        last = V.tensor_scalar(kh[:, par, a, :], src[:, a, :], wa("l3_kb")[:, a:a + 1], None, ALU.add)
                    last.then_inc(sg("l3_k_sb"), 1)

            def values(l, n, par):
                dve.wait_ge(sg(f"l{l}_v_ps"), START + n + 1)
                if not isinstance(n, int):
                    dve.wait_ge(sg(f"l{l}_av"), START + n * 6 - 6)
                src = ps[:, 7, 0:TPI * C].rearrange("p (t h d) -> p t h d", t=TPI, d=HD)
                if l < 3:
                    V.tensor_copy(vh[:, par, :, :, 0:HD], src).then_inc(sg(f"l{l}_v_sb"), 1)
                else:
                    for t in range(TPI):
                        last = V.tensor_tensor(vh[:, par, t, :, 0:HD], src[:, t], wb("l3_vb").rearrange("p (h d) -> p h d", d=HD), ALU.add)
                    last.then_inc(sg("l3_v_sb"), 1)

            for l in (1, 2, 3):
                if l == 1:
                    group_norm("gn1").then_inc(sg("l1_xn"), 1)
                    dve.wait_ge(sg("l1_xn"), 1)
                    link(V.tensor_tensor(st[0:C, 7, 0:B], chmv[0:C, 0:B, 0], st[0:C, 5, 0:B], ALU.mult))
                    link(V.tensor_tensor(st[0:C, 7, 0:B], st[0:C, 7, 0:B], st[0:C, 6, 0:B], ALU.add))
                    link(V.tensor_scalar(st[0:C, 7, 0:B], st[0:C, 7, 0:B], float(N), None, ALU.mult))
                    V.tensor_copy(xsr, last_dim(st[0:C, 7, 0:B], P)).then_inc(sg("l1_xsum"), 1)
                else:
                    layer_norm(f"ln{l}")
                if l == 3:
                    V.tensor_scalar(s64[:, 0, 0:2], wa("l3_qb"), QS, None, ALU.mult).then_inc(sg("l3_bias"), 1)
                keys(l, 0, 0)
                values(l, 0, 0)
                maxima(l, 0, 0)
                per = 4 if l == 1 else 2
                base = chain[0]
                with dve.Fori(0, B // 2) as it:
                    for j in range(6):
                        k, u, par = it * 6 + j, j % 3, j // 3
                        i, n, npar = it * 2 + par, it * 2 + par + 1, 1 - par
                        maxima(l, k + 1, (j + 1) % 2)
                        if l > 1:
                            nb = len(blocks(l))
                            dve.wait_ge(sg(f"l{l}_tr"), START + 2 * k + 1)
                            V.tensor_copy(et[:, 0, 0:nb, :], ps[:, 4, 0:nb * P].rearrange("p (b q) -> p b q", q=P)).then_inc(sg(f"l{l}_et0"), 1)
                        if u == 0:
                            keys(l, n, npar)
                        elif u == 1:
                            values(l, n, npar)
                        if l == 1:
                            dve.wait_ge(sg("l1_exp"), START + 2 * k + 2)
                            dve.wait_ge(sg("l1_ssq"), START + k)
                            for hh in range(2):
                                for qc in range(TPI):
                                    last = V.tensor_tensor_reduce(out=sqj[:, hh, qc, :], in0=ee[:, j % 2, hh, qc, :], in1=ee[:, j % 2, hh, qc, :],
                                                                  scale=1.0, scalar=0.0, op0=ALU.mult, op1=ALU.add,
                                                                  accum_out=ssq[:, par, 2 * u + hh, qc:qc + 1])
                            last.then_inc(sg("l1_ssq"), 1)
                        if u == 2:
                            dve.wait_ge(sg(f"l{l}_av"), START + 2 * k + 2)
                            o = ps[:, 6, 0:TPI * NH * (HD + 1)].rearrange("p (q h d) -> p q h d", q=TPI, d=HD + 1)
                            V.reciprocal(rden[:, par, :, :], o[:, :, :, HD]).then_inc(sg(f"l{l}_rden"), 1)
                            dve.wait_ge(sg(f"l{l}_rden"), i + 1)
                            for q in range(TPI):
                                last = V.tensor_tensor(on[:, bass.ds(i * TPI + q, 1), :].rearrange("p a (h d) -> p (a h) d", d=HD), o[:, q, :, 0:HD],
                                                       last_dim(rden[:, par, q, :], HD), ALU.mult)
                            last.then_inc(sg(f"l{l}_on"), 1)
                            if l == 1:
                                rd = rden[:, par, :, :].rearrange("p q h -> p h q")
                                dve.wait_ge(sg("l1_ssq"), START + k + 1)
                                V.tensor_tensor(sqw[:, par, :, :], ssq[:, par, :, :], rd, ALU.mult).then_inc(sg("l1_sqw"), 1)
                                dve.wait_ge(sg("l1_sqw"), i + 1)
                                V.tensor_tensor(ssqa[:, bass.ds(i, 1), :, :].rearrange("p a h q -> p (a h) q"), sqw[:, par, :, :], rd, ALU.mult).then_inc(sg("l1_sqa"), 1)
                if l == 1:
                    dve.wait_ge(sg("l1_ssq_ps"), 1)
                    var = junk[:, 0:B * NH]
                    sd = junk[:, 96:96 + B * NH]
                    link(V.tensor_reduce(out=var, in_=ps[:, 0, 0:B * NH * TPI].rearrange("p (a q) -> p a q", q=TPI), axis=AX.X, op=ALU.add))
                    V.tensor_scalar(st[:, 3:6, :].rearrange("p a b -> p (a b)"), var, 1.0 / (N * N), 1e-5 - 1.0 / (N * N), ALU.mult, ALU.add).then_inc(sg("l1_var"), 1)
                    dve.wait_ge(sg("l1_sd"), 1)
                    link(V.reciprocal(var, st[:, 0:3, :].rearrange("p a b -> p (a b)")))
                    v3 = var.rearrange("p (i g) -> p i g", g=NH)
                    s3 = sd.rearrange("p (i g) -> p i g", g=NH)
                    link(V.tensor_tensor(v3, v3, mid_dim(wb("l1_gamma"), 1, B), ALU.mult))
                    link(V.scalar_tensor_tensor(out=s3, in0=v3, scalar=-1.0 / N, in1=mid_dim(wb("l1_beta"), 1, B), op0=ALU.mult, op1=ALU.add))
                    dve.wait_ge(sg("l1_vs_ps"), 4)
                    on5 = on[:, :, :].rearrange("p (i q) (g d) -> p i q g d", q=TPI, d=HD)
                    vo = big[:, 0:B * C].rearrange("p (i g d) -> p i g d", g=NH, d=HD)
                    for c in range(4):
                        n = min(5, B - 5 * c)
                        last = V.tensor_tensor(vo[:, 5 * c:5 * c + n], ps[:, 1 + c, 0:n * C].rearrange("p (i g d) -> p i g d", g=NH, d=HD),
                                               last_dim(s3[:, 5 * c:5 * c + n], HD), ALU.mult)
                    link(last)
                    for r in range(4):
                        i0, i1 = 4 * r, 4 * r + 4
                        for q in range(TPI):
                            last = V.tensor_tensor(on5[:, i0:i1, q], on5[:, i0:i1, q], last_dim(v3[:, i0:i1], HD), ALU.mult)
                        link(last)
                        for q in range(TPI):
                            last = V.tensor_tensor(on5[:, i0:i1, q], on5[:, i0:i1, q], vo[:, i0:i1], ALU.add)
                        last.then_inc(sg("l1_out"), 1)
                    bias = "l1_pb"
                else:
                    bias = "l3_pb"
                for g in range(8):
                    dve.wait_ge(sg(f"l{l}_y_ps"), g + 1)
                    y = ps[:, 6 + g % 2, 0:4 * C].rearrange("p (t c) -> p t c", c=C)
                    tv = tok[:, g * 4:(g + 1) * 4, :]
                    if l == 1:
                        V.tensor_tensor(tv, y, mid_dim(wb("l1_pb"), 1, 4), ALU.add).then_inc(sg("l1_tok"), 1)
                    elif l == 2:
                        V.tensor_tensor(tv, y, tv, ALU.add).then_inc(sg("l2_tok"), 1)
                    else:
                        link(V.tensor_tensor(tv, tv, mid_dim(wb("l3_pb"), 1, 4), ALU.add))
                        V.tensor_tensor(tv, y, tv, ALU.add).then_inc(sg("l3_tok"), 1)
                dve.wait_ge(sg(f"l{l}_tok"), 8)
                if l == 2:
                    n1, n2 = HID // NG, C // NG
                    V.tensor_reduce(out=s64[:, 0, 0:NG], in_=wa("f2_w1")[:, 0:NG * n1].rearrange("p (g o) -> p g o", g=NG), axis=AX.X, op=ALU.add).then_inc(sg("f2_wsum"), 1)
                    w2v = wb("f2_w2").rearrange("p (j o) -> p j o", j=NJ)
                    for j in range(NJ):
                        last = V.tensor_reduce(out=cmp[:, j, 0:NG], in_=w2v[:, j, 0:NG * n2].rearrange("p (g o) -> p g o", g=NG), axis=AX.X, op=ALU.add)
                    link(last)
                    V.tensor_reduce(out=amax[:, 2, :], in_=cmp[:, 0:NJ, 0:NG].rearrange("p j g -> p g j"), axis=AX.X, op=ALU.add).then_inc(sg("f2_wsum"), 1)
                    dve.wait_ge(sg("f2_wtot"), 1)
                    V.tensor_scalar(s64[:, 1, 0:NG], ps[0:C, 0, 0:NG], -1.0 / (n1 * C), None, ALU.mult)
                    V.tensor_scalar(amax[:, 3, :], ps[:, 1, 0:NG], -1.0 / (n2 * HID), None, ALU.mult).then_inc(sg("f2_z"), 1)
                    V.memset(wa("f2_w1")[:, NG * n1:HID], 0.0).then_inc(sg("f2_w1z"), 1)
                    V.memset(w2v[:, :, NG * n2:C], 0.0).then_inc(sg("f2_w2z"), 1)
                    layer_norm("lnf2")
                    with dve.Fori(0, NG) as g:
                        dve.wait_ge(sg("f2_y1"), g * 6 + 12)
                        V.tensor_reduce(out=amax[:, 0, bass.ds(g, 1)], in_=y1[:, :, bass.ds(g * GT, GT)], axis=AX.XY, op=ALU.max,
                                        apply_absolute_value=True).then_inc(sg("f2_am"), 1)
                    dve.wait_ge(sg("f2_am"), NG)
                    dve.wait_ge(sg("f2_w2s"), NG)
                    dve.sem_inc(sg("f2_amax0"), 1)

                    def quant_scale(k):
                        dve.wait_ge(sg(f"f2_gmax{k}"), 1)
                        link(V.tensor_scalar(amax[:, 2 * k + 1, :], amax[:, 2 * k + 1, :], QEPS, None, ALU.add))
                        link(V.reciprocal(amax[:, 2 * k, :], amax[:, 2 * k + 1, :]))
                        link(V.tensor_scalar(amax[:, 2 * k, :], amax[:, 2 * k, :], QB, None, ALU.mult))

                    quant_scale(0)
                    for g in range(NG):
                        v = y1[:, :, g * GT:(g + 1) * GT]
                        link(V.tensor_scalar(v, v, amax[:, 0, g:g + 1], QB - QEPS, ALU.mult, ALU.min))
                        V.tensor_scalar(v, v, -QB + QEPS, None, ALU.max).then_inc(sg("f2_quant"), 1)
                    for g in range(NG):
                        for b in range(2):
                            dve.wait_ge(sg("f2_y2_ps"), 2 * g + b + 1)
                            t0 = g * 6 + b * 3
                            V.tensor_tensor(y2[:, t0:t0 + 3, :], ps[:, 4 + (g % 2) * 2 + b, 0:3 * C].rearrange("p (t c) -> p t c", c=C),
                                            mid_dim(wb("f2_b2"), 1, 3), ALU.add).then_inc(sg("f2_y2"), 1)
                        dve.wait_ge(sg("f2_y2"), 2 * g + 2)
                        last = V.tensor_reduce(out=amax[:, 2, g:g + 1], in_=y2[:, g * 6:(g + 1) * 6, :], axis=AX.XY, op=ALU.max, apply_absolute_value=True)
                    last.then_inc(sg("f2_amax1"), 1)
                    quant_scale(1)
                    for g in range(NG):
                        v, tv = y2[:, g * 6:(g + 1) * 6, :], tok[:, g * 6:(g + 1) * 6, :]
                        link(V.tensor_scalar(v, v, amax[:, 2, g:g + 1], QB - QEPS, ALU.mult, ALU.min))
                        link(V.scalar_tensor_tensor(out=tv, in0=v, scalar=-QB + QEPS, in1=tv, op0=ALU.max, op1=ALU.add))
            layer_norm("lnf3")
            dve.wait_ge(sg("f3_gl_ps"), 1)
            gl, ge = gate[:, 0, :, :], gate[:, 1, :, :]
            link(V.tensor_tensor(gl, ps[:, 0, 0:NT * NE].rearrange("p (t e) -> p t e", e=NE), mid_dim(wb("f3_gateb"), 1, NT), ALU.add))
            link(V.tensor_reduce(out=st[:, 0, :], in_=gl, axis=AX.X, op=ALU.max))
            V.tensor_tensor(gl, gl, last_dim(st[:, 0, :], NE), ALU.subtract).then_inc(sg("f3_gl"), 1)
            dve.wait_ge(sg("f3_gexp"), 1)
            link(V.tensor_reduce(out=st[:, 0, :], in_=ge, axis=AX.X, op=ALU.add))
            link(V.reciprocal(st[:, 1, :], st[:, 0, :]))
            link(V.tensor_tensor(gl, ge, last_dim(st[:, 1, :], NE), ALU.mult))
            pairs = [(0, 1), (0, 2), (0, 3), (1, 2), (1, 3), (2, 3)]
            c = {ab: cmp[:, n, :] for n, ab in enumerate(pairs)}
            for a, b in pairs:
                last = V.tensor_tensor(c[a, b], gate[:, 0, :, a], gate[:, 0, :, b], ALU.is_ge)
            link(last)
            terms = [([(0, 1), (0, 2), (0, 3)], [], ALU.is_gt, 1.5), ([(0, 1)], [(1, 2), (1, 3)], ALU.is_lt, -0.5),
                     ([(0, 2), (1, 2)], [(2, 3)], ALU.is_lt, 0.5), ([(0, 3), (1, 3), (2, 3)], [], ALU.is_lt, 1.5)]
            for e, (plus, minus, _, _) in enumerate(terms):
                (x, y), z = (plus + minus)[:2], (plus + minus)[2]
                V.tensor_tensor(gsel[:, e, :], c[x], c[y], ALU.add if y in plus else ALU.subtract)
            link(V.memset(junk[:, 0:1], 0.0))
            for e, (plus, minus, _, _) in enumerate(terms):
                z = (plus + minus)[2]
                V.tensor_tensor(gsel[:, e, :], gsel[:, e, :], c[z], ALU.add if z in plus else ALU.subtract)
            link(V.memset(junk[:, 0:1], 0.0))
            for e, (_, _, op, edge) in enumerate(terms):
                last = V.scalar_tensor_tensor(out=gate[:, 1, :, e], in0=gsel[:, e, :], scalar=edge, in1=gate[:, 0, :, e], op0=op, op1=ALU.mult)
            link(last)
            link(V.tensor_reduce(out=st[:, 0, :], in_=ge, axis=AX.X, op=ALU.add))
            link(V.tensor_scalar(st[:, 0, :], st[:, 0, :], 1e-9, None, ALU.add))
            link(V.reciprocal(st[:, 1, :], st[:, 0, :]))
            link(V.tensor_tensor(gl, ge, last_dim(st[:, 1, :], NE), ALU.mult))
            with dve.Fori(0, NT // 4) as t:
                dve.wait_ge(sg("moe_y_ps"), t + 1)
                for q in range(4):
                    tile = t * 4 + q
                    V.tensor_tensor(ysc[:, :, :], ps[:, q, 0:NE * C].rearrange("p (e c) -> p e c", e=NE),
                                    wb("f3_b2").rearrange("p (e c) -> p e c", e=NE), ALU.add).then_inc(sg("moe_y"), 1)
                    dve.wait_ge(sg("moe_y"), START + tile + 1)
                    V.tensor_tensor(ysc[:, :, :], ysc[:, :, :], last_dim(gate[:, 0, bass.ds(tile, 1), :].rearrange("p a e -> p (a e)"), C), ALU.mult).then_inc(sg("moe_w"), 1)
                    dve.wait_ge(sg("moe_w"), tile + 1)
                    V.tensor_reduce(out=junk[:, 0:C], in_=ysc[:, :, :].rearrange("p e c -> p c e"), axis=AX.X, op=ALU.add).then_inc(sg("moe_s"), 1)
                    dve.wait_ge(sg("moe_s"), tile + 1)
                    tv = tok[:, bass.ds(tile, 1), :].rearrange("p a c -> p (a c)")
                    last = V.tensor_tensor(tv, junk[:, 0:C], tv, ALU.add)
                last.then_inc(sg("moe_block"), 1)


def kernel(**inputs):
    from concourse import bacc
    from concourse.bass_utils import run_bass_kernel_spmd

    def get(name):
        return np.asarray(inputs[name])

    def heads_apart(w):
        out = np.zeros((w.shape[0], NH, 2 * HD), w.dtype)
        out[:, :, :HD] = w.reshape(w.shape[0], NH, HD)
        return out.reshape(w.shape[0], 2 * C)

    d0 = C // H0
    w0 = get("L0_conv_qkv_w").reshape(H0, 3, d0, C)
    w2, w3, b3 = get("L2_attn_w_attn"), get("L3_attn_qkv_w").T, get("L3_attn_qkv_b")
    parts96 = {
        "l0_q": w0[:, 0].reshape(C, C).T, "l0_k": w0[:, 1].reshape(C, C).T, "l0_v": w0[:, 2].reshape(C, C).T,
        "l0_p": get("L0_conv_proj_w").T, "l0_pb": get("L0_conv_proj_b")[:, None],
        "l1_q": get("L1_conv_Wq").T, "l1_k": get("L1_conv_Wk").T, "l1_v": get("L1_conv_Wv").T,
        "l1_hw": np.repeat(get("L1_conv_head_w").T, HD, axis=0), "l1_p": get("L1_conv_projW").T,
        "l2_q": heads_apart(w2[:, :C]), "l2_k": heads_apart(w2[:, C:2 * C]), "l2_v": w2[:, 2 * C:], "l2_p": get("L2_attn_w_proj"),
        "f2_w1": get("L2_ffn_W1").T,
        "l3_q": heads_apart(w3[:, :C]), "l3_k": heads_apart(w3[:, C:2 * C]), "l3_v": w3[:, 2 * C:], "l3_p": get("L3_attn_out_w").T,
        "l3_qb": heads_apart(b3[None, :C]).reshape(2, C).T, "l3_kb": heads_apart(b3[None, C:2 * C]).reshape(2, C).T,
        "f3_gate": get("L3_ffn_gate_w"), "f3_w1": get("L3_ffn_w1").transpose(1, 0, 2).reshape(C, NE * HID),
    }

    def rows(v):
        return np.broadcast_to(v.reshape(1, -1), (P, v.size))

    def padded(m):
        out = np.zeros((P, m.shape[1]), m.dtype)
        out[:m.shape[0]] = m
        return out

    f = np.float32
    parts128 = {
        "ident": np.eye(P, dtype=f),
        "avg3": padded(np.kron(np.eye(32, dtype=f), np.full((3, 3), 1 / 3, f))),
        "sum12": padded(np.kron(np.eye(H0, dtype=f), np.ones((d0, d0), f))),
        "mask": np.triu(np.full((P, P), NEG, f), 1),
        "l1_pb": rows(get("L1_conv_projb")), "l1_gamma": rows(get("L1_conv_gamma")), "l1_beta": rows(get("L1_conv_beta")),
        "f2_b1": get("L2_ffn_b1").reshape(NJ, P).T, "f2_w2": get("L2_ffn_W2").T.reshape(NJ, P, C).transpose(1, 0, 2).reshape(P, -1),
        "f2_b2": rows(get("L2_ffn_b2")), "l3_vb": rows(b3[2 * C:]), "l3_pb": rows(get("L3_attn_out_b")),
        "f3_gateb": rows(get("L3_ffn_gate_b")), "f3_b1": get("L3_ffn_b1").reshape(NE * NJ, P).T,
        "f3_w2": get("L3_ffn_w2").reshape(NE * NJ, P, C).transpose(1, 0, 2).reshape(P, -1), "f3_b2": rows(get("L3_ffn_b2")),
    }
    arrays = {
        "x_in": np.ascontiguousarray(get("x").transpose(1, 0, 2, 3).reshape(C, B * N)),
        "w96_in": np.ascontiguousarray(np.concatenate([parts96[n].reshape(C, -1) for n, _ in W96], axis=1)),
        "w128_in": np.ascontiguousarray(np.concatenate([parts128[n].reshape(P, -1) for n, _ in W128], axis=1)),
    }
    nc = bacc.Bacc("TRN2", target_bir_lowering=False, num_devices=1)
    args = [nc.dram_tensor(n, a.shape, mybir.dt.from_np(a.dtype), kind="ExternalInput").ap() for n, a in arrays.items()]
    out = nc.dram_tensor("out", [P, NT, C], F32, kind="ExternalOutput").ap()
    hybrid_kernel(nc, *args, out)
    got = run_bass_kernel_spmd(nc, [arrays], core_ids=[0]).results[0]["out"]
    return np.ascontiguousarray(got.transpose(1, 0, 2).reshape(B, N, C).transpose(0, 2, 1)).reshape(B, C, HH, WW)
```

```python
import numpy as np
from contextlib import ExitStack

import concourse.bass as bass
from concourse import mybir

F32 = mybir.dt.float32
BF16 = mybir.dt.bfloat16
F32R = mybir.dt.float32r
ALU = mybir.AluOpType
ACT = mybir.ActivationFunctionType
AX = mybir.AxisListType

B, C, HH, WW = 16, 96, 16, 16
N = HH * WW
P = 128
NT = B * N // P
TPI = N // P
SB = 8
M = (HH // SB) * (WW // SB)
H0 = 8
NH, HD = 6, 16
QS = HD ** -0.5
HID = 4 * C
NJ = HID // P
NG = 5
GI = B // NG
GT = GI * N
NE = 4
QB = 128.0
QEPS = 1e-5
STK = 16 * 6
START = 1
TR0 = 3
NEG = -1e30

ONE = C
W96 = [("l0_q", C), ("l0_k", C), ("l0_v", C), ("l0_p", C), ("l0_pb", 1),
       ("l1_q", C), ("l1_k", C), ("l1_v", C), ("l1_hw", NH), ("l1_p", C),
       ("l2_q", C), ("l2_k", C), ("l2_v", C), ("l2_p", 2 * C),
       ("f2_w1", HID),
       ("l3_q", C), ("l3_k", C), ("l3_v", C), ("l3_p", 2 * C),
       ("f3_gate", NE), ("f3_w1", NE * HID)]
W128 = [("ident", P), ("avg3", C), ("sum12", C), ("mask", P),
        ("l1_gamma", NH), ("l1_beta", NH),
        ("f2_w2", NJ * C), ("f2_b2", C), ("f3_w2", NE * NJ * C), ("f3_b2", NE * C)]


def columns(parts):
    at, where = 0, {}
    for name, n in parts:
        where[name] = (at, at + n)
        at += n
    return where, at


NORM = {"gn0": 1, "gn1": 2, "ln2": 3, "lnf2": 4, "ln3": 5, "lnf3": 6}
TURN = {"ln2": 0, "lnf2": 8, "ln3": 16, "lnf3": 24}


LOOP_ADDS = {"xb": B + 2, "q_ps": B + 2, "hi": B + 2, "lo": B + 2, "stacked": STK * (B + 2), "v_ps": B + 1, "v_sb": B + 1,
             "s_ps": 3 * B + 2, "max": 3 * B + 2, "exp": 6 * B + 2, "rec": 3 * B + 1, "norm": 6 * B + 2, "tr": 6 * B, "et0": 3 * B, "et1": 3 * B,
             "av": B + 1, "ot": B + 1, "out_ps": B + 1, "added": B + 1}


C96, N96 = columns(W96)
C128, N128 = columns(W128)


def hybrid_kernel(nc, x_d, w96_d, w128_d, out_d):
    ctx = ExitStack()
    with ctx:
        def sb(name, shape, dt=F32):
            return ctx.enter_context(nc.sbuf_tensor(name, shape, dt))

        sems = {}

        def sg(name):
            if name not in sems:
                sems[name] = ctx.enter_context(nc.semaphore(name))
            return sems[name]

        def own(l, what):
            return sg(f"l1_{what}" if l == 1 else f"causal_{what}")

        def upto(l, what, count):
            return own(l, what), count + (LOOP_ADDS[what] if l == 3 else 0)

        mix_d = nc.dram_tensor("l1_mix", [B, NH, N, HD], F32, kind="Internal").ap()

        w96 = sb("w96", [P, N96])
        w128 = sb("w128", [P, N128])
        xc = sb("xc", [C, B * N])
        xn = sb("xn", [P, (B + 2) * N])
        tok_all = sb("tok", [P, TPI + NT, C])
        tok = tok_all[:, TPI:, :]
        on_all = sb("on", [P, TPI + NT, C])
        on = on_all[:, TPI:, :]
        big = sb("big", [P, NJ * NG * GT])
        ones = sb("ones", [P, P])
        identb = sb("identb", [P, P], BF16)
        maskb = sb("maskb", [P, P], BF16)
        chst = sb("chst", [P, NT, 6])
        chmv = sb("chmv", [P, NT, 2])
        st = sb("st", [P, 8, NT])
        xb = sb("xb", [P, 2, N])
        qs = sb("qs", [C, N])
        kh = sb("kh", [P, 2, N])
        hi = sb("hi", [C, 2, N], F32R)
        lo = sb("lo", [C, 2, N], F32R)
        qk = sb("qk", [P, 2, NH, 2, N], F32R)
        vh = sb("vh", [P, 2, TPI, NH, 2 * HD])
        nmax = sb("nmax", [P, 2, 2, TPI])
        rsum = sb("rsum", [P, 2, 2, TPI])
        rrec = sb("rrec", [P, 2, 2, TPI])
        ee = sb("ee", [P, 3, 2, TPI, N])
        ots = sb("ots", [P, 2, N])
        junk = sb("junk", [P, N])
        sqa = sb("sqa", [P, TPI * N])
        sqj = sb("sqj", [P, 2, TPI * N])
        ssq = sb("ssq", [P, 2, NH])
        ssqa = sb("ssqa", [P, B, NH])

        ps = ctx.enter_context(nc.psum_tensor("ps", [P, 8, 512], F32))

        def wa(name, rows=P):
            a, b = C96[name]
            return w96[0:rows, a:b]

        def wb(name, rows=P):
            a, b = C128[name]
            return w128[0:rows, a:b]

        ident = wb("ident")

        def last_dim(ap, n):
            return ap.unsqueeze(ap.ndim).broadcast_to(list(ap.shape) + [n])

        def mid_dim(ap, at, n):
            shape = list(ap.shape)
            return ap.unsqueeze(at).broadcast_to(shape[:at] + [n] + shape[at:])

        bd_w = 2 * M * B + M
        l0_xt = big[:, 0:NT * C].rearrange("p (t c) -> p t c", c=C)
        l0_bd = big[:, NT * C:NT * C + B * bd_w]
        l0_at = big[0:B * M, NT * C + B * bd_w:NT * C + B * bd_w + B * N]
        qkv0 = sb("qkv0", [C, 3, B * M])
        rowsum = sb("rowsum", [C, B * N // SB])
        stf = sb("stf", [C, B * M])
        aff = sb("aff", [P, NT, M])
        a0 = sb("a0", [P, NT, M])
        pr = sb("pr", [C, B, M, M])
        pr2 = sb("pr2", [C, B, M, M])
        s64 = sb("s64", [C, 6, B * M])
        stft = sb("stft", [B * M, C])
        xsr = big[0:C, 2048:2048 + B * P].rearrange("p (i r) -> p i r", r=P)
        et = big[:, 4096:4096 + NH * 2 * N].rearrange("p (h x) -> p h x", h=NH)
        qh = big[:, 7168:7168 + 2 * NH * N].rearrange("p (a h t) -> p a h t", a=2, h=NH)
        y1 = big[:, :].rearrange("p (j t) -> p j t", j=NJ)
        y2 = on
        ysc = big[:, 2048:2048 + 4 * NE * C].rearrange("p (q e c) -> p q e c", q=4, e=NE)
        yred = big[:, 3584:3584 + 4 * C].rearrange("p (q c) -> p q c", q=4)
        h3 = big[:, 4096:4096 + 4 * 512].rearrange("p (s t) -> p s t", s=4)
        qk_f = qk[:, :, :, :, :].rearrange("p a h b x -> p (a h b x)")
        xhl = qk_f[:, 0:2048].rearrange("p (a b t) -> p a b t", a=2, b=2)
        w1hl = qk_f[:, 2048:2048 + 2 * NE * HID].rearrange("p (b x) -> p b x", b=2)
        amax = sb("amax", [P, 4, NG])
        gate = sb("gate", [P, 2, NT, NE])
        cmp = sb("cmp", [P, 6, NT])
        gsel = sb("gsel", [P, NE, NT])

        block = ctx.enter_context(nc.Block())

        def scores_cols(l, qc):
            return N if l == 1 else P * (qc + 1)

        def blocks(l):
            return [(q, t) for t in range(TPI) for q in range(TPI) if l == 1 or t <= q]

        @block.sync
        def _(sp):
            half = B * N // 4
            for i in range(4):
                sp.dma_start(xc[:, i * half:(i + 1) * half], x_d[:, i * half:(i + 1) * half]).then_inc(sg(f"x_loaded{i}"), 16)
            sp.dma_start(w128[:, :], w128_d).then_inc(sg("w128_loaded"), 16)
            sp.dma_start(w96[:, :], w96_d).then_inc(sg("w96_loaded"), 16)
            on_v = on[:, :, :].rearrange("p (i q) (g d) -> p i q g d", q=TPI, d=HD)
            for i in range(B):
                sp.wait_ge(sg("l1_out"), i // 4 + 1)
                for q in range(TPI):
                    sp.dma_start(mix_d[i, :, q * P:(q + 1) * P, :].rearrange("g q d -> q g d"),
                                 on_v[:, i, q]).then_inc(sg(f"l1_stored{i // 4}"), 16)
            flat = mix_d.rearrange("i g q d -> (i g q d)").rearrange("(t p c) -> p t c", p=P, c=C)
            for r in range(4):
                sp.wait_ge(sg(f"l1_stored{r}"), 16 * TPI * 4)
                sp.dma_start(tok[:, r * 8:(r + 1) * 8, :], flat[:, r * 8:(r + 1) * 8, :]).then_inc(sg(f"l1_mixed{r}"), 16)
            for l in (2, 3):

                def stack(n, par):
                    for part, moves in ((hi, ((0, 0, 2), (1, 0, 1), (2, 1, 2))), (lo, ((3, 0, 2), (2, 0, 1), (1, 1, 2)))):
                        sp.wait_ge(*upto(l, "hi" if part is hi else "lo", n + 1))
                        for t, a0, a1 in moves:
                            sp.dma_start(qk[t * HD:(t + 1) * HD, par, :, a0:a1, :].bitcast(F32),
                                         part[:, a0:a1, :].bitcast(F32)).then_inc(own(l, "stacked"), 16)

                stack(0, 0)
                stack(1, 1)
                with sp.Fori(0, B // 2) as it:
                    for par in range(2):
                        stack(it * 2 + (par + 2), par)
                sp.wait_ge(*upto(l, "stacked", STK * (B + 2)))
            with sp.Fori(0, NT // 4) as t:
                sp.wait_ge(sg("moe_block"), t + 1)
                sp.dma_start(out_d[:, bass.ds(t * 4, 4), :], tok[:, bass.ds(t * 4, 4), :]).then_inc(sg("stored"), 16)
            sp.wait_ge(sg("stored"), 16 * (NT // 4))


        @block.gpsimd
        def _(pool):
            nc.gpsimd.memset(ones[:, :], 1.0).then_inc(sg("ones_set"), 1)
            nc.gpsimd.memset(l0_bd, 0.0).then_inc(sg("bd_zeroed"), 1)
            nc.gpsimd.memset(xn[:, B * N:], 0.0).then_inc(sg("pad_zeroed"), 1)
            pool.wait_ge(sg("pad_zeroed"), 1)
            pool.sem_inc(sg("zeroed"), START)
            for n, t in enumerate((qh[C:P], xn[C:P, 0:B * N], xb[C:P], kh[C:P], ots[:, :, :], vh[:, :, :, :, :], qk[:, :, :, :, :].bitcast(F32),
                      tok_all[:, 0:TPI, :], on_all[:, 0:TPI, :])):
                pool.wait_ge(sg("zeroed"), START + n)
                nc.gpsimd.memset(t, 0.0).then_inc(sg("zeroed"), 1)
            pool.wait_ge(sg("zeroed"), START + 9)
            for n, t in enumerate((xn[ONE:ONE + 1, :], xb[ONE:ONE + 1, :, :], ots[ONE:ONE + 1, :, :])):
                nc.gpsimd.memset(t, 1.0).then_inc(sg("ones_rows"), 1)
                pool.wait_ge(sg("ones_rows"), n + 1)
            pool.wait_ge(sg("w128_loaded"), 16)
            nc.gpsimd.tensor_copy(identb[:, :], ident).then_inc(sg("bf_consts"), 1)
            nc.gpsimd.tensor_copy(maskb[:, :], wb("mask")).then_inc(sg("bf_consts"), 1)
            pool.wait_ge(sg("pad_zeroed"), 1)

            def stage(l, n, par):
                pool.wait_ge(sg("pad_zeroed"), 1)
                nc.gpsimd.tensor_copy(xb[0:C, par, :], xn[0:C, bass.ds(n * N, N)]).then_inc(own(l, "xb"), 1)

            def mix(l, n, par):
                pool.wait_ge(sg("l1_q_sb"), n + 1)
                for g in range(NH):
                    last = nc.gpsimd.tensor_tensor(qh[0:C, par, g, :], qs[:, :], wa("l1_hw", C)[:, g:g + 1].broadcast_to([C, N]), ALU.mult)
                last.then_inc(sg("l1_qmix"), 1)

            for l in (1, 2, 3):
                pool.wait_ge(sg(f"l{l}_xn"), 1)
                pool.wait_ge(sg("w96_loaded"), 16)
                for n in range(2):
                    stage(l, n, n)
                if l == 1:
                    for n in range(2):
                        mix(l, n, n)
                with pool.Fori(0, B // 2) as it:
                    for par in range(2):
                        i = it * 2 + par
                        pool.wait_ge(*upto(l, "v_ps", i + 1))
                        stage(l, i + 2, par)
                        if l == 1:
                            pool.wait_ge(sg("l1_s_ps"), i * 3 + 3)
                            mix(l, i + 2, par)
                if l == 3:
                    pool.wait_ge(*upto(l, "max", 3 * B + 2))
                    pool.wait_ge(*upto(l, "stacked", STK * (B + 2)))
                    nc.gpsimd.tensor_copy(w1hl[:, 0, :], wa("f3_w1")).then_inc(sg("f3_whi"), 1)
                    pool.wait_ge(sg("f3_whi"), 1)
                    nc.gpsimd.tensor_tensor(w1hl[:, 1, :], wa("f3_w1"), w1hl[:, 0, :].bitcast(F32), ALU.subtract).then_inc(sg("f3_wlo"), 1)
                if l == 2:
                    for k in range(2):
                        pool.wait_ge(sg(f"f2_amax{k}"), 1)
                        nc.gpsimd.partition_all_reduce(amax[:, 2 * k + 1, :], amax[:, 2 * k, :], P,
                                                       bass.bass_isa.ReduceOp.max).then_inc(sg(f"f2_gmax{k}"), 1)

        @block.scalar
        def _(act):
            for name in ["l1_et0", "l1_et1", "causal_et1", "moe_h"]:
                act.sem_inc(sg(name), START)
            def norm_sqrt(name, rows, cols):
                act.wait_ge(sg("norm_ve"), NORM[name])
                nc.scalar.activation(st[0:rows, 3, 0:cols], st[0:rows, 2, 0:cols], ACT.Sqrt).then_inc(sg("norm_sd"), 1)

            norm_sqrt("gn0", C, B)
            for g in range(8):
                act.wait_ge(sg("l0_xt_ps"), g + 1)
                nc.scalar.activation(l0_xt[:, g * 4:(g + 1) * 4, :], ps[:, 4 + g % 2, 0:4 * C].rearrange("p (t c) -> p t c", c=C),
                                     ACT.Copy).then_inc(sg("l0_xt"), 1)
            act.wait_ge(sg("l0_logit"), 1)
            nc.scalar.activation(aff[:, :, :], a0[:, :, :], ACT.Exp, scale=C ** -0.5).then_inc(sg("l0_exp"), 1)
            nc.scalar.activation(st[:, 5, :], st[:, 4, :], ACT.Exp, scale=-C ** -0.5).then_inc(sg("l0_exp"), 1)
            act.wait_ge(sg("l0_qkv_ps"), 1)
            nc.scalar.activation(qkv0[:, :, :], ps[0:C, 2, 0:3 * B * M].rearrange("p (a b) -> p a b", a=3), ACT.Copy).then_inc(sg("l0_qkv"), 1)
            act.wait_ge(sg("l0_sc"), 1)
            nc.scalar.activation(pr2[:, :, :, :], pr[:, :, :, :], ACT.Exp, scale=(C // H0) ** -0.5).then_inc(sg("l0_sexp"), 1)
            act.wait_ge(sg("l0_proj_ps"), 1)
            nc.scalar.activation(s64[:, 5, :], ps[0:C, 0, 0:B * M], ACT.Identity, bias=wa("l0_pb", C)).then_inc(sg("l0_stf2"), 1)
            act.wait_ge(sg("l0_stft_ps"), 1)
            nc.scalar.activation(stft[:, :], ps[0:B * M, 1, 0:C], ACT.Copy).then_inc(sg("l0_stft"), 1)
            for g in range(8):
                act.wait_ge(sg("l0_at_ps"), g + 1)
                nc.scalar.activation(l0_at[:, g * 512:(g + 1) * 512], ps[0:B * M, 4 + g % 2, :], ACT.Copy).then_inc(sg("l0_at"), 1)

            def copy_probs(l, k, h, hh):
                w = len(blocks(l)) * P
                act.wait_ge(*upto(l, "tr", TR0 + 2 * k + hh + 1))
                nc.scalar.activation(et[:, h, 0:w], ps[:, 4 + hh, 0:w], ACT.Copy).then_inc(own(l, f"et{hh}"), 1)

            def exps(l, k, kp, ke):
                act.wait_ge(*upto(l, "max", k + 1))
                if not isinstance(k, int):
                    act.wait_ge(*upto(l, "tr", TR0 + 2 * k - 4))
                    if l == 1:
                        act.wait_ge(sg("l1_ssq"), TR0 + k - 2)
                for hh in range(2):
                    for qc in range(TPI):
                        w = scores_cols(l, qc)
                        src = ps[:, 2 * kp + hh, qc * N:qc * N + w]
                        last = nc.scalar.activation(ee[:, ke, hh, qc, 0:w], src, ACT.Exp, bias=nmax[:, kp, hh, qc:qc + 1],
                                                    accum_out=rsum[:, kp, hh, qc:qc + 1])
                    last.then_inc(own(l, "exp"), 1)

            def queries(l, n, par):
                act.wait_ge(*upto(l, "q_ps", n + 1))
                if l == 1:
                    if not isinstance(n, int) or n > 0:
                        act.wait_ge(sg("l1_qmix"), n)
                    nc.scalar.activation(qs[:, :], ps[0:C, 7, 0:N], ACT.Copy, scale=QS).then_inc(sg("l1_q_sb"), 1)
                    nc.scalar.activation(kh[0:C, par, :], ps[0:C, 7, N:2 * N], ACT.Copy).then_inc(sg("l1_k_sb"), 1)
                else:
                    if not isinstance(n, int) or n > 0 or l == 3:
                        act.wait_ge(*upto(l, "stacked", n * STK))
                    nc.scalar.activation(hi[:, :, :], ps[0:C, 7, :].rearrange("p (a t) -> p a t", a=2), ACT.Copy).then_inc(own(l, "hi"), 1)

            def outputs_to_sbuf(l, i):
                act.wait_ge(*upto(l, "av", i + 2))
                nc.scalar.activation(ots[0:C, :, :], ps[0:C, 6, :].rearrange("p (a t) -> p a t", a=2), ACT.Copy).then_inc(own(l, "ot"), 1)

            for l in (1, 2, 3):
                if l == 1:
                    norm_sqrt("gn1", C, B)
                else:
                    norm_sqrt(f"ln{l}", P, NT)
                    for g in range(8):
                        act.wait_ge(sg("ln_t_ps"), TURN[f"ln{l}"] + g + 1)
                        nc.scalar.activation(xn[0:C, g * 512:(g + 1) * 512], ps[0:C, 4 + g % 4, :], ACT.Copy).then_inc(sg("xn_copied"), 1)
                    act.wait_ge(sg("xn_copied"), TURN[f"ln{l}"] + 8)
                    act.sem_inc(sg(f"l{l}_xn"), 1)
                queries(l, 0, 0)
                queries(l, 1, 1)
                exps(l, 0, 0, 0)
                with act.Fori(0, B // 2) as it:
                    for j in range(6):
                        k, u, i, par = it * 6 + j, j % 3, it * 2 + j // 3, j // 3
                        exps(l, k + 1, (j + 1) % 2, (u + 1) % 3)
                        if u == 0:
                            outputs_to_sbuf(l, i - 1)
                        if l == 1:
                            copy_probs(l, k, 2 * u, 0)
                        copy_probs(l, k, 2 * u + 1, 1)
                        if l == 1 and u == 2:
                            act.wait_ge(sg("l1_norm"), 2 * k + 2)
                            nc.scalar.activation(sqa[:, :], ee[:, u, 1, :, :].rearrange("p q t -> p (q t)"), ACT.Square,
                                                 accum_out=ssq[:, par, NH - 1:NH]).then_inc(sg("l1_ssq_act"), 1)
                        if u == 1:
                            queries(l, i + 2, par)
                outputs_to_sbuf(l, B - 1)
                if l == 1:
                    act.wait_ge(sg("l1_var"), 1)
                    nc.scalar.activation(st[:, 0:3, :], st[:, 3:6, :], ACT.Sqrt).then_inc(sg("l1_sd"), 1)
                    for g in range(8):
                        act.wait_ge(sg("l1_mt_ps"), g + 1)
                        nc.scalar.activation(xn[0:C, g * 512:(g + 1) * 512], ps[0:C, 4 + g % 2, :], ACT.Copy).then_inc(sg("l1_mt"), 1)
                if l == 2:
                    act.wait_ge(sg("f2_z"), 1)
                    for g in range(NG):
                        n = HID // NG
                        nc.scalar.activation(wa("f2_w1", C)[:, g * n:(g + 1) * n], wa("f2_w1", C)[:, g * n:(g + 1) * n], ACT.Sign,
                                             bias=s64[:, 1, g:g + 1]).then_inc(sg("f2_w1s"), 1)
                    for g in range(NG):
                        n = C // NG
                        v = wb("f2_w2").rearrange("p (j o) -> p j o", j=NJ)[:, :, g * n:(g + 1) * n]
                        nc.scalar.activation(v, v, ACT.Sign, bias=amax[:, 3, g:g + 1]).then_inc(sg("f2_w2s"), 1)
                    norm_sqrt("lnf2", P, NT)
                    for g in range(8):
                        act.wait_ge(sg("ln_t_ps"), TURN["lnf2"] + g + 1)
                        nc.scalar.activation(xn[0:C, g * 512:(g + 1) * 512], ps[0:C, 4 + g % 4, :], ACT.Copy).then_inc(sg("xn_copied"), 1)
                    act.sem_inc(sg("f2_y1"), 6)
                    with act.Fori(0, NG) as g:
                        for b in range(2):
                            for j in range(NJ):
                                act.wait_ge(sg("f2_y1_ps"), g * 6 + (b * NJ + j + 1))
                                nc.scalar.activation(y1[:, j, bass.ds(g * GT + b * (GT // 2), GT // 2)], ps[:, b * NJ + j, 0:GT // 2],
                                                     ACT.Copy).then_inc(sg("f2_y1"), 1)
                    for g in range(NG):
                        act.wait_ge(sg("f2_quant"), g + 1)
                        nc.scalar.activation(y1[:, :, g * GT:(g + 1) * GT], y1[:, :, g * GT:(g + 1) * GT], ACT.Gelu).then_inc(sg("f2_gelu"), 1)
            norm_sqrt("lnf3", P, NT)
            for g in range(8):
                act.wait_ge(sg("ln_t_ps"), TURN["lnf3"] + g + 1)
                nc.scalar.activation(xn[0:C, g * 512:(g + 1) * 512], ps[0:C, 4 + g % 4, :], ACT.Copy).then_inc(sg("xn_copied"), 1)
            act.wait_ge(sg("f3_gl"), 1)
            nc.scalar.activation(gate[:, 1, :, :], gate[:, 0, :, :], ACT.Exp).then_inc(sg("f3_gexp"), 1)
            with act.Fori(0, NT // 4) as t:
                for s in range(NE * NJ):
                    act.wait_ge(sg("moe_h_ps"), t * (NE * NJ) + (s + 1))
                    nc.scalar.activation(h3[:, s % 4, :], ps[:, 4 + s % 4, :], ACT.Gelu).then_inc(sg("moe_h"), 1)

        @block.tensor
        def _(pe):
            for name in ["l1_tr", "causal_tr"]:
                pe.sem_inc(sg(name), TR0)
            mm = nc.tensor.matmul

            def group_sums(name):
                pe.wait_ge(sg("gn_mv"), NORM[name])
                mm(ps[0:C, 0, 0:B], wb("avg3", C), chmv[0:C, 0:B, 0], start=True, stop=True).then_inc(sg("gn_mg"), 1)
                pe.wait_ge(sg("gn_e"), NORM[name])
                mm(ps[0:C, 0, B:2 * B], wb("avg3", C), st[0:C, 1, 0:B], start=True, stop=True).then_inc(sg("gn_vg"), 1)

            def normed_to_channels(name):
                for g in range(8):
                    pe.wait_ge(sg("ln_tn"), TURN[name] + g + 1)
                    if g >= 4:
                        pe.wait_ge(sg("xn_copied"), TURN[name] + g - 3)
                    for t in range(4):
                        last = nc.tensor.transpose(ps[0:C, 4 + g % 4, t * P:(t + 1) * P], on[:, g * 4 + t, :], ident)
                    last.then_inc(sg("ln_t_ps"), 1)

            def tiles_to_channels(src, ready, done, freed, nbank):
                for g in range(8):
                    if ready is not None:
                        ready(g)
                    if g >= nbank:
                        pe.wait_ge(freed, g - nbank + 1)
                    for t in range(4):
                        last = nc.tensor.transpose(ps[0:C, 4 + g % nbank, t * P:(t + 1) * P], src[:, g * 4 + t, :], ident)
                    last.then_inc(done, 1)

            pe.wait_ge(sg("w128_loaded"), 16)
            group_sums("gn0")
            pe.wait_ge(sg("gn0_xn"), 1)
            for g in range(8):
                if g >= 2:
                    pe.wait_ge(sg("l0_xt"), g - 1)
                for t in range(4):
                    a = (g * 4 + t) * P
                    last = nc.tensor.transpose(ps[:, 4 + g % 2, t * C:(t + 1) * C], xn[0:C, a:a + P], wb("ident", C)[:, 0:C])
                last.then_inc(sg("l0_xt_ps"), 1)
            pe.wait_ge(sg("l0_stf"), 1)
            for t in range(NT):
                i = t // TPI
                last = mm(ps[:, 1, t * M:(t + 1) * M], xn[0:C, t * P:(t + 1) * P], stf[:, i * M:(i + 1) * M], start=True, stop=True)
            last.then_inc(sg("l0_logit_ps"), 1)
            pe.wait_ge(sg("l0_aff"), 1)
            pe.wait_ge(sg("ones_set"), 1)
            mm(ps[0:C, 0, 0:NT * M], ones[:, 0:C], aff[:, :, :], start=True, stop=True)
            pe.wait_ge(sg("l0_xt"), 8)
            for i in range(B):
                for t in range(TPI):
                    last = mm(ps[0:C, 3, i * M:(i + 1) * M], l0_xt[:, i * TPI + t, :], aff[:, i * TPI + t, :], start=(t == 0), stop=(t == TPI - 1))
            last.then_inc(sg("l0_sums_ps"), 1)
            pe.wait_ge(sg("l0_bd"), 1)
            pe.wait_ge(sg("w96_loaded"), 16)
            pe.wait_ge(sg("l0_stf1"), 1)
            for a, name in enumerate(("l0_q", "l0_k", "l0_v")):
                last = mm(ps[0:C, 2, a * B * M:(a + 1) * B * M], wa(name, C), s64[:, 2, :], start=True, stop=True)
            last.then_inc(sg("l0_qkv_ps"), 1)
            pe.wait_ge(sg("l0_prod"), 1)
            mm(ps[0:C, 1, 0:B * M * M], wb("sum12", C), pr[:, :, :, :], start=True, stop=True).then_inc(sg("l0_sc_ps"), 1)
            pe.wait_ge(sg("l0_o"), 1)
            mm(ps[0:C, 0, 0:B * M], wa("l0_p", C), s64[:, 4, :], start=True, stop=True).then_inc(sg("l0_proj_ps"), 1)
            pe.wait_ge(sg("l0_stf2"), 1)
            nc.tensor.transpose(ps[0:B * M, 1, 0:C], s64[:, 5, :], wb("ident", C)[:, 0:C]).then_inc(sg("l0_stft_ps"), 1)
            for g in range(8):
                if g >= 2:
                    pe.wait_ge(sg("l0_at"), g - 1)
                for t in range(4):
                    a = (g * 4 + t) * B * M
                    last = nc.tensor.transpose(ps[0:B * M, 4 + g % 2, t * P:(t + 1) * P], l0_bd[:, a:a + B * M], ident)
                last.then_inc(sg("l0_at_ps"), 1)
            pe.wait_ge(sg("l0_stft"), 1)
            for g in range(8):
                pe.wait_ge(sg("l0_at"), g + 1)
                if g >= 2:
                    pe.wait_ge(sg("l0_res"), g - 1)
                mm(ps[0:C, 2 + g % 2, :], stft[:, :], l0_at[:, g * 512:(g + 1) * 512], start=True, stop=True).then_inc(sg("l0_out_ps"), 1)

            def score_unit(l, par, u, kp, k):
                if not isinstance(k, int):
                    pe.wait_ge(*upto(l, "exp", 2 * k - 2))
                if l == 1:
                    for hh in range(2):
                        for qc in range(TPI):
                            last = mm(ps[:, 2 * kp + hh, qc * N:(qc + 1) * N], qh[:, par, 2 * u + hh, qc * P:(qc + 1) * P],
                                      kh[:, par, :], start=True, stop=True)
                else:
                    for qc in range(TPI):
                        w = scores_cols(l, qc)
                        for hh in range(2):
                            h = 2 * u + hh
                            mm(ps[:, 2 * kp + hh, qc * N:qc * N + w], qk[:, par, h, 0, qc * P:(qc + 1) * P], qk[:, par, h, 1, 0:w],
                               start=True, stop=False)
                            last = mm(ps[:, 2 * kp + hh, qc * N + qc * P:qc * N + (qc + 1) * P], identb[:, :], maskb[:, :], start=False, stop=True)
                last.then_inc(own(l, "s_ps"), 1)

            def project_qk(l, n, par):
                pe.wait_ge(*upto(l, "xb", n + 1))
                if not isinstance(n, int) or n > 0:
                    pe.wait_ge(*upto(l, "v_sb", n))
                mm(ps[0:C, 7, 0:N], wa(f"l{l}_q"), xb[:, par, :], start=True, stop=True)
                mm(ps[0:C, 7, N:2 * N], wa(f"l{l}_k"), xb[:, par, :], start=True, stop=True).then_inc(own(l, "q_ps"), 1)

            def parts_ready(l, n):
                for what in ("q_sb", "k_sb") if l == 1 else ("hi", "lo"):
                    if l == 1:
                        pe.wait_ge(sg(f"l1_{what}"), n + 1)
                    else:
                        pe.wait_ge(*upto(l, what, n + 1))

            def project_v(l, n, par):
                for t in range(TPI):
                    last = mm(ps[:, 7, t * C:(t + 1) * C], xb[:, par, t * P:(t + 1) * P], wa(f"l{l}_v"), start=True, stop=True)
                last.then_inc(own(l, "v_ps"), 1)

            def outputs(l, i):
                pe.wait_ge(*upto(l, "ot", i + 2))
                if l == 1:
                    for g in range(2):
                        for q in range(TPI):
                            a = (q * 2 + g) * C
                            last = nc.tensor.transpose(ps[:, 6, a:a + C], ots[0:C, g, q * P:(q + 1) * P], wb("ident", C)[:, 0:C])
                else:
                    for t in range(TPI):
                        for g in range(2):
                            last = mm(ps[:, 6, t * C:(t + 1) * C], ots[:, g, t * P:(t + 1) * P], wa(f"l{l}_p")[:, g * C:(g + 1) * C],
                                      start=(g == 0), stop=(g == 1))
                last.then_inc(own(l, "out_ps"), 1)

            def keys_ready(l, n):
                if l == 1:
                    pe.wait_ge(sg("l1_qmix"), n + 1)
                    pe.wait_ge(sg("l1_k_sb"), n + 1)
                else:
                    pe.wait_ge(*upto(l, "stacked", (n + 1) * STK))

            for l in (1, 2, 3):
                if l == 1:
                    group_sums("gn1")
                    pe.wait_ge(sg("l0_res"), 8)
                else:
                    normed_to_channels(f"ln{l}")
                pe.wait_ge(sg("bf_consts"), 2)
                pe.wait_ge(sg("ones_rows"), 3)
                if l > 1:
                    pe.wait_ge(sg(f"l{l}_xn"), 1)
                    pe.wait_ge(sg(f"l{l}_wq"), 1)
                mm(ps[0:C, 6, :], ident[:, 0:C], xn[:, B * N:(B + 2) * N], start=True, stop=True).then_inc(own(l, "av"), 1)
                project_qk(l, 0, 0)
                parts_ready(l, 0)
                project_v(l, 0, 0)
                project_qk(l, 1, 1)
                keys_ready(l, 0)
                score_unit(l, 0, 0, 0, 0)
                score_unit(l, 0, 1, 1, 1)
                with pe.Fori(0, B // 2) as it:
                    for j in range(6):
                        k, u, par = it * 6 + j, j % 3, j // 3
                        i, npar = it * 2 + par, 1 - par
                        if u == 1:
                            keys_ready(l, i + 1)
                        score_unit(l, par if u == 0 else npar, (u + 2) % 3, j % 2, k + 2)
                        for hh in range(2):
                            pe.wait_ge(*upto(l, "norm", 2 * k + (hh + 1)))
                            pe.wait_ge(*upto(l, f"et{hh}", START + k))
                            for b, (qc, tc) in enumerate(blocks(l)):
                                last = nc.tensor.transpose(ps[:, 4 + hh, b * P:(b + 1) * P], ee[:, u, hh, qc, tc * P:(tc + 1) * P], ident)
                            last.then_inc(own(l, "tr"), 1)
                        if u == 0:
                            parts_ready(l, i + 1)
                            project_v(l, i + 1, npar)
                            outputs(l, i - 1)
                        if u == 1:
                            project_qk(l, i + 2, par)
                        if u == 2:
                            pe.wait_ge(*upto(l, "added", i + 1))
                            pe.wait_ge(*upto(l, "v_sb", i + 1))
                            for hh in range(2):
                                pe.wait_ge(*upto(l, f"et{hh}", START + k + 1))
                            for g in range(2):
                                for tc in range(TPI):
                                    q0 = 0 if l == 1 or tc == 0 else P
                                    for r in range(3):
                                        last = mm(ps[32 * r:32 * (r + 1), 6, g * N + q0:(g + 1) * N], vh[:, par, tc, 3 * g + r, :],
                                                  et[:, 3 * g + r, tc * N:tc * N + N - q0], start=(tc == 0), stop=(tc == TPI - 1))
                            last.then_inc(own(l, "av"), 1)
                outputs(l, B - 1)
                pe.wait_ge(*upto(l, "max", 3 * B + 2))
                pe.wait_ge(*upto(l, "exp", 6 * B + 2))
                pe.wait_ge(*upto(l, "v_sb", B + 1))
                parts_ready(l, B + 1)
                pe.wait_ge(*upto(l, "added", B + 1))
                for hh in range(2):
                    pe.wait_ge(*upto(l, f"et{hh}", START + 3 * B))
                if l == 1:
                    pe.wait_ge(sg("l1_ssqa"), B)
                    mm(ps[:, 0, 0:B * NH], ones[:, :], ssqa[:, :, :], start=True, stop=True).then_inc(sg("l1_ssq_ps"), 1)
                    pe.wait_ge(sg("l1_xsum"), 1)
                    for i in range(B):
                        last = mm(ps[:, 1 + i // 5, (i % 5) * C:(i % 5 + 1) * C], xsr[:, i, :], wa("l1_v", C), start=True, stop=True)
                        if i % 5 == 4 or i == B - 1:
                            last.then_inc(sg("l1_vs_ps"), 1)
                    pe.wait_ge(sg("l1_sd"), 1)
                    tiles_to_channels(tok, lambda g: pe.wait_ge(sg(f"l1_mixed{g // 2}"), 16), sg("l1_mt_ps"), sg("l1_mt"), 2)
                    for g in range(8):
                        pe.wait_ge(sg("l1_mt"), g + 1)
                        if g >= 2:
                            pe.wait_ge(sg("l1_tok"), g - 1)
                        for t in range(4):
                            a = (g * 4 + t) * P
                            mm(ps[:, 6 + g % 2, t * C:(t + 1) * C], xc[:, a:a + P], wb("ident", C)[:, 0:C], start=True, stop=False)
                            last = mm(ps[:, 6 + g % 2, t * C:(t + 1) * C], xn[:, a:a + P], wa("l1_p"), start=False, stop=True)
                        last.then_inc(sg("l1_y_ps"), 1)
                if l == 2:
                    pe.wait_ge(sg("f2_wsum"), 2)
                    mm(ps[0:C, 0, 0:NG], ones[0:C, 0:C], s64[:, 0, 0:NG], start=True, stop=True)
                    mm(ps[:, 1, 0:NG], ones[:, :], amax[:, 2, :], start=True, stop=True).then_inc(sg("f2_wtot"), 1)
                    normed_to_channels("lnf2")
                    pe.wait_ge(sg("xn_copied"), TURN["lnf2"] + 8)
                    pe.wait_ge(sg("f2_w1z"), 1)
                    pe.wait_ge(sg("f2_w1s"), NG)
                    with pe.Fori(0, NG) as g:
                        for b in range(2):
                            for j in range(NJ):
                                pe.wait_ge(sg("f2_y1"), g * 6 + (b * NJ + j + 1))
                                mm(ps[:, b * NJ + j, 0:GT // 2], wa("f2_w1")[:, j * P:(j + 1) * P],
                                   xn[:, bass.ds(g * GT + b * (GT // 2), GT // 2)], start=True, stop=True).then_inc(sg("f2_y1_ps"), 1)
                    pe.wait_ge(sg("f2_w2s"), NG)
                    pe.wait_ge(sg("f2_w2z"), 1)
                    for g in range(NG):
                        pe.wait_ge(sg("f2_gelu"), g + 1)
                        for b in range(2):
                            if g >= 2:
                                pe.wait_ge(sg("f2_y2"), 2 * (g - 2) + b + 1)
                            for t in range(3):
                                for j in range(NJ):
                                    a = g * GT + (b * 3 + t) * P
                                    last = mm(ps[:, 4 + (g % 2) * 2 + b, t * C:(t + 1) * C], y1[:, j, a:a + P],
                                              wb("f2_w2")[:, j * C:(j + 1) * C], start=(j == 0), stop=(j == NJ - 1))
                            last.then_inc(sg("f2_y2_ps"), 1)
            normed_to_channels("lnf3")
            pe.wait_ge(sg("xn_copied"), TURN["lnf3"] + 8)
            for t in range(NT):
                last = mm(ps[:, 0, t * NE:(t + 1) * NE], xn[:, t * P:(t + 1) * P], wa("f3_gate"), start=True, stop=True)
            last.then_inc(sg("f3_gl_ps"), 1)
            pe.wait_ge(sg("f3_gl"), 1)
            NS = NE * NJ

            def hidden(t, par, s):
                if s >= 4:
                    pe.wait_ge(sg("moe_h"), START + t * NS + (s - 3))
                for n, (w, x) in enumerate(((0, 0), (0, 1), (1, 0))):
                    last = mm(ps[:, 4 + s % 4, :], w1hl[:, w, s * P:(s + 1) * P], xhl[:, par, x, :],
                              start=(n == 0), stop=(n == 2))
                last.then_inc(sg("moe_h_ps"), 1)

            pe.wait_ge(sg("f3_wlo"), 1)
            with pe.Fori(0, NT // 8) as it:
                for par in range(2):
                    t = it * 2 + par
                    pe.wait_ge(sg("moe_x"), 2 * t + 2)
                    for s in range(NS + 2):
                        if s < NS:
                            if s < 4:
                                pe.wait_ge(sg("moe_h"), START + t * NS)
                            hidden(t, par, s)
                        if s >= 2:
                            r = s - 2
                            e, j = r // NJ, r % NJ
                            pe.wait_ge(sg("moe_h"), START + t * NS + (r + 1))
                            for q in range(4):
                                if r == 0:
                                    pe.wait_ge(sg("moe_y"), t * 4 + (q + 1))
                                last = mm(ps[:, q, e * C:(e + 1) * C], h3[:, r % 4, q * P:(q + 1) * P],
                                          wb("f3_w2")[:, r * C:(r + 1) * C], start=(j == 0), stop=(j == NJ - 1))
                    last.then_inc(sg("moe_y_ps"), 1)

        @block.vector
        def _(dve):
            dve.sem_inc(sg("causal_et0"), START)
            dve.sem_inc(sg("l1_ssq"), TR0)
            dve.sem_inc(sg("moe_y"), 4)
            V = nc.vector
            chain = [0]

            def link(ins):
                chain[0] += 1
                ins.then_inc(sg("dve_chain"), 1)
                dve.wait_ge(sg("dve_chain"), chain[0])

            def group_norm(name):
                for i in range(B):
                    if name == "gn0" and i % 4 == 0:
                        dve.wait_ge(sg(f"x_loaded{i // 4}"), 16)
                    last = V.bn_stats(chst[0:C, i, :], xc[:, i * N:(i + 1) * N])
                link(last)
                for i in range(B):
                    last = V.bn_aggr(chmv[0:C, i, :], chst[0:C, i, :])
                last.then_inc(sg("gn_mv"), 1)
                dve.wait_ge(sg("gn_mv"), NORM[name])
                dve.wait_ge(sg("gn_mg"), NORM[name])
                link(V.tensor_copy(st[0:C, 4, 0:B], ps[0:C, 0, 0:B]))
                link(V.tensor_tensor(st[0:C, 0, 0:B], chmv[0:C, 0:B, 0], st[0:C, 4, 0:B], ALU.subtract))
                link(V.tensor_tensor(st[0:C, 1, 0:B], st[0:C, 0, 0:B], st[0:C, 0, 0:B], ALU.mult))
                V.tensor_tensor(st[0:C, 1, 0:B], st[0:C, 1, 0:B], chmv[0:C, 0:B, 1], ALU.add).then_inc(sg("gn_e"), 1)
                dve.wait_ge(sg("gn_vg"), NORM[name])
                V.tensor_scalar(st[0:C, 2, 0:B], ps[0:C, 0, B:2 * B], 1e-5, None, ALU.add).then_inc(sg("norm_ve"), 1)
                dve.wait_ge(sg("norm_sd"), NORM[name])
                link(V.reciprocal(st[0:C, 5, 0:B], st[0:C, 3, 0:B]))
                link(V.scalar_tensor_tensor(out=st[0:C, 6, 0:B], in0=st[0:C, 4, 0:B], scalar=-1.0, in1=st[0:C, 5, 0:B], op0=ALU.mult, op1=ALU.mult))
                for i in range(B):
                    last = V.tensor_scalar(xn[0:C, i * N:(i + 1) * N], xc[:, i * N:(i + 1) * N], st[0:C, 5, i:i + 1], st[0:C, 6, i:i + 1], ALU.mult, ALU.add)
                return last

            def layer_norm(name):
                for t in range(NT):
                    last = V.bn_stats(chst[:, t, :], tok[:, t, :])
                link(last)
                for t in range(NT):
                    last = V.bn_aggr(chmv[:, t, :], chst[:, t, :])
                link(last)
                V.tensor_scalar(st[:, 2, :], chmv[:, :, 1], 1e-5, None, ALU.add).then_inc(sg("norm_ve"), 1)
                dve.wait_ge(sg("norm_sd"), NORM[name])
                link(V.reciprocal(st[:, 5, :], st[:, 3, :]))
                link(V.scalar_tensor_tensor(out=st[:, 6, :], in0=chmv[:, :, 0], scalar=-1.0, in1=st[:, 5, :], op0=ALU.mult, op1=ALU.mult))
                for t in range(NT):
                    last = V.tensor_scalar(on[:, t, :], tok[:, t, :], st[:, 5, t:t + 1], st[:, 6, t:t + 1], ALU.mult, ALU.add)
                    if t % 4 == 3:
                        last.then_inc(sg("ln_tn"), 1)

            group_norm("gn0").then_inc(sg("gn0_xn"), 1)
            dve.wait_ge(sg("gn0_xn"), 1)
            link(V.tensor_reduce(out=rowsum[:, :], in_=xn[0:C, 0:B * N].rearrange("p (a w) -> p a w", w=SB), axis=AX.X, op=ALU.add))
            link(V.tensor_reduce(out=stf[:, :].rearrange("p (g w) -> p g w", w=WW // SB),
                                 in_=rowsum[:, :].rearrange("p (g h w) -> p g w h", h=SB, w=WW // SB), axis=AX.X, op=ALU.add))
            V.tensor_scalar(stf[:, :], stf[:, :], 1.0 / (SB * SB), None, ALU.mult).then_inc(sg("l0_stf"), 1)
            dve.wait_ge(sg("l0_logit_ps"), 1)
            lg = ps[:, 1, 0:NT * M].rearrange("p (t m) -> p t m", m=M)
            link(V.tensor_reduce(out=st[:, 4, :], in_=lg, axis=AX.X, op=ALU.max))
            link(V.tensor_scalar(st[:, 4, :], st[:, 4, :], 0.0, None, ALU.max))
            V.tensor_tensor(a0[:, :, :], lg, last_dim(st[:, 4, :], M), ALU.subtract).then_inc(sg("l0_logit"), 1)
            dve.wait_ge(sg("l0_exp"), 2)
            link(V.tensor_reduce(out=st[:, 6, :], in_=aff[:, :, :], axis=AX.X, op=ALU.add))
            link(V.scalar_tensor_tensor(out=st[:, 6, :], in0=st[:, 5, :], scalar=float(9 - M), in1=st[:, 6, :], op0=ALU.mult, op1=ALU.add))
            link(V.reciprocal(st[:, 7, :], st[:, 6, :]))
            V.tensor_tensor(aff[:, :, :], aff[:, :, :], last_dim(st[:, 7, :], M), ALU.mult).then_inc(sg("l0_aff"), 1)
            dve.wait_ge(sg("bd_zeroed"), 1)
            dve.wait_ge(sg("l0_aff"), 1)
            bd = l0_bd.rearrange("p (i x) -> p i x", x=bd_w)[:, :, 0:2 * B * M].rearrange("p i (t x) -> p i t x", t=TPI)[:, :, :, 0:M]
            V.tensor_copy(bd, aff[:, :, :].rearrange("p (i t) m -> p i t m", t=TPI)).then_inc(sg("l0_bd"), 1)
            dve.wait_ge(sg("l0_sums_ps"), 1)
            link(V.tensor_reduce(out=s64[:, 0, :].rearrange("p (i m) -> p i m", m=M),
                                 in_=ps[0:C, 0, 0:NT * M].rearrange("p (i t m) -> p i m t", t=TPI, m=M), axis=AX.X, op=ALU.add))
            link(V.tensor_scalar(s64[:, 0, :], s64[:, 0, :], 1e-12, None, ALU.add))
            link(V.reciprocal(s64[:, 1, :], s64[:, 0, :]))
            V.tensor_tensor(s64[:, 2, :], ps[0:C, 3, 0:B * M], s64[:, 1, :], ALU.mult).then_inc(sg("l0_stf1"), 1)
            dve.wait_ge(sg("l0_qkv"), 1)
            q0, k0, v0 = (qkv0[:, a, :].rearrange("p (i m) -> p i m", m=M) for a in range(3))
            V.tensor_tensor(pr[:, :, :, :], last_dim(q0, M), mid_dim(k0, 2, M), ALU.mult).then_inc(sg("l0_prod"), 1)
            dve.wait_ge(sg("l0_sc_ps"), 1)
            sc = ps[0:C, 1, 0:B * M * M].rearrange("p (a n) -> p a n", n=M)
            link(V.tensor_reduce(out=s64[:, 3, :], in_=sc, axis=AX.X, op=ALU.max))
            pr_f = pr[:, :, :, :].rearrange("p i m n -> p (i m) n")
            pr2_f = pr2[:, :, :, :].rearrange("p i m n -> p (i m) n")
            V.tensor_tensor(pr_f, sc, last_dim(s64[:, 3, :], M), ALU.subtract).then_inc(sg("l0_sc"), 1)
            dve.wait_ge(sg("l0_sexp"), 1)
            link(V.tensor_reduce(out=s64[:, 3, :], in_=pr2_f, axis=AX.X, op=ALU.add))
            link(V.reciprocal(s64[:, 1, :], s64[:, 3, :]))
            link(V.tensor_tensor(pr_f, pr2_f, last_dim(s64[:, 1, :], M), ALU.mult))
            link(V.tensor_tensor(pr2[:, :, :, :], pr[:, :, :, :], mid_dim(v0, 2, M), ALU.mult))
            V.tensor_reduce(out=s64[:, 4, :], in_=pr2_f, axis=AX.X, op=ALU.add).then_inc(sg("l0_o"), 1)
            for g in range(8):
                dve.wait_ge(sg("l0_out_ps"), g + 1)
                V.tensor_tensor(xc[:, g * 512:(g + 1) * 512], ps[0:C, 2 + g % 2, :], xc[:, g * 512:(g + 1) * 512], ALU.add).then_inc(sg("l0_res"), 1)
            dve.wait_ge(sg("l0_res"), 8)

            def maxima(l, k, kp):
                dve.wait_ge(*upto(l, "s_ps", k + 1))
                if l == 1:
                    src = ps[:, 2 * kp:2 * kp + 2, :].rearrange("p h (q t) -> p (h q) t", q=TPI)
                    last = V.tensor_reduce(out=nmax[:, kp, :, :].rearrange("p h q -> p (h q)"), in_=src, axis=AX.X, op=ALU.max, negate=True)
                else:
                    for qc in range(TPI):
                        last = V.tensor_reduce(out=nmax[:, kp, :, qc], in_=ps[:, 2 * kp:2 * kp + 2, qc * N:qc * N + scores_cols(l, qc)],
                                               axis=AX.X, op=ALU.max, negate=True)
                last.then_inc(own(l, "max"), 1)

            def keys(l, n):
                if l > 1:
                    dve.wait_ge(*upto(l, "hi", n + 1))
                    if not isinstance(n, int) or n > 0 or l == 3:
                        dve.wait_ge(*upto(l, "stacked", n * STK))
                    V.tensor_tensor(lo[:, :, :], ps[0:C, 7, :].rearrange("p (a t) -> p a t", a=2), hi[:, :, :].bitcast(F32), ALU.subtract).then_inc(own(l, "lo"), 1)

            def values(l, n, par):
                dve.wait_ge(*upto(l, "v_ps", n + 1))
                if not isinstance(n, int):
                    dve.wait_ge(*upto(l, "ot", n))
                src = ps[:, 7, 0:TPI * C].rearrange("p (t h d) -> p t h d", t=TPI, d=HD)
                V.tensor_copy(vh[:, par, :, :, 0:HD], src).then_inc(own(l, "v_sb"), 1)

            def add_outputs(l, i):
                dve.wait_ge(*upto(l, "out_ps", i + 2))
                if l == 1:
                    for q in range(TPI):
                        src = ps[:, 6, q * 2 * C:(q + 1) * 2 * C].rearrange("p (h d) -> p h d", d=2 * HD)[:, :, 0:HD]
                        dst = on_all[:, TPI + i * TPI + q, :] if isinstance(i, int) else on_all[:, bass.ds(i * TPI + (TPI + q), 1), :].rearrange("p a c -> p (a c)")
                        last = V.tensor_copy(dst.rearrange("p (h d) -> p h d", d=HD), src)
                else:
                    tv = tok_all[:, bass.ds(i * TPI + TPI, TPI), :]
                    last = V.tensor_tensor(tv, ps[:, 6, 0:TPI * C].rearrange("p (t c) -> p t c", c=C), tv, ALU.add)
                last.then_inc(own(l, "added"), 1)

            def normalise(l, k, kp, ke):
                dve.wait_ge(*upto(l, "exp", 2 * k + 2))
                V.reciprocal(rrec[:, kp, :, :], rsum[:, kp, :, :]).then_inc(own(l, "rec"), 1)
                dve.wait_ge(*upto(l, "rec", k + 1))
                for hh in range(2):
                    for qc in range(TPI):
                        v = ee[:, ke, hh, qc, 0:scores_cols(l, qc)]
                        last = V.tensor_scalar(v, v, rrec[:, kp, hh, qc:qc + 1], None, ALU.mult)
                    last.then_inc(own(l, "norm"), 1)

            for l in (1, 2, 3):
                if l == 1:
                    group_norm("gn1").then_inc(sg("l1_xn"), 1)
                    dve.wait_ge(sg("l1_xn"), 1)
                    link(V.tensor_tensor(st[0:C, 7, 0:B], chmv[0:C, 0:B, 0], st[0:C, 5, 0:B], ALU.mult))
                    link(V.tensor_tensor(st[0:C, 7, 0:B], st[0:C, 7, 0:B], st[0:C, 6, 0:B], ALU.add))
                    link(V.tensor_scalar(st[0:C, 7, 0:B], st[0:C, 7, 0:B], float(N), None, ALU.mult))
                    V.tensor_copy(xsr, last_dim(st[0:C, 7, 0:B], P)).then_inc(sg("l1_xsum"), 1)
                else:
                    layer_norm(f"ln{l}")
                if l > 1:
                    V.tensor_scalar(wa(f"l{l}_q"), wa(f"l{l}_q"), QS, None, ALU.mult).then_inc(sg(f"l{l}_wq"), 1)
                keys(l, 0)
                values(l, 0, 0)
                keys(l, 1)
                maxima(l, 0, 0)
                maxima(l, 1, 1)
                normalise(l, 0, 0, 0)
                with dve.Fori(0, B // 2) as it:
                    for j in range(6):
                        k, u, par = it * 6 + j, j % 3, j // 3
                        i, npar = it * 2 + par, 1 - par
                        maxima(l, k + 2, j % 2)
                        if l > 1:
                            w = len(blocks(l)) * P
                            dve.wait_ge(*upto(l, "tr", TR0 + 2 * k + 1))
                            V.tensor_copy(et[:, 2 * u, 0:w], ps[:, 4, 0:w]).then_inc(own(l, "et0"), 1)
                        else:
                            dve.wait_ge(sg("l1_norm"), 2 * k + 2)
                            dve.wait_ge(sg("l1_ssq"), TR0 + k)
                            for hh in range(1 if u == 2 else 2):
                                a = ee[:, u, hh, :, :].rearrange("p q t -> p (q t)")
                                last = V.tensor_tensor_reduce(out=sqj[:, hh, :], in0=a, in1=a, scale=1.0, scalar=0.0, op0=ALU.mult,
                                                              op1=ALU.add, accum_out=ssq[:, par, 2 * u + hh:2 * u + hh + 1])
                            last.then_inc(sg("l1_ssq"), 1)
                            if u == 2:
                                dve.wait_ge(sg("l1_ssq"), TR0 + k + 1)
                                dve.wait_ge(sg("l1_ssq_act"), i + 1)
                                V.tensor_copy(ssqa[:, bass.ds(i, 1), :].rearrange("p a h -> p (a h)"), ssq[:, par, :]).then_inc(sg("l1_ssqa"), 1)
                        normalise(l, k + 1, (j + 1) % 2, (u + 1) % 3)
                        if u == 0:
                            values(l, i + 1, npar)
                            add_outputs(l, i - 1)
                        if u == 1:
                            keys(l, i + 2)
                add_outputs(l, B - 1)
                dve.wait_ge(*upto(l, "added", B + 1))
                if l == 1:
                    dve.wait_ge(sg("l1_ssq_ps"), 1)
                    var = junk[:, 0:B * NH]
                    sd = junk[:, 96:96 + B * NH]
                    V.tensor_scalar(st[:, 3:6, :].rearrange("p a b -> p (a b)"), ps[:, 0, 0:B * NH], 1.0 / (N * N), 1e-5 - 1.0 / (N * N),
                                    ALU.mult, ALU.add).then_inc(sg("l1_var"), 1)
                    dve.wait_ge(sg("l1_sd"), 1)
                    link(V.reciprocal(var, st[:, 0:3, :].rearrange("p a b -> p (a b)")))
                    v3 = var.rearrange("p (i g) -> p i g", g=NH)
                    s3 = sd.rearrange("p (i g) -> p i g", g=NH)
                    link(V.tensor_tensor(v3, v3, mid_dim(wb("l1_gamma"), 1, B), ALU.mult))
                    link(V.scalar_tensor_tensor(out=s3, in0=v3, scalar=-1.0 / N, in1=mid_dim(wb("l1_beta"), 1, B), op0=ALU.mult, op1=ALU.add))
                    dve.wait_ge(sg("l1_vs_ps"), 4)
                    on5 = on[:, :, :].rearrange("p (i q) (g d) -> p i q g d", q=TPI, d=HD)
                    vo = big[:, 0:B * C].rearrange("p (i g d) -> p i g d", g=NH, d=HD)
                    for c in range(4):
                        n = min(5, B - 5 * c)
                        last = V.tensor_tensor(vo[:, 5 * c:5 * c + n], ps[:, 1 + c, 0:n * C].rearrange("p (i g d) -> p i g d", g=NH, d=HD),
                                               last_dim(s3[:, 5 * c:5 * c + n], HD), ALU.mult)
                    link(last)
                    for r in range(4):
                        i0, i1 = 4 * r, 4 * r + 4
                        for q in range(TPI):
                            last = V.tensor_tensor(on5[:, i0:i1, q], on5[:, i0:i1, q], last_dim(v3[:, i0:i1], HD), ALU.mult)
                        link(last)
                        for q in range(TPI):
                            last = V.tensor_tensor(on5[:, i0:i1, q], on5[:, i0:i1, q], vo[:, i0:i1], ALU.add)
                        last.then_inc(sg("l1_out"), 1)
                    for g in range(8):
                        dve.wait_ge(sg("l1_y_ps"), g + 1)
                        V.tensor_copy(tok[:, g * 4:(g + 1) * 4, :], ps[:, 6 + g % 2, 0:4 * C].rearrange("p (t c) -> p t c", c=C)).then_inc(sg("l1_tok"), 1)
                    dve.wait_ge(sg("l1_tok"), 8)
                if l == 2:
                    n1, n2 = HID // NG, C // NG
                    V.tensor_reduce(out=s64[:, 0, 0:NG], in_=wa("f2_w1", C)[:, 0:NG * n1].rearrange("p (g o) -> p g o", g=NG), axis=AX.X, op=ALU.add).then_inc(sg("f2_wsum"), 1)
                    w2v = wb("f2_w2").rearrange("p (j o) -> p j o", j=NJ)
                    for j in range(NJ):
                        last = V.tensor_reduce(out=cmp[:, j, 0:NG], in_=w2v[:, j, 0:NG * n2].rearrange("p (g o) -> p g o", g=NG), axis=AX.X, op=ALU.add)
                    link(last)
                    V.tensor_reduce(out=amax[:, 2, :], in_=cmp[:, 0:NJ, 0:NG].rearrange("p j g -> p g j"), axis=AX.X, op=ALU.add).then_inc(sg("f2_wsum"), 1)
                    dve.wait_ge(sg("f2_wtot"), 1)
                    V.tensor_scalar(s64[:, 1, 0:NG], ps[0:C, 0, 0:NG], -1.0 / (n1 * C), None, ALU.mult)
                    V.tensor_scalar(amax[:, 3, :], ps[:, 1, 0:NG], -1.0 / (n2 * HID), None, ALU.mult).then_inc(sg("f2_z"), 1)
                    V.memset(wa("f2_w1", C)[:, NG * n1:HID], 0.0).then_inc(sg("f2_w1z"), 1)
                    V.memset(w2v[:, :, NG * n2:C], 0.0).then_inc(sg("f2_w2z"), 1)
                    layer_norm("lnf2")
                    with dve.Fori(0, NG) as g:
                        dve.wait_ge(sg("f2_y1"), g * 6 + 12)
                        V.tensor_reduce(out=amax[:, 0, bass.ds(g, 1)], in_=y1[:, :, bass.ds(g * GT, GT)], axis=AX.XY, op=ALU.max,
                                        apply_absolute_value=True).then_inc(sg("f2_am"), 1)
                    dve.wait_ge(sg("f2_am"), NG)
                    dve.wait_ge(sg("f2_w2s"), NG)
                    dve.sem_inc(sg("f2_amax0"), 1)

                    def quant_scale(k):
                        dve.wait_ge(sg(f"f2_gmax{k}"), 1)
                        link(V.tensor_scalar(amax[:, 2 * k + 1, :], amax[:, 2 * k + 1, :], QEPS, None, ALU.add))
                        link(V.reciprocal(amax[:, 2 * k, :], amax[:, 2 * k + 1, :]))
                        link(V.tensor_scalar(amax[:, 2 * k, :], amax[:, 2 * k, :], QB, None, ALU.mult))

                    quant_scale(0)
                    for g in range(NG):
                        v = y1[:, :, g * GT:(g + 1) * GT]
                        link(V.tensor_scalar(v, v, amax[:, 0, g:g + 1], QB - QEPS, ALU.mult, ALU.min))
                        V.tensor_scalar(v, v, -QB + QEPS, None, ALU.max).then_inc(sg("f2_quant"), 1)
                    for g in range(NG):
                        for b in range(2):
                            dve.wait_ge(sg("f2_y2_ps"), 2 * g + b + 1)
                            t0 = g * 6 + b * 3
                            V.tensor_tensor(y2[:, t0:t0 + 3, :], ps[:, 4 + (g % 2) * 2 + b, 0:3 * C].rearrange("p (t c) -> p t c", c=C),
                                            mid_dim(wb("f2_b2"), 1, 3), ALU.add).then_inc(sg("f2_y2"), 1)
                        dve.wait_ge(sg("f2_y2"), 2 * g + 2)
                        last = V.tensor_reduce(out=amax[:, 2, g:g + 1], in_=y2[:, g * 6:(g + 1) * 6, :], axis=AX.XY, op=ALU.max, apply_absolute_value=True)
                    last.then_inc(sg("f2_amax1"), 1)
                    quant_scale(1)
                    for g in range(NG):
                        v, tv = y2[:, g * 6:(g + 1) * 6, :], tok[:, g * 6:(g + 1) * 6, :]
                        link(V.tensor_scalar(v, v, amax[:, 2, g:g + 1], QB - QEPS, ALU.mult, ALU.min))
                        link(V.scalar_tensor_tensor(out=tv, in0=v, scalar=-QB + QEPS, in1=tv, op0=ALU.max, op1=ALU.add))
            layer_norm("lnf3")
            dve.wait_ge(sg("f3_gl_ps"), 1)
            gl, ge = gate[:, 0, :, :], gate[:, 1, :, :]
            gp = ps[:, 0, 0:NT * NE].rearrange("p (t e) -> p t e", e=NE)
            link(V.tensor_reduce(out=st[:, 0, :], in_=gp, axis=AX.X, op=ALU.max))
            V.tensor_tensor(gl, gp, last_dim(st[:, 0, :], NE), ALU.subtract).then_inc(sg("f3_gl"), 1)
            dve.wait_ge(sg("f3_gexp"), 1)
            link(V.tensor_reduce(out=st[:, 0, :], in_=ge, axis=AX.X, op=ALU.add))
            link(V.reciprocal(st[:, 1, :], st[:, 0, :]))
            link(V.tensor_tensor(gl, ge, last_dim(st[:, 1, :], NE), ALU.mult))
            pairs = [(0, 1), (0, 2), (0, 3), (1, 2), (1, 3), (2, 3)]
            c = {ab: cmp[:, n, :] for n, ab in enumerate(pairs)}
            for a, b in pairs:
                last = V.tensor_tensor(c[a, b], gate[:, 0, :, a], gate[:, 0, :, b], ALU.is_ge)
            link(last)
            terms = [([(0, 1), (0, 2), (0, 3)], [], ALU.is_gt, 1.5), ([(0, 1)], [(1, 2), (1, 3)], ALU.is_lt, -0.5),
                     ([(0, 2), (1, 2)], [(2, 3)], ALU.is_lt, 0.5), ([(0, 3), (1, 3), (2, 3)], [], ALU.is_lt, 1.5)]
            for e, (plus, minus, _, _) in enumerate(terms):
                (x, y), z = (plus + minus)[:2], (plus + minus)[2]
                V.tensor_tensor(gsel[:, e, :], c[x], c[y], ALU.add if y in plus else ALU.subtract)
            link(V.memset(junk[:, 0:1], 0.0))
            for e, (plus, minus, _, _) in enumerate(terms):
                z = (plus + minus)[2]
                V.tensor_tensor(gsel[:, e, :], gsel[:, e, :], c[z], ALU.add if z in plus else ALU.subtract)
            link(V.memset(junk[:, 0:1], 0.0))
            for e, (_, _, op, edge) in enumerate(terms):
                last = V.scalar_tensor_tensor(out=gate[:, 1, :, e], in0=gsel[:, e, :], scalar=edge, in1=gate[:, 0, :, e], op0=op, op1=ALU.mult)
            link(last)
            link(V.tensor_reduce(out=st[:, 0, :], in_=ge, axis=AX.X, op=ALU.add))
            link(V.tensor_scalar(st[:, 0, :], st[:, 0, :], 1e-9, None, ALU.add))
            link(V.reciprocal(st[:, 1, :], st[:, 0, :]))
            link(V.tensor_tensor(gl, ge, last_dim(st[:, 1, :], NE), ALU.mult))

            def split(t, par):
                x = xn[:, bass.ds(t * 512, 512)]
                V.tensor_copy(xhl[:, par, 0, :], x).then_inc(sg("moe_x"), 1)
                dve.wait_ge(sg("moe_x"), 2 * t + 1)
                V.tensor_tensor(xhl[:, par, 1, :], x, xhl[:, par, 0, :].bitcast(F32), ALU.subtract).then_inc(sg("moe_x"), 1)

            split(0, 0)
            with dve.Fori(0, NT // 8) as it:
                for par in range(2):
                    t = it * 2 + par
                    split(t + 1, 1 - par)
                    dve.wait_ge(sg("moe_y_ps"), t + 1)
                    for q in range(4):
                        V.tensor_tensor(ysc[:, q], ps[:, q, 0:NE * C].rearrange("p (e c) -> p e c", e=NE),
                                        wb("f3_b2").rearrange("p (e c) -> p e c", e=NE), ALU.add).then_inc(sg("moe_y"), 1)
                    dve.wait_ge(sg("moe_y"), t * 4 + 8)
                    V.tensor_tensor(ysc[:, :, :, :].rearrange("p q e c -> p (q e) c"), ysc[:, :, :, :].rearrange("p q e c -> p (q e) c"),
                                    last_dim(gate[:, 0, bass.ds(t * 4, 4), :].rearrange("p q e -> p (q e)"), C), ALU.mult).then_inc(sg("moe_w"), 1)
                    dve.wait_ge(sg("moe_w"), t + 1)
                    V.tensor_reduce(out=yred[:, :, :], in_=ysc[:, :, :, :].rearrange("p q e c -> p q c e"), axis=AX.X, op=ALU.add).then_inc(sg("moe_s"), 1)
                    dve.wait_ge(sg("moe_s"), t + 1)
                    tv = tok[:, bass.ds(t * 4, 4), :]
                    V.tensor_tensor(tv, yred[:, :, :], tv, ALU.add).then_inc(sg("moe_block"), 1)


def kernel(**inputs):
    from concourse import bacc
    from concourse.bass_utils import run_bass_kernel_spmd

    def get(name):
        return np.asarray(inputs[name])

    def heads_apart(w, bias=None):
        out = np.zeros((P, 2, C), w.dtype)
        out[:C].reshape(3, 2 * HD, 2, C)[:, :HD] = w.reshape(2, 3, HD, C).transpose(1, 2, 0, 3)
        if bias is not None:
            out[ONE, 0] = bias
        return out

    def with_bias(w, bias):
        return np.concatenate([w, bias.reshape(1, -1)])

    d0 = C // H0
    w0 = get("L0_conv_qkv_w").reshape(H0, 3, d0, C)
    w2, w3, b3 = get("L2_attn_w_attn"), get("L3_attn_qkv_w").T, get("L3_attn_qkv_b")
    def by_width(w):
        return w.reshape(-1, NH, HD).transpose(0, 2, 1).reshape(-1, C)

    parts96 = {
        "l0_q": w0[:, 0].reshape(C, C).T, "l0_k": w0[:, 1].reshape(C, C).T, "l0_v": w0[:, 2].reshape(C, C).T,
        "l0_p": get("L0_conv_proj_w").T, "l0_pb": get("L0_conv_proj_b")[:, None],
        "l1_q": get("L1_conv_Wq").T, "l1_k": get("L1_conv_Wk").T, "l1_v": get("L1_conv_Wv").T,
        "l1_hw": np.repeat(get("L1_conv_head_w").T, HD, axis=0), "l1_p": with_bias(get("L1_conv_projW").T, get("L1_conv_projb")),
        "l2_q": by_width(w2[:, :C]), "l2_k": by_width(w2[:, C:2 * C]), "l2_v": w2[:, 2 * C:], "l2_p": heads_apart(get("L2_attn_w_proj")),
        "f2_w1": with_bias(get("L2_ffn_W1").T, get("L2_ffn_b1")),
        "l3_q": by_width(with_bias(w3[:, :C], b3[:C])), "l3_k": by_width(with_bias(w3[:, C:2 * C], b3[C:2 * C])), "l3_v": with_bias(w3[:, 2 * C:], b3[2 * C:]),
        "l3_p": heads_apart(get("L3_attn_out_w").T, get("L3_attn_out_b")),
        "f3_gate": with_bias(get("L3_ffn_gate_w"), get("L3_ffn_gate_b")),
        "f3_w1": with_bias(get("L3_ffn_w1").transpose(1, 0, 2).reshape(C, NE * HID), get("L3_ffn_b1")),
    }

    def rows(v):
        return np.broadcast_to(v.reshape(1, -1), (P, v.size))

    def padded(m):
        out = np.zeros((P, m.shape[1]), m.dtype)
        out[:m.shape[0]] = m
        return out

    f = np.float32
    parts128 = {
        "ident": np.eye(P, dtype=f),
        "avg3": padded(np.kron(np.eye(32, dtype=f), np.full((3, 3), 1 / 3, f))),
        "sum12": padded(np.kron(np.eye(H0, dtype=f), np.ones((d0, d0), f))),
        "mask": np.triu(np.full((P, P), NEG, f), 1),
        "l1_gamma": rows(get("L1_conv_gamma")), "l1_beta": rows(get("L1_conv_beta")),
        "f2_w2": get("L2_ffn_W2").T.reshape(NJ, P, C).transpose(1, 0, 2).reshape(P, -1),
        "f2_b2": rows(get("L2_ffn_b2")),
        "f3_w2": get("L3_ffn_w2").reshape(NE * NJ, P, C).transpose(1, 0, 2).reshape(P, -1), "f3_b2": rows(get("L3_ffn_b2")),
    }
    arrays = {
        "x_in": np.ascontiguousarray(get("x").transpose(1, 0, 2, 3).reshape(C, B * N)),
        "w96_in": np.ascontiguousarray(np.concatenate([padded(parts96[n].reshape(len(parts96[n]), -1)) for n, _ in W96], axis=1)),
        "w128_in": np.ascontiguousarray(np.concatenate([parts128[n].reshape(P, -1) for n, _ in W128], axis=1)),
    }
    nc = bacc.Bacc("TRN2", target_bir_lowering=False, num_devices=1)
    args = [nc.dram_tensor(n, a.shape, mybir.dt.from_np(a.dtype), kind="ExternalInput").ap() for n, a in arrays.items()]
    out = nc.dram_tensor("out", [P, NT, C], F32, kind="ExternalOutput").ap()
    hybrid_kernel(nc, *args, out)
    got = run_bass_kernel_spmd(nc, [arrays], core_ids=[0]).results[0]["out"]
    return np.ascontiguousarray(got.transpose(1, 0, 2).reshape(B, N, C).transpose(0, 2, 1)).reshape(B, C, HH, WW)
```

```python
import numpy as np
from contextlib import ExitStack

import concourse.bass as bass
from concourse import mybir

F32 = mybir.dt.float32
BF16 = mybir.dt.bfloat16
F32R = mybir.dt.float32r
ALU = mybir.AluOpType
ACT = mybir.ActivationFunctionType
AX = mybir.AxisListType

B, C, HH, WW = 16, 96, 16, 16
N = HH * WW
P = 128
NT = B * N // P
TPI = N // P
SB = 8
M = (HH // SB) * (WW // SB)
H0 = 8
NH, HD = 6, 16
QS = HD ** -0.5
HID = 4 * C
NJ = HID // P
NG = 5
GI = B // NG
GT = GI * N
NE = 4
QB = 128.0
QEPS = 1e-5
STK = 16 * 6
START = 1
TR0 = 3
NEG = -1e30

ONE = C
W96 = [("l0_q", C), ("l0_k", C), ("l0_v", C), ("l0_p", C), ("l0_pb", 1),
       ("l1_q", C), ("l1_k", C), ("l1_v", C), ("l1_hw", NH), ("l1_p", C),
       ("l2_q", C), ("l2_k", C), ("l2_v", C), ("l2_p", 2 * C),
       ("f2_w1", HID),
       ("l3_q", C), ("l3_k", C), ("l3_v", C), ("l3_p", 2 * C),
       ("f3_gate", NE), ("f3_w1", NE * HID)]
W128 = [("ident", P), ("avg3", C), ("sum12", C), ("mask", P),
        ("l1_gamma", NH), ("l1_beta", NH),
        ("f2_w2", NJ * C), ("f2_b2", C), ("f3_w2", NE * NJ * C), ("f3_b2", NE * C)]


def columns(parts):
    at, where = 0, {}
    for name, n in parts:
        where[name] = (at, at + n)
        at += n
    return where, at


NORM = {"gn0": 1, "gn1": 2, "ln2": 3, "lnf2": 4, "ln3": 5, "lnf3": 6}
TURN = {"ln2": 0, "lnf2": 8, "ln3": 16, "lnf3": 24}


LOOP_ADDS = {"xb": B + 2, "q_ps": B + 2, "hi": B + 2, "lo": B + 2, "stacked": STK * (B + 2), "v_ps": B + 1, "v_sb": B + 1,
             "s_ps": 3 * B + 2, "max": 3 * B + 2, "exp": 6 * B + 2, "rec": 3 * B + 1, "norm": 6 * B + 2, "tr": 6 * B, "et0": 3 * B, "et1": 3 * B,
             "av": B + 1, "ot": B + 1, "out_ps": B + 1, "added": B + 1}


F2_PE = ["h0", "h1", "h2", "h3", "y0", "h4", "y1", "y2", "y3", "y4"]
F2_ACT = ["c0", "c1", "c2", "e0", "c3", "e1", "c4", "e2", "e3", "e4"]
F2_DVE = ["a0", "a1", "q0", "a2", "q1", "a3", "q2", "y0", "a4", "q3", "y1", "f0", "q4", "y2", "f1", "y3", "f2", "y4", "f3", "f4"]


C96, N96 = columns(W96)
C128, N128 = columns(W128)


def hybrid_kernel(nc, x_d, w96_d, w128_d, out_d):
    ctx = ExitStack()
    with ctx:
        def sb(name, shape, dt=F32):
            return ctx.enter_context(nc.sbuf_tensor(name, shape, dt))

        sems = {}

        def sg(name):
            if name not in sems:
                sems[name] = ctx.enter_context(nc.semaphore(name))
            return sems[name]

        def own(l, what):
            return sg(f"l1_{what}" if l == 1 else f"causal_{what}")

        def upto(l, what, count):
            return own(l, what), count + (LOOP_ADDS[what] if l == 3 else 0)

        mix_d = nc.dram_tensor("l1_mix", [B, NH, N, HD], F32, kind="Internal").ap()

        w96 = sb("w96", [P, N96])
        w128 = sb("w128", [P, N128])
        xc = sb("xc", [C, B * N])
        xn = sb("xn", [P, (B + 2) * N])
        tok_all = sb("tok", [P, TPI + NT, C])
        tok = tok_all[:, TPI:, :]
        on_all = sb("on", [P, TPI + NT, C])
        on = on_all[:, TPI:, :]
        on1 = on_all[:, :, :].rearrange("p (q i) c -> p q i c", q=TPI)
        big = sb("big", [P, NJ * NG * GT])
        ones = sb("ones", [P, P])
        identb = sb("identb", [P, P], BF16)
        maskb = sb("maskb", [P, P], BF16)
        chst = sb("chst", [P, NT, 6])
        chmv = sb("chmv", [P, NT, 2])
        st = sb("st", [P, 8, NT])
        xb = sb("xb", [P, 2, N])
        qs = sb("qs", [C, N])
        kh = sb("kh", [P, 2, N])
        hi = sb("hi", [C, 2, N], F32R)
        lo = sb("lo", [C, 2, N], F32R)
        qk = sb("qk", [P, 2, NH, 2, N], F32R)
        vh = sb("vh", [P, 2, TPI, NH, 2 * HD])
        nmax = sb("nmax", [P, 2, 2, TPI])
        rsum = sb("rsum", [P, 2, 2, TPI])
        rrec = sb("rrec", [P, 2, 2, TPI])
        ee = sb("ee", [P, 3, 2, TPI, N])
        ots = sb("ots", [P, 2, N])
        junk = sb("junk", [P, N])
        sqa = sb("sqa", [P, TPI * N])
        sqj = sb("sqj", [P, 2, TPI * N])
        ssq = sb("ssq", [P, 2, NH])
        ssqa = sb("ssqa", [P, B, NH])

        ps = ctx.enter_context(nc.psum_tensor("ps", [P, 8, 512], F32))

        def wa(name, rows=P):
            a, b = C96[name]
            return w96[0:rows, a:b]

        def wb(name, rows=P):
            a, b = C128[name]
            return w128[0:rows, a:b]

        ident = wb("ident")

        def last_dim(ap, n):
            return ap.unsqueeze(ap.ndim).broadcast_to(list(ap.shape) + [n])

        def mid_dim(ap, at, n):
            shape = list(ap.shape)
            return ap.unsqueeze(at).broadcast_to(shape[:at] + [n] + shape[at:])

        bd_w = 2 * M * B + M
        l0_xt = big[:, 0:NT * C].rearrange("p (t c) -> p t c", c=C)
        l0_bd = big[:, NT * C:NT * C + B * bd_w]
        l0_at = big[0:B * M, NT * C + B * bd_w:NT * C + B * bd_w + B * N]
        qkv0 = sb("qkv0", [C, 3, B * M])
        rowsum = sb("rowsum", [C, B * N // SB])
        stf = sb("stf", [C, B * M])
        aff = sb("aff", [P, NT, M])
        a0 = sb("a0", [P, NT, M])
        pr = sb("pr", [C, B, M, M])
        pr2 = sb("pr2", [C, B, M, M])
        s64 = sb("s64", [C, 6, B * M])
        stft = sb("stft", [B * M, C])
        xsr = big[0:C, 2048:2048 + B * P].rearrange("p (i r) -> p i r", r=P)
        et = big[:, 4096:4096 + NH * 2 * N].rearrange("p (h x) -> p h x", h=NH)
        xt = big[:, 4096:4096 + NT * C].rearrange("p (t c) -> p t c", c=C)
        qh = big[:, 7168:7168 + 2 * NH * N].rearrange("p (a h t) -> p a h t", a=2, h=NH)
        y1 = big[:, :].rearrange("p (j t) -> p j t", j=NJ)
        y2 = on
        ysc = big[:, 2048:2048 + 4 * NE * C].rearrange("p (q e c) -> p q e c", q=4, e=NE)
        yred = big[:, 3584:3584 + 4 * C].rearrange("p (q c) -> p q c", q=4)
        h3 = big[:, 4096:4096 + 4 * 512].rearrange("p (s t) -> p s t", s=4)
        qk_f = qk[:, :, :, :, :].rearrange("p a h b x -> p (a h b x)")
        xhl = qk_f[:, 0:2048].rearrange("p (a b t) -> p a b t", a=2, b=2)
        w1hl = qk_f[:, 2048:2048 + 2 * NE * HID].rearrange("p (b x) -> p b x", b=2)
        amax = sb("amax", [P, 4, NG])
        gate = sb("gate", [P, 2, NT, NE])
        cmp = sb("cmp", [P, 6, NT])
        gsel = sb("gsel", [P, NE, NT])

        block = ctx.enter_context(nc.Block())

        def scores_cols(l, qc):
            return N if l == 1 else P * (qc + 1)

        def blocks(l):
            return [(q, t) for t in range(TPI) for q in range(TPI) if l == 1 or t <= q]

        @block.sync
        def _(sp):
            half = B * N // 4
            for i in range(4):
                sp.dma_start(xc[:, i * half:(i + 1) * half], x_d[:, i * half:(i + 1) * half]).then_inc(sg(f"x_loaded{i}"), 16)
            sp.dma_start(w128[:, :], w128_d).then_inc(sg("w128_loaded"), 16)
            sp.dma_start(w96[:, :], w96_d).then_inc(sg("w96_loaded"), 16)
            for r in range(4):
                sp.wait_ge(sg("l1_out"), r + 1)
                for q in range(TPI):
                    sp.dma_start(mix_d[4 * r:4 * r + 4, :, q * P:(q + 1) * P, :].rearrange("i g q d -> q (i g) d"),
                                 on1[:, q, 4 * r + 1:4 * r + 5, :].rearrange("p i (g d) -> p (i g) d", d=HD)).then_inc(sg(f"l1_stored{r}"), 16)
            for l in (2, 3):

                def stack(n, par):
                    for part, moves in ((hi, ((0, 0, 2), (1, 0, 1), (2, 1, 2))), (lo, ((3, 0, 2), (2, 0, 1), (1, 1, 2)))):
                        sp.wait_ge(*upto(l, "hi" if part is hi else "lo", n + 1))
                        for t, a0, a1 in moves:
                            sp.dma_start(qk[t * HD:(t + 1) * HD, par, :, a0:a1, :].bitcast(F32),
                                         part[:, a0:a1, :].bitcast(F32)).then_inc(own(l, "stacked"), 16)

                stack(0, 0)
                stack(1, 1)
                with sp.Fori(0, B // 2) as it:
                    for par in range(2):
                        stack(it * 2 + (par + 2), par)
                sp.wait_ge(*upto(l, "stacked", STK * (B + 2)))
            with sp.Fori(0, NT // 4) as t:
                sp.wait_ge(sg("moe_block"), t + 1)
                sp.dma_start(out_d[:, bass.ds(t * 4, 4), :], tok[:, bass.ds(t * 4, 4), :]).then_inc(sg("stored"), 16)
            sp.wait_ge(sg("stored"), 16 * (NT // 4))


        @block.gpsimd
        def _(pool):
            nc.gpsimd.memset(ones[:, :], 1.0).then_inc(sg("ones_set"), 1)
            nc.gpsimd.memset(l0_bd, 0.0).then_inc(sg("bd_zeroed"), 1)
            nc.gpsimd.memset(xn[:, B * N:], 0.0).then_inc(sg("pad_zeroed"), 1)
            pool.wait_ge(sg("pad_zeroed"), 1)
            pool.sem_inc(sg("zeroed"), START)
            for n, t in enumerate((qh[C:P], xn[C:P, 0:B * N], xb[C:P], kh[C:P], ots[:, :, :], vh[:, :, :, :, :], qk[:, :, :, :, :].bitcast(F32),
                      tok_all[:, 0:TPI, :], on_all[:, 0:TPI, :])):
                pool.wait_ge(sg("zeroed"), START + n)
                nc.gpsimd.memset(t, 0.0).then_inc(sg("zeroed"), 1)
            pool.wait_ge(sg("zeroed"), START + 9)
            for n, t in enumerate((xn[ONE:ONE + 1, :], xb[ONE:ONE + 1, :, :], ots[ONE:ONE + 1, :, :])):
                nc.gpsimd.memset(t, 1.0).then_inc(sg("ones_rows"), 1)
                pool.wait_ge(sg("ones_rows"), n + 1)
            pool.wait_ge(sg("w128_loaded"), 16)
            nc.gpsimd.tensor_copy(identb[:, :], ident).then_inc(sg("bf_consts"), 1)
            nc.gpsimd.tensor_copy(maskb[:, :], wb("mask")).then_inc(sg("bf_consts"), 1)
            pool.wait_ge(sg("pad_zeroed"), 1)

            def stage(l, n, par):
                pool.wait_ge(sg("pad_zeroed"), 1)
                nc.gpsimd.tensor_copy(xb[0:C, par, :], xn[0:C, bass.ds(n * N, N)]).then_inc(own(l, "xb"), 1)

            def mix(l, n, par):
                pool.wait_ge(sg("l1_q_sb"), n + 1)
                for g in range(NH):
                    last = nc.gpsimd.tensor_tensor(qh[0:C, par, g, :], qs[:, :], wa("l1_hw", C)[:, g:g + 1].broadcast_to([C, N]), ALU.mult)
                last.then_inc(sg("l1_qmix"), 1)

            for l in (1, 2, 3):
                pool.wait_ge(sg("w96_loaded"), 16)
                if l == 1:
                    pool.wait_ge(sg("l0_res"), 8)
                    nc.gpsimd.memset(et[:, 3:NH], 0.0).then_inc(sg("et_zeroed"), 1)
                for n in range(2):
                    pool.wait_ge(sg(f"l{l}_xn"), n + 1 if l == 1 else 1)
                    stage(l, n, n)
                if l == 1:
                    for n in range(2):
                        mix(l, n, n)
                    pool.wait_ge(sg("l1_xn"), B)
                with pool.Fori(0, B // 2) as it:
                    for par in range(2):
                        i = it * 2 + par
                        pool.wait_ge(*upto(l, "v_ps", i + 1))
                        stage(l, i + 2, par)
                        if l == 1:
                            pool.wait_ge(sg("l1_s_ps"), i * 3 + 3)
                            mix(l, i + 2, par)
                if l == 1:
                    flat = mix_d.rearrange("i g q d -> (i g q d)").rearrange("(t p c) -> p t c", p=P, c=C)
                    for r in range(4):
                        pool.wait_ge(sg(f"l1_stored{r}"), 16 * TPI)
                        pool.dma_start(tok[:, r * 8:(r + 1) * 8, :], flat[:, r * 8:(r + 1) * 8, :]).then_inc(sg(f"l1_mixed{r}"), 16)
                if l == 3:
                    pool.wait_ge(*upto(l, "max", 3 * B + 2))
                    pool.wait_ge(*upto(l, "stacked", STK * (B + 2)))
                    nc.gpsimd.tensor_copy(w1hl[:, 0, :], wa("f3_w1")).then_inc(sg("f3_whi"), 1)
                    pool.wait_ge(sg("f3_whi"), 1)
                    nc.gpsimd.tensor_tensor(w1hl[:, 1, :], wa("f3_w1"), w1hl[:, 0, :].bitcast(F32), ALU.subtract).then_inc(sg("f3_wlo"), 1)
                if l == 2:
                    for step in F2_DVE:
                        if step[0] in "ay":
                            k, g = "ay".index(step[0]), int(step[1])
                            pool.wait_ge(sg(f"f2_amax{k}"), g + 1)
                            nc.gpsimd.partition_all_reduce(amax[:, 2 * k + 1, g:g + 1], amax[:, 2 * k, g:g + 1], P,
                                                           bass.bass_isa.ReduceOp.max).then_inc(sg(f"f2_gmax{k}"), 1)

        @block.scalar
        def _(act):
            for name in ["l1_et0", "l1_et1", "causal_et1", "moe_h"]:
                act.sem_inc(sg(name), START)
            def norm_sqrt(name, rows, cols):
                act.wait_ge(sg("norm_ve"), NORM[name])
                nc.scalar.activation(st[0:rows, 3, 0:cols], st[0:rows, 2, 0:cols], ACT.Sqrt).then_inc(sg("norm_sd"), 1)

            def norm_tail(name):
                norm_sqrt(name, P, NT)
                act.wait_ge(sg("norm_scale"), TURN[name] // 8 + 1)
                for g in range(9):
                    if g < 8:
                        t = 4 * g + 3
                        nc.scalar.activation(on[:, t, :], tok[:, t, :], ACT.Identity, bias=st[:, 6, t:t + 1],
                                             scale=st[:, 5, t:t + 1]).then_inc(sg("ln_ta"), 1)
                    if g >= 1:
                        act.wait_ge(sg("ln_t_ps"), TURN[name] + g)
                        nc.scalar.activation(xn[0:C, (g - 1) * 512:g * 512], ps[0:C, 4 + (g - 1) % 4, :], ACT.Copy).then_inc(sg("xn_copied"), 1)

            norm_sqrt("gn0", C, B)
            for g in range(8):
                act.wait_ge(sg("l0_xt_ps"), g + 1)
                nc.scalar.activation(l0_xt[:, g * 4:(g + 1) * 4, :], ps[:, 4 + g % 2, 0:4 * C].rearrange("p (t c) -> p t c", c=C),
                                     ACT.Copy).then_inc(sg("l0_xt"), 1)
            act.wait_ge(sg("l0_logit"), 1)
            nc.scalar.activation(aff[:, :, :], a0[:, :, :], ACT.Exp, scale=C ** -0.5).then_inc(sg("l0_exp"), 1)
            nc.scalar.activation(st[:, 5, :], st[:, 4, :], ACT.Exp, scale=-C ** -0.5).then_inc(sg("l0_exp"), 1)
            act.wait_ge(sg("l0_qkv_ps"), 1)
            nc.scalar.activation(qkv0[:, :, :], ps[0:C, 2, 0:3 * B * M].rearrange("p (a b) -> p a b", a=3), ACT.Copy).then_inc(sg("l0_qkv"), 1)
            act.wait_ge(sg("l0_sc"), 1)
            nc.scalar.activation(pr2[:, :, :, :], pr[:, :, :, :], ACT.Exp, scale=(C // H0) ** -0.5).then_inc(sg("l0_sexp"), 1)
            act.wait_ge(sg("l0_proj_ps"), 1)
            nc.scalar.activation(s64[:, 5, :], ps[0:C, 0, 0:B * M], ACT.Identity, bias=wa("l0_pb", C)).then_inc(sg("l0_stf2"), 1)
            act.wait_ge(sg("l0_stft_ps"), 1)
            nc.scalar.activation(stft[:, :], ps[0:B * M, 1, 0:C], ACT.Copy).then_inc(sg("l0_stft"), 1)
            for g in range(8):
                act.wait_ge(sg("l0_at_ps"), g + 1)
                nc.scalar.activation(l0_at[:, g * 512:(g + 1) * 512], ps[0:B * M, 4 + g % 2, :], ACT.Copy).then_inc(sg("l0_at"), 1)

            def copy_probs(l, k, h, hh):
                w = len(blocks(l)) * P
                act.wait_ge(*upto(l, "tr", TR0 + 2 * k + hh + 1))
                nc.scalar.activation(et[:, h, 0:w], ps[:, 4 + hh, 0:w], ACT.Copy).then_inc(own(l, f"et{hh}"), 1)

            def exps(l, k, kp, ke):
                act.wait_ge(*upto(l, "max", k + 1))
                if not isinstance(k, int):
                    act.wait_ge(*upto(l, "tr", TR0 + 2 * k - 4))
                    if l == 1:
                        act.wait_ge(sg("l1_ssq"), TR0 + k - 2)
                for hh in range(2):
                    for qc in range(TPI):
                        w = scores_cols(l, qc)
                        src = ps[:, 2 * kp + hh, qc * N:qc * N + w]
                        last = nc.scalar.activation(ee[:, ke, hh, qc, 0:w], src, ACT.Exp, bias=nmax[:, kp, hh, qc:qc + 1],
                                                    accum_out=rsum[:, kp, hh, qc:qc + 1])
                    last.then_inc(own(l, "exp"), 1)

            def queries(l, n, par):
                act.wait_ge(*upto(l, "q_ps", n + 1))
                if l == 1:
                    if not isinstance(n, int) or n > 0:
                        act.wait_ge(sg("l1_qmix"), n)
                    nc.scalar.activation(qs[:, :], ps[0:C, 7, 0:N], ACT.Copy, scale=QS).then_inc(sg("l1_q_sb"), 1)
                    nc.scalar.activation(kh[0:C, par, :], ps[0:C, 7, N:2 * N], ACT.Copy).then_inc(sg("l1_k_sb"), 1)
                else:
                    if not isinstance(n, int) or n > 0 or l == 3:
                        act.wait_ge(*upto(l, "stacked", n * STK))
                    nc.scalar.activation(hi[:, :, :], ps[0:C, 7, :].rearrange("p (a t) -> p a t", a=2), ACT.Copy).then_inc(own(l, "hi"), 1)

            def outputs_to_sbuf(l, i):
                act.wait_ge(*upto(l, "av", i + 2))
                nc.scalar.activation(ots[0:C, :, :], ps[0:C, 6, :].rearrange("p (a t) -> p a t", a=2), ACT.Copy).then_inc(own(l, "ot"), 1)

            for l in (1, 2, 3):
                if l == 1:
                    norm_sqrt("gn1", C, B)
                else:
                    norm_tail(f"ln{l}")
                    act.wait_ge(sg("xn_copied"), TURN[f"ln{l}"] + 8)
                    act.sem_inc(sg(f"l{l}_xn"), 1)
                queries(l, 0, 0)
                queries(l, 1, 1)
                exps(l, 0, 0, 0)
                with act.Fori(0, B // 2) as it:
                    for j in range(6):
                        k, u, i, par = it * 6 + j, j % 3, it * 2 + j // 3, j // 3
                        exps(l, k + 1, (j + 1) % 2, (u + 1) % 3)
                        if u == 0:
                            outputs_to_sbuf(l, i - 1)
                        if l == 1 and u == 1:
                            queries(l, i + 2, par)
                        if l == 1 or u == 1:
                            copy_probs(l, k, 2 * u, 0)
                        copy_probs(l, k, 2 * u + 1, 1)
                        if l == 1 and u == 2:
                            act.wait_ge(sg("l1_norm"), 2 * k + 2)
                            nc.scalar.activation(sqa[:, :], ee[:, u, 1, :, :].rearrange("p q t -> p (q t)"), ACT.Square,
                                                 accum_out=ssq[:, par, 2 * u + 1:2 * u + 2]).then_inc(sg("l1_ssq_act"), 1)
                        if l > 1 and u == 0:
                            queries(l, i + 2, par)
                outputs_to_sbuf(l, B - 1)
                if l == 1:
                    act.wait_ge(sg("l1_var"), 1)
                    nc.scalar.activation(st[:, 0:3, :], st[:, 3:6, :], ACT.Sqrt).then_inc(sg("l1_sd"), 1)
                    for g in range(8):
                        act.wait_ge(sg("l1_xt_ps"), g + 1)
                        nc.scalar.activation(xt[:, g * 4:(g + 1) * 4, :], ps[:, 6 + g % 2, 0:4 * C].rearrange("p (t c) -> p t c", c=C),
                                             ACT.Copy).then_inc(sg("l1_xt"), 1)
                    for g in range(8):
                        act.wait_ge(sg("l1_mt_ps"), g + 1)
                        nc.scalar.activation(xn[0:C, g * 512:(g + 1) * 512], ps[0:C, 4 + g % 2, :], ACT.Copy).then_inc(sg("l1_mt"), 1)
                if l == 2:
                    act.wait_ge(sg("f2_z"), 1)
                    for g in range(NG):
                        n = HID // NG
                        nc.scalar.activation(wa("f2_w1", C)[:, g * n:(g + 1) * n], wa("f2_w1", C)[:, g * n:(g + 1) * n], ACT.Sign,
                                             bias=s64[:, 1, g:g + 1]).then_inc(sg("f2_w1s"), 1)
                    for g in range(NG):
                        n = C // NG
                        v = wb("f2_w2").rearrange("p (j o) -> p j o", j=NJ)[:, :, g * n:(g + 1) * n]
                        nc.scalar.activation(v, v, ACT.Sign, bias=amax[:, 3, g:g + 1]).then_inc(sg("f2_w2s"), 1)
                    norm_tail("lnf2")
                    act.sem_inc(sg("f2_y1"), 6)
                    for step in F2_ACT:
                        g = int(step[1])
                        if step[0] == "c":
                            for b in range(2):
                                for j in range(NJ):
                                    act.wait_ge(sg("f2_y1_ps"), g * 6 + (b * NJ + j + 1))
                                    nc.scalar.activation(y1[:, j, g * GT + b * (GT // 2):g * GT + (b + 1) * (GT // 2)], ps[:, b * NJ + j, 0:GT // 2],
                                                         ACT.Copy).then_inc(sg("f2_y1"), 1)
                        else:
                            act.wait_ge(sg("f2_quant"), g + 1)
                            nc.scalar.activation(y1[:, :, g * GT:(g + 1) * GT], y1[:, :, g * GT:(g + 1) * GT], ACT.Gelu).then_inc(sg("f2_gelu"), 1)
            norm_tail("lnf3")
            act.wait_ge(sg("f3_gl"), 1)
            nc.scalar.activation(gate[:, 1, :, :], gate[:, 0, :, :], ACT.Exp).then_inc(sg("f3_gexp"), 1)
            with act.Fori(0, NT // 4) as t:
                for s in range(NE * NJ):
                    act.wait_ge(sg("moe_h_ps"), t * (NE * NJ) + (s + 1))
                    nc.scalar.activation(h3[:, s % 4, :], ps[:, 4 + s % 4, :], ACT.Gelu).then_inc(sg("moe_h"), 1)

        @block.tensor
        def _(pe):
            for name in ["l1_tr", "causal_tr"]:
                pe.sem_inc(sg(name), TR0)
            mm = nc.tensor.matmul

            def group_sums(name):
                pe.wait_ge(sg("gn_mv"), NORM[name])
                mm(ps[0:C, 0, 0:B], wb("avg3", C), chmv[0:C, 0:B, 0], start=True, stop=True).then_inc(sg("gn_mg"), 1)
                pe.wait_ge(sg("gn_e"), NORM[name])
                mm(ps[0:C, 0, B:2 * B], wb("avg3", C), st[0:C, 1, 0:B], start=True, stop=True).then_inc(sg("gn_vg"), 1)

            def normed_to_channels(name):
                for g in range(8):
                    pe.wait_ge(sg("ln_tn"), TURN[name] + g + 1)
                    pe.wait_ge(sg("ln_ta"), TURN[name] + g + 1)
                    if g >= 4:
                        pe.wait_ge(sg("xn_copied"), TURN[name] + g - 3)
                    for t in range(4):
                        last = nc.tensor.transpose(ps[0:C, 4 + g % 4, t * P:(t + 1) * P], on[:, g * 4 + t, :], ident)
                    last.then_inc(sg("ln_t_ps"), 1)

            pe.wait_ge(sg("w128_loaded"), 16)
            group_sums("gn0")
            pe.wait_ge(sg("gn0_xn"), B)
            for g in range(8):
                if g >= 2:
                    pe.wait_ge(sg("l0_xt"), g - 1)
                for t in range(4):
                    a = (g * 4 + t) * P
                    last = nc.tensor.transpose(ps[:, 4 + g % 2, t * C:(t + 1) * C], xn[0:C, a:a + P], wb("ident", C)[:, 0:C])
                last.then_inc(sg("l0_xt_ps"), 1)
            pe.wait_ge(sg("l0_stf"), 1)
            for t in range(NT):
                i = t // TPI
                last = mm(ps[:, 1, t * M:(t + 1) * M], xn[0:C, t * P:(t + 1) * P], stf[:, i * M:(i + 1) * M], start=True, stop=True)
            last.then_inc(sg("l0_logit_ps"), 1)
            pe.wait_ge(sg("l0_aff"), 1)
            pe.wait_ge(sg("ones_set"), 1)
            mm(ps[0:C, 0, 0:NT * M], ones[:, 0:C], aff[:, :, :], start=True, stop=True)
            pe.wait_ge(sg("l0_xt"), 8)
            for i in range(B):
                for t in range(TPI):
                    last = mm(ps[0:C, 3, i * M:(i + 1) * M], l0_xt[:, i * TPI + t, :], aff[:, i * TPI + t, :], start=(t == 0), stop=(t == TPI - 1))
            last.then_inc(sg("l0_sums_ps"), 1)
            pe.wait_ge(sg("l0_bd"), 1)
            pe.wait_ge(sg("w96_loaded"), 16)
            pe.wait_ge(sg("l0_stf1"), 1)
            for a, name in enumerate(("l0_q", "l0_k", "l0_v")):
                last = mm(ps[0:C, 2, a * B * M:(a + 1) * B * M], wa(name, C), s64[:, 2, :], start=True, stop=True)
            last.then_inc(sg("l0_qkv_ps"), 1)
            pe.wait_ge(sg("l0_prod"), 1)
            mm(ps[0:C, 1, 0:B * M * M], wb("sum12", C), pr[:, :, :, :], start=True, stop=True).then_inc(sg("l0_sc_ps"), 1)
            pe.wait_ge(sg("l0_o"), 1)
            mm(ps[0:C, 0, 0:B * M], wa("l0_p", C), s64[:, 4, :], start=True, stop=True).then_inc(sg("l0_proj_ps"), 1)
            pe.wait_ge(sg("l0_stf2"), 1)
            nc.tensor.transpose(ps[0:B * M, 1, 0:C], s64[:, 5, :], wb("ident", C)[:, 0:C]).then_inc(sg("l0_stft_ps"), 1)
            for g in range(8):
                if g >= 2:
                    pe.wait_ge(sg("l0_at"), g - 1)
                for t in range(4):
                    a = (g * 4 + t) * B * M
                    last = nc.tensor.transpose(ps[0:B * M, 4 + g % 2, t * P:(t + 1) * P], l0_bd[:, a:a + B * M], ident)
                last.then_inc(sg("l0_at_ps"), 1)
            pe.wait_ge(sg("l0_stft"), 1)
            for g in range(8):
                pe.wait_ge(sg("l0_at"), g + 1)
                if g >= 2:
                    pe.wait_ge(sg("l0_res"), g - 1)
                mm(ps[0:C, 2 + g % 2, :], stft[:, :], l0_at[:, g * 512:(g + 1) * 512], start=True, stop=True).then_inc(sg("l0_out_ps"), 1)

            def score_unit(l, par, u, kp, k):
                if not isinstance(k, int):
                    pe.wait_ge(*upto(l, "exp", 2 * k - 2))
                if l == 1:
                    for hh in range(2):
                        for qc in range(TPI):
                            last = mm(ps[:, 2 * kp + hh, qc * N:(qc + 1) * N], qh[:, par, 2 * u + hh, qc * P:(qc + 1) * P],
                                      kh[:, par, :], start=True, stop=True)
                else:
                    for qc in range(TPI):
                        w = scores_cols(l, qc)
                        for hh in range(2):
                            h = 2 * u + hh
                            mm(ps[:, 2 * kp + hh, qc * N:qc * N + w], qk[:, par, h, 0, qc * P:(qc + 1) * P], qk[:, par, h, 1, 0:w],
                               start=True, stop=False)
                            last = mm(ps[:, 2 * kp + hh, qc * N + qc * P:qc * N + (qc + 1) * P], identb[:, :], maskb[:, :], start=False, stop=True)
                last.then_inc(own(l, "s_ps"), 1)

            def project_qk(l, n, par):
                pe.wait_ge(*upto(l, "xb", n + 1))
                if not isinstance(n, int):
                    pe.wait_ge(*upto(l, "v_sb", n - 1))
                    parts_ready(l, n - 1)
                mm(ps[0:C, 7, 0:N], wa(f"l{l}_q"), xb[:, par, :], start=True, stop=True)
                mm(ps[0:C, 7, N:2 * N], wa(f"l{l}_k"), xb[:, par, :], start=True, stop=True).then_inc(own(l, "q_ps"), 1)

            def parts_ready(l, n):
                for what in ("q_sb", "k_sb") if l == 1 else ("hi", "lo"):
                    if l == 1:
                        pe.wait_ge(sg(f"l1_{what}"), n + 1)
                    else:
                        pe.wait_ge(*upto(l, what, n + 1))

            def project_v(l, n, par):
                for t in range(TPI):
                    last = mm(ps[:, 7, t * C:(t + 1) * C], xb[:, par, t * P:(t + 1) * P], wa(f"l{l}_v"), start=True, stop=True)
                last.then_inc(own(l, "v_ps"), 1)

            def outputs(l, i):
                pe.wait_ge(*upto(l, "ot", i + 2))
                if l == 1:
                    for g in range(2):
                        for q in range(TPI):
                            a = (q * 2 + g) * C
                            last = nc.tensor.transpose(ps[:, 6, a:a + C], ots[0:C, g, q * P:(q + 1) * P], wb("ident", C)[:, 0:C])
                else:
                    for t in range(TPI):
                        for g in range(2):
                            last = mm(ps[:, 6, t * C:(t + 1) * C], ots[:, g, t * P:(t + 1) * P], wa(f"l{l}_p")[:, g * C:(g + 1) * C],
                                      start=(g == 0), stop=(g == 1))
                last.then_inc(own(l, "out_ps"), 1)

            def weigh_values(l, par, g):
                for tc in range(TPI):
                    q0 = 0 if l == 1 or tc == 0 else P
                    for r in range(3):
                        last = mm(ps[32 * r:32 * (r + 1), 6, g * N + q0:(g + 1) * N], vh[:, par, tc, 3 * g + r, :],
                                  et[:, 3 * g + r, tc * N:tc * N + N - q0], start=(tc == 0), stop=(tc == TPI - 1))
                return last

            def keys_ready(l, n):
                if l == 1:
                    pe.wait_ge(sg("l1_qmix"), n + 1)
                    pe.wait_ge(sg("l1_k_sb"), n + 1)
                else:
                    pe.wait_ge(*upto(l, "stacked", (n + 1) * STK))

            for l in (1, 2, 3):
                if l == 1:
                    group_sums("gn1")
                    pe.wait_ge(sg("l0_res"), 8)
                else:
                    normed_to_channels(f"ln{l}")
                pe.wait_ge(sg("bf_consts"), 2)
                pe.wait_ge(sg("ones_rows"), 3)
                pe.wait_ge(sg("et_zeroed"), 1)
                if l > 1:
                    pe.wait_ge(sg(f"l{l}_xn"), 1)
                    pe.wait_ge(sg(f"l{l}_wq"), 1)
                mm(ps[0:C, 6, :], ident[:, 0:C], xn[:, B * N:(B + 2) * N], start=True, stop=True)
                project_qk(l, 0, 0)
                parts_ready(l, 0)
                project_v(l, 0, 0)
                pe.wait_ge(*upto(l, "v_sb", 1))
                project_qk(l, 1, 1)
                keys_ready(l, 0)
                score_unit(l, 0, 0, 0, 0)
                score_unit(l, 0, 1, 1, 1)
                with pe.Fori(0, B // 2) as it:
                    for j in range(6):
                        k, u, par = it * 6 + j, j % 3, j // 3
                        i, npar = it * 2 + par, 1 - par
                        if u == 1:
                            keys_ready(l, i + 1)
                        score_unit(l, par if u == 0 else npar, (u + 2) % 3, j % 2, k + 2)
                        if u == 0:
                            for hh in range(2):
                                pe.wait_ge(*upto(l, f"et{hh}", START + k))
                            weigh_values(l, npar, 1).then_inc(own(l, "av"), 1)
                        for hh in range(2):
                            pe.wait_ge(*upto(l, "norm", 2 * k + (hh + 1)))
                            pe.wait_ge(*upto(l, f"et{hh}", START + k))
                            for b, (qc, tc) in enumerate(blocks(l)):
                                last = nc.tensor.transpose(ps[:, 4 + hh, b * P:(b + 1) * P], ee[:, u, hh, qc, tc * P:(tc + 1) * P], ident)
                            last.then_inc(own(l, "tr"), 1)
                        if u == 0:
                            project_qk(l, i + 2, par)
                        if u == 1:
                            outputs(l, i - 1)
                            parts_ready(l, i + 2)
                            project_v(l, i + 1, npar)
                        if u == 2:
                            pe.wait_ge(*upto(l, "added", i + 1))
                            pe.wait_ge(*upto(l, "v_sb", i + 1))
                            weigh_values(l, par, 0)
                for hh in range(2):
                    pe.wait_ge(*upto(l, f"et{hh}", START + 3 * B))
                weigh_values(l, (B - 1) % 2, 1).then_inc(own(l, "av"), 1)
                outputs(l, B - 1)
                pe.wait_ge(*upto(l, "max", 3 * B + 2))
                pe.wait_ge(*upto(l, "exp", 6 * B + 2))
                pe.wait_ge(*upto(l, "v_sb", B + 1))
                parts_ready(l, B + 1)
                pe.wait_ge(*upto(l, "added", B + 1))
                if l == 1:
                    pe.wait_ge(sg("l1_ssqa"), B)
                    mm(ps[:, 0, 0:B * NH], ones[:, :], ssqa[:, :, :], start=True, stop=True).then_inc(sg("l1_ssq_ps"), 1)
                    pe.wait_ge(sg("l1_xsum"), 1)
                    for i in range(B):
                        last = mm(ps[:, 1 + i // 5, (i % 5) * C:(i % 5 + 1) * C], xsr[:, i, :], wa("l1_v", C), start=True, stop=True)
                        if i % 5 == 4 or i == B - 1:
                            last.then_inc(sg("l1_vs_ps"), 1)
                    for g in range(8):
                        if g >= 2:
                            pe.wait_ge(sg("l1_xt"), g - 1)
                        for t in range(4):
                            a = (g * 4 + t) * P
                            last = nc.tensor.transpose(ps[:, 6 + g % 2, t * C:(t + 1) * C], xc[:, a:a + P], wb("ident", C)[:, 0:C])
                        last.then_inc(sg("l1_xt_ps"), 1)
                    pe.wait_ge(sg("l1_xt"), 8)

                    def project_mixed(g):
                        pe.wait_ge(sg("l1_mt"), g + 1)
                        if g >= 2:
                            pe.wait_ge(sg("l1_tok"), g - 1)
                        for t in range(4):
                            a = (g * 4 + t) * P
                            last = mm(ps[:, 6 + g % 2, t * C:(t + 1) * C], xn[:, a:a + P], wa("l1_p"), start=True, stop=True)
                        last.then_inc(sg("l1_y_ps"), 1)

                    for g in range(8):
                        if g == 0:
                            pe.wait_ge(sg("l1_vs_out"), 1)
                        pe.wait_ge(sg(f"l1_mixed{g // 2}"), 16)
                        if g >= 2:
                            pe.wait_ge(sg("l1_mt"), g - 1)
                        for t in range(4):
                            last = nc.tensor.transpose(ps[0:C, 4 + g % 2, t * P:(t + 1) * P], tok[:, g * 4 + t, :], ident)
                        last.then_inc(sg("l1_mt_ps"), 1)
                        if g >= 1:
                            project_mixed(g - 1)
                    project_mixed(7)
                if l == 2:
                    pe.wait_ge(sg("f2_wsum"), 2)
                    mm(ps[0:C, 0, 0:NG], ones[0:C, 0:C], s64[:, 0, 0:NG], start=True, stop=True)
                    mm(ps[:, 1, 0:NG], ones[:, :], amax[:, 2, :], start=True, stop=True).then_inc(sg("f2_wtot"), 1)
                    normed_to_channels("lnf2")
                    pe.wait_ge(sg("xn_copied"), TURN["lnf2"] + 8)
                    pe.wait_ge(sg("f2_w1z"), 1)
                    pe.wait_ge(sg("f2_w1s"), NG)
                    for step in F2_PE:
                        g = int(step[1])
                        if step[0] == "h":
                            for b in range(2):
                                for j in range(NJ):
                                    a = g * GT + b * (GT // 2)
                                    pe.wait_ge(sg("f2_y1"), g * 6 + (b * NJ + j + 1))
                                    mm(ps[:, b * NJ + j, 0:GT // 2], wa("f2_w1")[:, j * P:(j + 1) * P], xn[:, a:a + GT // 2],
                                       start=True, stop=True).then_inc(sg("f2_y1_ps"), 1)
                        else:
                            if g == 0:
                                pe.wait_ge(sg("f2_w2s"), NG)
                                pe.wait_ge(sg("f2_w2z"), 1)
                            pe.wait_ge(sg("f2_gelu"), g + 1)
                            for b in range(2):
                                if g >= 1:
                                    pe.wait_ge(sg("f2_y2"), 2 * (g - 1) + b + 1)
                                for t in range(3):
                                    for j in range(NJ):
                                        a = g * GT + (b * 3 + t) * P
                                        last = mm(ps[:, 6 + b, t * C:(t + 1) * C], y1[:, j, a:a + P],
                                                  wb("f2_w2")[:, j * C:(j + 1) * C], start=(j == 0), stop=(j == NJ - 1))
                                last.then_inc(sg("f2_y2_ps"), 1)
            normed_to_channels("lnf3")
            pe.wait_ge(sg("xn_copied"), TURN["lnf3"] + 8)
            for t in range(NT):
                last = mm(ps[:, 0, t * NE:(t + 1) * NE], xn[:, t * P:(t + 1) * P], wa("f3_gate"), start=True, stop=True)
            last.then_inc(sg("f3_gl_ps"), 1)
            pe.wait_ge(sg("f3_gl"), 1)
            NS = NE * NJ

            def hidden(t, par, s):
                if s >= 4:
                    pe.wait_ge(sg("moe_h"), START + t * NS + (s - 3))
                for n, (w, x) in enumerate(((0, 0), (0, 1), (1, 0))):
                    last = mm(ps[:, 4 + s % 4, :], w1hl[:, w, s * P:(s + 1) * P], xhl[:, par, x, :],
                              start=(n == 0), stop=(n == 2))
                last.then_inc(sg("moe_h_ps"), 1)

            pe.wait_ge(sg("f3_wlo"), 1)
            with pe.Fori(0, NT // 8) as it:
                for par in range(2):
                    t = it * 2 + par
                    pe.wait_ge(sg("moe_x"), 2 * t + 2)
                    for s in range(NS + 2):
                        if s < NS:
                            if s < 4:
                                pe.wait_ge(sg("moe_h"), START + t * NS)
                            hidden(t, par, s)
                        if s >= 2:
                            r = s - 2
                            e, j = r // NJ, r % NJ
                            pe.wait_ge(sg("moe_h"), START + t * NS + (r + 1))
                            for q in range(4):
                                if r == 0:
                                    pe.wait_ge(sg("moe_y"), t * 4 + (q + 1))
                                last = mm(ps[:, q, e * C:(e + 1) * C], h3[:, r % 4, q * P:(q + 1) * P],
                                          wb("f3_w2")[:, r * C:(r + 1) * C], start=(j == 0), stop=(j == NJ - 1))
                    last.then_inc(sg("moe_y_ps"), 1)

        @block.vector
        def _(dve):
            dve.sem_inc(sg("causal_et0"), START)
            dve.sem_inc(sg("l1_ssq"), TR0)
            dve.sem_inc(sg("moe_y"), 4)
            V = nc.vector
            chain = [0]

            def link(ins):
                chain[0] += 1
                ins.then_inc(sg("dve_chain"), 1)
                dve.wait_ge(sg("dve_chain"), chain[0])

            def group_norm(name):
                for i in range(B):
                    if name == "gn0" and i % 4 == 0:
                        dve.wait_ge(sg(f"x_loaded{i // 4}"), 16)
                    last = V.bn_stats(chst[0:C, i, :], xc[:, i * N:(i + 1) * N])
                link(last)
                for i in range(B):
                    last = V.bn_aggr(chmv[0:C, i, :], chst[0:C, i, :])
                last.then_inc(sg("gn_mv"), 1)
                dve.wait_ge(sg("gn_mv"), NORM[name])
                dve.wait_ge(sg("gn_mg"), NORM[name])
                link(V.tensor_copy(st[0:C, 4, 0:B], ps[0:C, 0, 0:B]))
                link(V.tensor_tensor(st[0:C, 0, 0:B], chmv[0:C, 0:B, 0], st[0:C, 4, 0:B], ALU.subtract))
                link(V.tensor_tensor(st[0:C, 1, 0:B], st[0:C, 0, 0:B], st[0:C, 0, 0:B], ALU.mult))
                V.tensor_tensor(st[0:C, 1, 0:B], st[0:C, 1, 0:B], chmv[0:C, 0:B, 1], ALU.add).then_inc(sg("gn_e"), 1)
                dve.wait_ge(sg("gn_vg"), NORM[name])
                V.tensor_scalar(st[0:C, 2, 0:B], ps[0:C, 0, B:2 * B], 1e-5, None, ALU.add).then_inc(sg("norm_ve"), 1)
                dve.wait_ge(sg("norm_sd"), NORM[name])
                link(V.reciprocal(st[0:C, 5, 0:B], st[0:C, 3, 0:B]))
                link(V.scalar_tensor_tensor(out=st[0:C, 6, 0:B], in0=st[0:C, 4, 0:B], scalar=-1.0, in1=st[0:C, 5, 0:B], op0=ALU.mult, op1=ALU.mult))
                for i in range(B):
                    V.tensor_scalar(xn[0:C, i * N:(i + 1) * N], xc[:, i * N:(i + 1) * N], st[0:C, 5, i:i + 1], st[0:C, 6, i:i + 1],
                                    ALU.mult, ALU.add).then_inc(sg("gn0_xn" if name == "gn0" else "l1_xn"), 1)

            def token_stats(tiles):
                for t in tiles:
                    last = V.bn_stats(chst[:, t, :], tok[:, t, :])
                link(last)
                for t in tiles:
                    last = V.bn_aggr(chmv[:, t, :], chst[:, t, :])
                return last

            def layer_norm(name):
                if name not in ("ln2", "ln3"):
                    link(token_stats(range(NT)))
                V.tensor_scalar(st[:, 2, :], chmv[:, :, 1], 1e-5, None, ALU.add).then_inc(sg("norm_ve"), 1)
                dve.wait_ge(sg("norm_sd"), NORM[name])
                link(V.reciprocal(st[:, 5, :], st[:, 3, :]))
                V.scalar_tensor_tensor(out=st[:, 6, :], in0=chmv[:, :, 0], scalar=-1.0, in1=st[:, 5, :], op0=ALU.mult,
                                       op1=ALU.mult).then_inc(sg("norm_scale"), 1)
                dve.wait_ge(sg("norm_scale"), TURN[name] // 8 + 1)
                for g in range(8):
                    for t in range(4 * g, 4 * g + 3):
                        last = V.tensor_scalar(on[:, t, :], tok[:, t, :], st[:, 5, t:t + 1], st[:, 6, t:t + 1], ALU.mult, ALU.add)
                    last.then_inc(sg("ln_tn"), 1)

            group_norm("gn0")
            dve.wait_ge(sg("gn0_xn"), B)
            link(V.tensor_reduce(out=rowsum[:, :], in_=xn[0:C, 0:B * N].rearrange("p (a w) -> p a w", w=SB), axis=AX.X, op=ALU.add))
            link(V.tensor_reduce(out=stf[:, :].rearrange("p (g w) -> p g w", w=WW // SB),
                                 in_=rowsum[:, :].rearrange("p (g h w) -> p g w h", h=SB, w=WW // SB), axis=AX.X, op=ALU.add))
            V.tensor_scalar(stf[:, :], stf[:, :], 1.0 / (SB * SB), None, ALU.mult).then_inc(sg("l0_stf"), 1)
            dve.wait_ge(sg("l0_logit_ps"), 1)
            lg = ps[:, 1, 0:NT * M].rearrange("p (t m) -> p t m", m=M)
            link(V.tensor_reduce(out=st[:, 4, :], in_=lg, axis=AX.X, op=ALU.max))
            link(V.tensor_scalar(st[:, 4, :], st[:, 4, :], 0.0, None, ALU.max))
            V.tensor_tensor(a0[:, :, :], lg, last_dim(st[:, 4, :], M), ALU.subtract).then_inc(sg("l0_logit"), 1)
            dve.wait_ge(sg("l0_exp"), 2)
            link(V.tensor_reduce(out=st[:, 6, :], in_=aff[:, :, :], axis=AX.X, op=ALU.add))
            link(V.scalar_tensor_tensor(out=st[:, 6, :], in0=st[:, 5, :], scalar=float(9 - M), in1=st[:, 6, :], op0=ALU.mult, op1=ALU.add))
            link(V.reciprocal(st[:, 7, :], st[:, 6, :]))
            V.tensor_tensor(aff[:, :, :], aff[:, :, :], last_dim(st[:, 7, :], M), ALU.mult).then_inc(sg("l0_aff"), 1)
            dve.wait_ge(sg("bd_zeroed"), 1)
            dve.wait_ge(sg("l0_aff"), 1)
            bd = l0_bd.rearrange("p (i x) -> p i x", x=bd_w)[:, :, 0:2 * B * M].rearrange("p i (t x) -> p i t x", t=TPI)[:, :, :, 0:M]
            V.tensor_copy(bd, aff[:, :, :].rearrange("p (i t) m -> p i t m", t=TPI)).then_inc(sg("l0_bd"), 1)
            dve.wait_ge(sg("l0_sums_ps"), 1)
            link(V.tensor_reduce(out=s64[:, 0, :].rearrange("p (i m) -> p i m", m=M),
                                 in_=ps[0:C, 0, 0:NT * M].rearrange("p (i t m) -> p i m t", t=TPI, m=M), axis=AX.X, op=ALU.add))
            link(V.tensor_scalar(s64[:, 0, :], s64[:, 0, :], 1e-12, None, ALU.add))
            link(V.reciprocal(s64[:, 1, :], s64[:, 0, :]))
            V.tensor_tensor(s64[:, 2, :], ps[0:C, 3, 0:B * M], s64[:, 1, :], ALU.mult).then_inc(sg("l0_stf1"), 1)
            dve.wait_ge(sg("l0_qkv"), 1)
            q0, k0, v0 = (qkv0[:, a, :].rearrange("p (i m) -> p i m", m=M) for a in range(3))
            V.tensor_tensor(pr[:, :, :, :], last_dim(q0, M), mid_dim(k0, 2, M), ALU.mult).then_inc(sg("l0_prod"), 1)
            dve.wait_ge(sg("l0_sc_ps"), 1)
            sc = ps[0:C, 1, 0:B * M * M].rearrange("p (a n) -> p a n", n=M)
            link(V.tensor_reduce(out=s64[:, 3, :], in_=sc, axis=AX.X, op=ALU.max))
            pr_f = pr[:, :, :, :].rearrange("p i m n -> p (i m) n")
            pr2_f = pr2[:, :, :, :].rearrange("p i m n -> p (i m) n")
            V.tensor_tensor(pr_f, sc, last_dim(s64[:, 3, :], M), ALU.subtract).then_inc(sg("l0_sc"), 1)
            dve.wait_ge(sg("l0_sexp"), 1)
            link(V.tensor_reduce(out=s64[:, 3, :], in_=pr2_f, axis=AX.X, op=ALU.add))
            link(V.reciprocal(s64[:, 1, :], s64[:, 3, :]))
            link(V.tensor_tensor(pr_f, pr2_f, last_dim(s64[:, 1, :], M), ALU.mult))
            link(V.tensor_tensor(pr2[:, :, :, :], pr[:, :, :, :], mid_dim(v0, 2, M), ALU.mult))
            V.tensor_reduce(out=s64[:, 4, :], in_=pr2_f, axis=AX.X, op=ALU.add).then_inc(sg("l0_o"), 1)
            for g in range(8):
                dve.wait_ge(sg("l0_out_ps"), g + 1)
                V.tensor_tensor(xc[:, g * 512:(g + 1) * 512], ps[0:C, 2 + g % 2, :], xc[:, g * 512:(g + 1) * 512], ALU.add).then_inc(sg("l0_res"), 1)
            dve.wait_ge(sg("l0_res"), 8)

            def maxima(l, k, kp):
                dve.wait_ge(*upto(l, "s_ps", k + 1))
                if l == 1:
                    src = ps[:, 2 * kp:2 * kp + 2, :].rearrange("p h (q t) -> p (h q) t", q=TPI)
                    last = V.tensor_reduce(out=nmax[:, kp, :, :].rearrange("p h q -> p (h q)"), in_=src, axis=AX.X, op=ALU.max, negate=True)
                else:
                    for qc in range(TPI):
                        last = V.tensor_reduce(out=nmax[:, kp, :, qc], in_=ps[:, 2 * kp:2 * kp + 2, qc * N:qc * N + scores_cols(l, qc)],
                                               axis=AX.X, op=ALU.max, negate=True)
                last.then_inc(own(l, "max"), 1)

            def keys(l, n):
                if l > 1:
                    dve.wait_ge(*upto(l, "hi", n + 1))
                    if not isinstance(n, int) or n > 0 or l == 3:
                        dve.wait_ge(*upto(l, "stacked", n * STK))
                    V.tensor_tensor(lo[:, :, :], ps[0:C, 7, :].rearrange("p (a t) -> p a t", a=2), hi[:, :, :].bitcast(F32), ALU.subtract).then_inc(own(l, "lo"), 1)

            def values(l, n, par):
                dve.wait_ge(*upto(l, "v_ps", n + 1))
                if not isinstance(n, int):
                    dve.wait_ge(*upto(l, "av", n))
                src = ps[:, 7, 0:TPI * C].rearrange("p (t h d) -> p t h d", t=TPI, d=HD)
                V.tensor_copy(vh[:, par, :, :, 0:HD], src).then_inc(own(l, "v_sb"), 1)

            def add_outputs(l, i):
                dve.wait_ge(*upto(l, "out_ps", i + 2))
                if l == 1:
                    for q in range(TPI):
                        src = ps[:, 6, q * 2 * C:(q + 1) * 2 * C].rearrange("p (h d) -> p h d", d=2 * HD)[:, :, 0:HD]
                        dst = on1[:, q, i + 1, :] if isinstance(i, int) else on1[:, q, bass.ds(i + 1, 1), :].rearrange("p a c -> p (a c)")
                        last = V.tensor_copy(dst.rearrange("p (h d) -> p h d", d=HD), src)
                else:
                    tv = tok_all[:, bass.ds(i * TPI + TPI, TPI), :]
                    last = V.tensor_tensor(tv, ps[:, 6, 0:TPI * C].rearrange("p (t c) -> p t c", c=C), tv, ALU.add)
                last.then_inc(own(l, "added"), 1)

            def normalise(l, k, kp, ke):
                dve.wait_ge(*upto(l, "exp", 2 * k + 2))
                V.reciprocal(rrec[:, kp, :, :], rsum[:, kp, :, :]).then_inc(own(l, "rec"), 1)
                dve.wait_ge(*upto(l, "rec", k + 1))
                for hh in range(2):
                    for qc in range(TPI):
                        v = ee[:, ke, hh, qc, 0:scores_cols(l, qc)]
                        last = V.tensor_scalar(v, v, rrec[:, kp, hh, qc:qc + 1], None, ALU.mult)
                    last.then_inc(own(l, "norm"), 1)

            for l in (1, 2, 3):
                if l == 1:
                    group_norm("gn1")
                    dve.wait_ge(sg("l1_xn"), B)
                    link(V.tensor_tensor(st[0:C, 7, 0:B], chmv[0:C, 0:B, 0], st[0:C, 5, 0:B], ALU.mult))
                    link(V.tensor_tensor(st[0:C, 7, 0:B], st[0:C, 7, 0:B], st[0:C, 6, 0:B], ALU.add))
                    link(V.tensor_scalar(st[0:C, 7, 0:B], st[0:C, 7, 0:B], float(N), None, ALU.mult))
                    V.tensor_copy(xsr, last_dim(st[0:C, 7, 0:B], P)).then_inc(sg("l1_xsum"), 1)
                else:
                    layer_norm(f"ln{l}")
                if l > 1:
                    V.tensor_scalar(wa(f"l{l}_q"), wa(f"l{l}_q"), QS, None, ALU.mult).then_inc(sg(f"l{l}_wq"), 1)
                keys(l, 0)
                values(l, 0, 0)
                maxima(l, 0, 0)
                maxima(l, 1, 1)
                keys(l, 1)
                normalise(l, 0, 0, 0)
                with dve.Fori(0, B // 2) as it:
                    for j in range(6):
                        k, u, par = it * 6 + j, j % 3, j // 3
                        i, npar = it * 2 + par, 1 - par
                        maxima(l, k + 2, j % 2)
                        if l > 1 and u != 1:
                            w = len(blocks(l)) * P
                            dve.wait_ge(*upto(l, "tr", TR0 + 2 * k + 1))
                            V.tensor_copy(et[:, 2 * u, 0:w], ps[:, 4, 0:w]).then_inc(own(l, "et0"), 1)
                        if l == 1:
                            dve.wait_ge(sg("l1_norm"), 2 * k + 2)
                            dve.wait_ge(sg("l1_ssq"), TR0 + k)
                            for hh in range(1 if u == 2 else 2):
                                a = ee[:, u, hh, :, :].rearrange("p q t -> p (q t)")
                                last = V.tensor_tensor_reduce(out=sqj[:, hh, :], in0=a, in1=a, scale=1.0, scalar=0.0, op0=ALU.mult,
                                                              op1=ALU.add, accum_out=ssq[:, par, 2 * u + hh:2 * u + hh + 1])
                            last.then_inc(sg("l1_ssq"), 1)
                            if u == 2:
                                dve.wait_ge(sg("l1_ssq"), TR0 + k + 1)
                                dve.wait_ge(sg("l1_ssq_act"), i + 1)
                                V.tensor_copy(ssqa[:, bass.ds(i, 1), :].rearrange("p a h -> p (a h)"), ssq[:, par, :]).then_inc(sg("l1_ssqa"), 1)
                        normalise(l, k + 1, (j + 1) % 2, (u + 1) % 3)
                        if u == 0:
                            keys(l, i + 2)
                        if u == 1:
                            add_outputs(l, i - 1)
                            values(l, i + 1, npar)
                add_outputs(l, B - 1)
                dve.wait_ge(*upto(l, "added", B + 1))
                if l == 1:
                    dve.wait_ge(sg("l1_ssq_ps"), 1)
                    var = junk[:, 0:B * NH]
                    sd = junk[:, 96:96 + B * NH]
                    V.tensor_scalar(st[:, 3:6, :].rearrange("p a b -> p (a b)"), ps[:, 0, 0:B * NH], 1.0 / (N * N), 1e-5 - 1.0 / (N * N),
                                    ALU.mult, ALU.add).then_inc(sg("l1_var"), 1)
                    dve.wait_ge(sg("l1_sd"), 1)
                    link(V.reciprocal(var, st[:, 0:3, :].rearrange("p a b -> p (a b)")))
                    v3 = var.rearrange("p (i g) -> p i g", g=NH)
                    s3 = sd.rearrange("p (i g) -> p i g", g=NH)
                    link(V.tensor_tensor(v3, v3, mid_dim(wb("l1_gamma"), 1, B), ALU.mult))
                    link(V.scalar_tensor_tensor(out=s3, in0=v3, scalar=-1.0 / N, in1=mid_dim(wb("l1_beta"), 1, B), op0=ALU.mult, op1=ALU.add))
                    dve.wait_ge(sg("l1_vs_ps"), 4)
                    on5 = on1[:, :, 1:, :].rearrange("p q i (g d) -> p q i g d", d=HD)
                    vo = big[:, 0:B * C].rearrange("p (i g d) -> p i g d", g=NH, d=HD)
                    for c in range(4):
                        n = min(5, B - 5 * c)
                        last = V.tensor_tensor(vo[:, 5 * c:5 * c + n], ps[:, 1 + c, 0:n * C].rearrange("p (i g d) -> p i g d", g=NH, d=HD),
                                               last_dim(s3[:, 5 * c:5 * c + n], HD), ALU.mult)
                    last.then_inc(sg("l1_vs_out"), 1)
                    dve.wait_ge(sg("l1_vs_out"), 1)
                    for r in range(4):
                        i0, i1 = 4 * r, 4 * r + 4
                        for q in range(TPI):
                            last = V.tensor_tensor(on5[:, q, i0:i1], on5[:, q, i0:i1], last_dim(v3[:, i0:i1], HD), ALU.mult)
                        link(last)
                        for q in range(TPI):
                            last = V.tensor_tensor(on5[:, q, i0:i1], on5[:, q, i0:i1], vo[:, i0:i1], ALU.add)
                        last.then_inc(sg("l1_out"), 1)
                    dve.wait_ge(sg("l1_xt"), 8)
                    for g in range(8):
                        dve.wait_ge(sg("l1_y_ps"), g + 1)
                        V.tensor_tensor(tok[:, g * 4:(g + 1) * 4, :], ps[:, 6 + g % 2, 0:4 * C].rearrange("p (t c) -> p t c", c=C),
                                        xt[:, g * 4:(g + 1) * 4, :], ALU.add).then_inc(sg("l1_tok"), 1)
                        if g >= 1:
                            dve.wait_ge(sg("l1_tok"), g)
                            token_stats(range(4 * g - 4, 4 * g))
                    dve.wait_ge(sg("l1_tok"), 8)
                    link(token_stats(range(NT - 4, NT)))
                if l == 2:
                    n1, n2 = HID // NG, C // NG
                    V.tensor_reduce(out=s64[:, 0, 0:NG], in_=wa("f2_w1", C)[:, 0:NG * n1].rearrange("p (g o) -> p g o", g=NG), axis=AX.X, op=ALU.add).then_inc(sg("f2_wsum"), 1)
                    w2v = wb("f2_w2").rearrange("p (j o) -> p j o", j=NJ)
                    for j in range(NJ):
                        last = V.tensor_reduce(out=cmp[:, j, 0:NG], in_=w2v[:, j, 0:NG * n2].rearrange("p (g o) -> p g o", g=NG), axis=AX.X, op=ALU.add)
                    link(last)
                    V.tensor_reduce(out=amax[:, 2, :], in_=cmp[:, 0:NJ, 0:NG].rearrange("p j g -> p g j"), axis=AX.X, op=ALU.add).then_inc(sg("f2_wsum"), 1)
                    dve.wait_ge(sg("f2_wtot"), 1)
                    V.tensor_scalar(s64[:, 1, 0:NG], ps[0:C, 0, 0:NG], -1.0 / (n1 * C), None, ALU.mult)
                    V.tensor_scalar(amax[:, 3, :], ps[:, 1, 0:NG], -1.0 / (n2 * HID), None, ALU.mult).then_inc(sg("f2_z"), 1)
                    V.memset(wa("f2_w1", C)[:, NG * n1:HID], 0.0).then_inc(sg("f2_w1z"), 1)
                    V.memset(w2v[:, :, NG * n2:C], 0.0).then_inc(sg("f2_w2z"), 1)
                    layer_norm("lnf2")

                    def quant_scale(k, g):
                        dve.wait_ge(sg(f"f2_gmax{k}"), g + 1)
                        m, q = amax[:, 2 * k + 1, g:g + 1], amax[:, 2 * k, g:g + 1]
                        link(V.tensor_scalar(m, m, QEPS, None, ALU.add))
                        link(V.reciprocal(q, m))
                        link(V.tensor_scalar(q, q, QB, None, ALU.mult))

                    for step in F2_DVE:
                        what, g = step[0], int(step[1])
                        if what == "a":
                            dve.wait_ge(sg("f2_y1"), g * 6 + 12)
                            V.tensor_reduce(out=amax[:, 0, g:g + 1], in_=y1[:, :, g * GT:(g + 1) * GT], axis=AX.XY, op=ALU.max,
                                            apply_absolute_value=True).then_inc(sg("f2_amax0"), 1)
                        elif what == "q":
                            quant_scale(0, g)
                            v = y1[:, :, g * GT:(g + 1) * GT]
                            link(V.tensor_scalar(v, v, amax[:, 0, g:g + 1], QB - QEPS, ALU.mult, ALU.min))
                            V.tensor_scalar(v, v, -QB + QEPS, None, ALU.max).then_inc(sg("f2_quant"), 1)
                        elif what == "y":
                            if g == 0:
                                dve.wait_ge(sg("f2_w2s"), NG)
                            for b in range(2):
                                dve.wait_ge(sg("f2_y2_ps"), 2 * g + b + 1)
                                t0 = g * 6 + b * 3
                                V.tensor_tensor(y2[:, t0:t0 + 3, :], ps[:, 6 + b, 0:3 * C].rearrange("p (t c) -> p t c", c=C),
                                                mid_dim(wb("f2_b2"), 1, 3), ALU.add).then_inc(sg("f2_y2"), 1)
                            dve.wait_ge(sg("f2_y2"), 2 * g + 2)
                            V.tensor_reduce(out=amax[:, 2, g:g + 1], in_=y2[:, g * 6:(g + 1) * 6, :], axis=AX.XY, op=ALU.max,
                                            apply_absolute_value=True).then_inc(sg("f2_amax1"), 1)
                        else:
                            quant_scale(1, g)
                            v, tv = y2[:, g * 6:(g + 1) * 6, :], tok[:, g * 6:(g + 1) * 6, :]
                            link(V.tensor_scalar(v, v, amax[:, 2, g:g + 1], QB - QEPS, ALU.mult, ALU.min))
                            link(V.scalar_tensor_tensor(out=tv, in0=v, scalar=-QB + QEPS, in1=tv, op0=ALU.max, op1=ALU.add))
                            link(token_stats(range(6 * g, 6 * g + 6 if g < NG - 1 else NT)))
            layer_norm("lnf3")
            def split(t, par):
                x = xn[:, bass.ds(t * 512, 512)]
                V.tensor_copy(xhl[:, par, 0, :], x).then_inc(sg("moe_x"), 1)
                dve.wait_ge(sg("moe_x"), 2 * t + 1)
                V.tensor_tensor(xhl[:, par, 1, :], x, xhl[:, par, 0, :].bitcast(F32), ALU.subtract).then_inc(sg("moe_x"), 1)

            dve.wait_ge(sg("xn_copied"), TURN["lnf3"] + 8)
            split(0, 0)
            dve.wait_ge(sg("f3_gl_ps"), 1)
            gl, ge = gate[:, 0, :, :], gate[:, 1, :, :]
            gp = ps[:, 0, 0:NT * NE].rearrange("p (t e) -> p t e", e=NE)
            link(V.tensor_reduce(out=st[:, 0, :], in_=gp, axis=AX.X, op=ALU.max))
            V.tensor_tensor(gl, gp, last_dim(st[:, 0, :], NE), ALU.subtract).then_inc(sg("f3_gl"), 1)
            dve.wait_ge(sg("f3_gexp"), 1)
            link(V.tensor_reduce(out=st[:, 0, :], in_=ge, axis=AX.X, op=ALU.add))
            link(V.reciprocal(st[:, 1, :], st[:, 0, :]))
            link(V.tensor_tensor(gl, ge, last_dim(st[:, 1, :], NE), ALU.mult))
            pairs = [(0, 1), (0, 2), (0, 3), (1, 2), (1, 3), (2, 3)]
            c = {ab: cmp[:, n, :] for n, ab in enumerate(pairs)}
            for a, b in pairs:
                last = V.tensor_tensor(c[a, b], gate[:, 0, :, a], gate[:, 0, :, b], ALU.is_ge)
            link(last)
            terms = [([(0, 1), (0, 2), (0, 3)], [], ALU.is_gt, 1.5), ([(0, 1)], [(1, 2), (1, 3)], ALU.is_lt, -0.5),
                     ([(0, 2), (1, 2)], [(2, 3)], ALU.is_lt, 0.5), ([(0, 3), (1, 3), (2, 3)], [], ALU.is_lt, 1.5)]
            for e, (plus, minus, _, _) in enumerate(terms):
                x, y = (plus + minus)[:2]
                last = V.tensor_tensor(gsel[:, e, :], c[x], c[y], ALU.add if y in plus else ALU.subtract)
            link(last)
            for e, (plus, minus, _, _) in enumerate(terms):
                z = (plus + minus)[2]
                last = V.tensor_tensor(gsel[:, e, :], gsel[:, e, :], c[z], ALU.add if z in plus else ALU.subtract)
            link(last)
            for e, (_, _, op, edge) in enumerate(terms):
                last = V.scalar_tensor_tensor(out=gate[:, 1, :, e], in0=gsel[:, e, :], scalar=edge, in1=gate[:, 0, :, e], op0=op, op1=ALU.mult)
            link(last)
            link(V.tensor_reduce(out=st[:, 0, :], in_=ge, axis=AX.X, op=ALU.add))
            link(V.tensor_scalar(st[:, 0, :], st[:, 0, :], 1e-9, None, ALU.add))
            link(V.reciprocal(st[:, 1, :], st[:, 0, :]))
            link(V.tensor_tensor(gl, ge, last_dim(st[:, 1, :], NE), ALU.mult))
            with dve.Fori(0, NT // 8) as it:
                for par in range(2):
                    t = it * 2 + par
                    split(t + 1, 1 - par)
                    dve.wait_ge(sg("moe_y_ps"), t + 1)
                    for q in range(4):
                        V.tensor_tensor(ysc[:, q], ps[:, q, 0:NE * C].rearrange("p (e c) -> p e c", e=NE),
                                        wb("f3_b2").rearrange("p (e c) -> p e c", e=NE), ALU.add).then_inc(sg("moe_y"), 1)
                    dve.wait_ge(sg("moe_y"), t * 4 + 8)
                    V.tensor_tensor(ysc[:, :, :, :].rearrange("p q e c -> p (q e) c"), ysc[:, :, :, :].rearrange("p q e c -> p (q e) c"),
                                    last_dim(gate[:, 0, bass.ds(t * 4, 4), :].rearrange("p q e -> p (q e)"), C), ALU.mult).then_inc(sg("moe_w"), 1)
                    dve.wait_ge(sg("moe_w"), t + 1)
                    V.tensor_reduce(out=yred[:, :, :], in_=ysc[:, :, :, :].rearrange("p q e c -> p q c e"), axis=AX.X, op=ALU.add).then_inc(sg("moe_s"), 1)
                    dve.wait_ge(sg("moe_s"), t + 1)
                    tv = tok[:, bass.ds(t * 4, 4), :]
                    V.tensor_tensor(tv, yred[:, :, :], tv, ALU.add).then_inc(sg("moe_block"), 1)


def kernel(**inputs):
    from concourse import bacc
    from concourse.bass_utils import run_bass_kernel_spmd

    def get(name):
        return np.asarray(inputs[name])

    def heads_apart(w, bias=None):
        out = np.zeros((P, 2, C), w.dtype)
        out[:C].reshape(3, 2 * HD, 2, C)[:, :HD] = w.reshape(2, 3, HD, C).transpose(1, 2, 0, 3)
        if bias is not None:
            out[ONE, 0] = bias
        return out

    def with_bias(w, bias):
        return np.concatenate([w, bias.reshape(1, -1)])

    d0 = C // H0
    w0 = get("L0_conv_qkv_w").reshape(H0, 3, d0, C)
    w2, w3, b3 = get("L2_attn_w_attn"), get("L3_attn_qkv_w").T, get("L3_attn_qkv_b")
    def by_width(w):
        return w.reshape(-1, NH, HD).transpose(0, 2, 1).reshape(-1, C)

    parts96 = {
        "l0_q": w0[:, 0].reshape(C, C).T, "l0_k": w0[:, 1].reshape(C, C).T, "l0_v": w0[:, 2].reshape(C, C).T,
        "l0_p": get("L0_conv_proj_w").T, "l0_pb": get("L0_conv_proj_b")[:, None],
        "l1_q": get("L1_conv_Wq").T, "l1_k": get("L1_conv_Wk").T, "l1_v": get("L1_conv_Wv").T,
        "l1_hw": np.repeat(get("L1_conv_head_w").T, HD, axis=0), "l1_p": with_bias(get("L1_conv_projW").T, get("L1_conv_projb")),
        "l2_q": by_width(w2[:, :C]), "l2_k": by_width(w2[:, C:2 * C]), "l2_v": w2[:, 2 * C:], "l2_p": heads_apart(get("L2_attn_w_proj")),
        "f2_w1": with_bias(get("L2_ffn_W1").T, get("L2_ffn_b1")),
        "l3_q": by_width(with_bias(w3[:, :C], b3[:C])), "l3_k": by_width(with_bias(w3[:, C:2 * C], b3[C:2 * C])), "l3_v": with_bias(w3[:, 2 * C:], b3[2 * C:]),
        "l3_p": heads_apart(get("L3_attn_out_w").T, get("L3_attn_out_b")),
        "f3_gate": with_bias(get("L3_ffn_gate_w"), get("L3_ffn_gate_b")),
        "f3_w1": with_bias(get("L3_ffn_w1").transpose(1, 0, 2).reshape(C, NE * HID), get("L3_ffn_b1")),
    }

    def rows(v):
        return np.broadcast_to(v.reshape(1, -1), (P, v.size))

    def padded(m):
        out = np.zeros((P, m.shape[1]), m.dtype)
        out[:m.shape[0]] = m
        return out

    f = np.float32
    parts128 = {
        "ident": np.eye(P, dtype=f),
        "avg3": padded(np.kron(np.eye(32, dtype=f), np.full((3, 3), 1 / 3, f))),
        "sum12": padded(np.kron(np.eye(H0, dtype=f), np.ones((d0, d0), f))),
        "mask": np.triu(np.full((P, P), NEG, f), 1),
        "l1_gamma": rows(get("L1_conv_gamma")), "l1_beta": rows(get("L1_conv_beta")),
        "f2_w2": get("L2_ffn_W2").T.reshape(NJ, P, C).transpose(1, 0, 2).reshape(P, -1),
        "f2_b2": rows(get("L2_ffn_b2")),
        "f3_w2": get("L3_ffn_w2").reshape(NE * NJ, P, C).transpose(1, 0, 2).reshape(P, -1), "f3_b2": rows(get("L3_ffn_b2")),
    }
    arrays = {
        "x_in": np.ascontiguousarray(get("x").transpose(1, 0, 2, 3).reshape(C, B * N)),
        "w96_in": np.ascontiguousarray(np.concatenate([padded(parts96[n].reshape(len(parts96[n]), -1)) for n, _ in W96], axis=1)),
        "w128_in": np.ascontiguousarray(np.concatenate([parts128[n].reshape(P, -1) for n, _ in W128], axis=1)),
    }
    nc = bacc.Bacc("TRN2", target_bir_lowering=False, num_devices=1)
    args = [nc.dram_tensor(n, a.shape, mybir.dt.from_np(a.dtype), kind="ExternalInput").ap() for n, a in arrays.items()]
    out = nc.dram_tensor("out", [P, NT, C], F32, kind="ExternalOutput").ap()
    hybrid_kernel(nc, *args, out)
    got = run_bass_kernel_spmd(nc, [arrays], core_ids=[0]).results[0]["out"]
    return np.ascontiguousarray(got.transpose(1, 0, 2).reshape(B, N, C).transpose(0, 2, 1)).reshape(B, C, HH, WW)
```
